# Optimizing a Trainium2 kernel written in Bass

```python
import numpy as np
import jax
import jax.numpy as jnp

def _softmax(x, axis=-1):
    return jax.nn.softmax(x, axis=axis)

def _gelu(x):
    return jax.nn.gelu(x, approximate=True)

def _silu(x):
    return jax.nn.silu(x)

def _sigmoid(x):
    return jax.nn.sigmoid(x)

def _layernorm(x, axis=-1, eps=1e-05):
    m = jnp.mean(x, axis=axis, keepdims=True)
    v = jnp.var(x, axis=axis, keepdims=True)
    return (x - m) / jnp.sqrt(v + eps)

def _scatter_add(tgt, idx, src, axis=0):
    return tgt.at[idx].add(src)

def _segment_sum(src, seg, n):
    return jax.ops.segment_sum(src, seg, n)
kernel_name = 'mk_gnn_resnorm_d4_gnn_r16_b71bc1'

def setup_inputs(seed: int=0):
    np.random.seed(seed)
    _w = jnp.asarray

    def _rec_inputs():
        import jax
        import jax.numpy as jnp
        _gk = jax.random.key(seed)
        x = -0.0003713 + 1 * jax.random.normal(jax.random.fold_in(_gk, 1), (6250, 128), jnp.float32)
        _s = jax.random.randint(jax.random.fold_in(_gk, 2), (50000,), 0, 6250, jnp.int32)
        _d = jax.random.randint(jax.random.fold_in(_gk, 3), (50000,), 0, 6250, jnp.int32)
        _loop = jnp.arange(6250, dtype=jnp.int32)
        src = jnp.concatenate([_s, _d, _loop])
        dst = jnp.concatenate([_d, _s, _loop])
        _o = jnp.argsort(dst, stable=True)
        src = src[_o]
        dst = dst[_o]
        return (x, src, dst)
    x, src, dst = _rec_inputs()

    def _L0_gnn_setup():
        import jax, jax.numpy as jnp
        import numpy as np
        N = 6250
        E = 37500
        D_IN = 128
        D = 128
        L = 3

        def gru_cell(m, h, w_ih, w_hh, b_ih, b_hh):
            gi = m @ w_ih.T + b_ih
            gh = h @ w_hh.T + b_hh
            ir, iz, inn = jnp.split(gi, 3, axis=-1)
            hr, hz, hn = jnp.split(gh, 3, axis=-1)
            r = jax.nn.sigmoid(ir + hr)
            z = jax.nn.sigmoid(iz + hz)
            n = jnp.tanh(inn + r * hn)
            return (1.0 - z) * n + z * h
        key = jax.random.key(seed)
        ks = jax.random.split(key, 10)
        s = 1.0 / np.sqrt(D)
        x = jax.random.normal(ks[0], (N, D_IN), dtype=jnp.float32)
        edge_index = jax.random.randint(ks[1], (2, E), 0, N, dtype=jnp.int64)
        lin_w = jax.random.normal(ks[2], (D, D_IN), dtype=jnp.float32) * (1.0 / np.sqrt(D_IN))
        lin_b = jnp.zeros((D,), dtype=jnp.float32)
        weight = jax.random.normal(ks[3], (L, D, D), dtype=jnp.float32) * s
        w_ih = jax.random.normal(ks[4], (3 * D, D), dtype=jnp.float32) * s
        w_hh = jax.random.normal(ks[5], (3 * D, D), dtype=jnp.float32) * s
        b_ih = jnp.zeros((3 * D,), dtype=jnp.float32)
        b_hh = jnp.zeros((3 * D,), dtype=jnp.float32)
        return {'x': x, 'lin_w': lin_w, 'lin_b': lin_b, 'weight': weight, 'w_ih': w_ih, 'w_hh': w_hh, 'b_ih': b_ih, 'b_hh': b_hh, 'edge_index': edge_index}
    _L0_gnn_all = _L0_gnn_setup()
    _L0_gnn_in = {k: v for k, v in _L0_gnn_all.items() if k in ('lin_w', 'lin_b', 'weight', 'w_ih', 'w_hh', 'b_ih', 'b_hh')}
    del _L0_gnn_all

    def _L1_gnn_setup():
        import jax, jax.numpy as jnp
        import numpy as np
        N, M, E = (3125, 6250, 50000)
        F_IN, F_OUT = (128, 128)
        BN_EPS = 1e-05
        key = jax.random.key(seed)
        ks = jax.random.split(key, 7)
        x = jax.random.normal(ks[0], (N, F_IN), dtype=jnp.float32)
        row = jax.random.randint(ks[1], (E,), 0, N)
        col = jax.random.randint(ks[2], (E,), 0, M)
        hyperedge_index = jnp.stack([row, col]).astype(jnp.int32)
        hyperedge_weight = jax.random.uniform(ks[3], (M,), dtype=jnp.float32) + 0.5
        W = jax.random.normal(ks[4], (F_IN, F_OUT), dtype=jnp.float32) / np.sqrt(F_IN)
        b = jax.random.normal(ks[5], (F_OUT,), dtype=jnp.float32) * 0.02
        gamma = jnp.ones((F_OUT,), dtype=jnp.float32)
        beta = jnp.zeros((F_OUT,), dtype=jnp.float32)
        return {'x': x, 'hyperedge_index': hyperedge_index, 'hyperedge_weight': hyperedge_weight, 'W': W, 'b': b, 'gamma': gamma, 'beta': beta}
    _L1_gnn_all = _L1_gnn_setup()
    _L1_gnn_in = {k: v for k, v in _L1_gnn_all.items() if k in ('hyperedge_weight', 'W', 'b', 'gamma', 'beta')}
    del _L1_gnn_all

    def _L2_gnn_setup():
        import jax, jax.numpy as jnp
        import numpy as np
        N_NODES = 6250
        D_IN = 128
        D_OUT = 128
        N_EDGES = 100000
        BN_EPS = 1e-05

        def _glorot(key, fan_in, fan_out):
            limit = np.sqrt(6.0 / (fan_in + fan_out))
            return jax.random.uniform(key, (fan_in, fan_out), jnp.float32, -limit, limit)
        key = jax.random.key(seed)
        k_x, k_e, k0, k1, k2 = jax.random.split(key, 5)
        x = jax.random.normal(k_x, (N_NODES, D_IN), jnp.float32)
        edge_index = jax.random.randint(k_e, (2, N_EDGES), 0, N_NODES, jnp.int64)
        return {'x': x, 'edge_index': edge_index, 'kernel': _glorot(k0, D_IN, D_OUT), 'kernel1': _glorot(k1, D_IN, D_IN), 'kernel2': _glorot(k2, D_IN, D_IN), 'gamma': jnp.ones((D_IN,), jnp.float32), 'beta': jnp.zeros((D_IN,), jnp.float32)}
    _L2_gnn_all = _L2_gnn_setup()
    _L2_gnn_in = {k: v for k, v in _L2_gnn_all.items() if k in ('kernel', 'kernel1', 'kernel2', 'gamma', 'beta')}
    del _L2_gnn_all

    def _L3_gnn_setup():
        import jax, jax.numpy as jnp
        import numpy as np
        N_NODES = 3125
        N_EDGES = 50000
        D = 128

        def _mlp(h, W1, b1, W2, b2):
            return jax.nn.relu(h @ W1 + b1) @ W2 + b2
        key = jax.random.key(seed)
        ks = jax.random.split(key, 6)
        s = 0.05
        x = jax.random.normal(ks[0], (N_NODES, D), dtype=jnp.float32)
        edge_index = jax.random.randint(ks[1], (2, N_EDGES), 0, N_NODES, dtype=jnp.int64)
        We1 = jax.random.normal(ks[2], (2 * D, D), dtype=jnp.float32) * s
        be1 = jnp.zeros((D,), dtype=jnp.float32)
        We2 = jax.random.normal(ks[3], (D, D), dtype=jnp.float32) * s
        be2 = jnp.zeros((D,), dtype=jnp.float32)
        Wn1 = jax.random.normal(ks[4], (2 * D, D), dtype=jnp.float32) * s
        bn1 = jnp.zeros((D,), dtype=jnp.float32)
        Wn2 = jax.random.normal(ks[5], (D, D), dtype=jnp.float32) * s
        bn2 = jnp.zeros((D,), dtype=jnp.float32)
        return {'x': x, 'edge_index': edge_index, 'We1': We1, 'be1': be1, 'We2': We2, 'be2': be2, 'Wn1': Wn1, 'bn1': bn1, 'Wn2': Wn2, 'bn2': bn2}
    _L3_gnn_all = _L3_gnn_setup()
    _L3_gnn_in = {k: v for k, v in _L3_gnn_all.items() if k in ('We1', 'be1', 'We2', 'be2', 'Wn1', 'bn1', 'Wn2', 'bn2')}
    del _L3_gnn_all
    return {'x': x, 'src': src, 'dst': dst, 'L0_gnn_lin_w': _L0_gnn_in['lin_w'], 'L0_gnn_lin_b': _L0_gnn_in['lin_b'], 'L0_gnn_weight': _L0_gnn_in['weight'], 'L0_gnn_w_ih': _L0_gnn_in['w_ih'], 'L0_gnn_w_hh': _L0_gnn_in['w_hh'], 'L0_gnn_b_ih': _L0_gnn_in['b_ih'], 'L0_gnn_b_hh': _L0_gnn_in['b_hh'], 'L1_gnn_hyperedge_weight': _L1_gnn_in['hyperedge_weight'], 'L1_gnn_W': _L1_gnn_in['W'], 'L1_gnn_b': _L1_gnn_in['b'], 'L1_gnn_gamma': _L1_gnn_in['gamma'], 'L1_gnn_beta': _L1_gnn_in['beta'], 'L2_gnn_kernel': _L2_gnn_in['kernel'], 'L2_gnn_kernel1': _L2_gnn_in['kernel1'], 'L2_gnn_kernel2': _L2_gnn_in['kernel2'], 'L2_gnn_gamma': _L2_gnn_in['gamma'], 'L2_gnn_beta': _L2_gnn_in['beta'], 'L3_gnn_We1': _L3_gnn_in['We1'], 'L3_gnn_be1': _L3_gnn_in['be1'], 'L3_gnn_We2': _L3_gnn_in['We2'], 'L3_gnn_be2': _L3_gnn_in['be2'], 'L3_gnn_Wn1': _L3_gnn_in['Wn1'], 'L3_gnn_bn1': _L3_gnn_in['bn1'], 'L3_gnn_Wn2': _L3_gnn_in['Wn2'], 'L3_gnn_bn2': _L3_gnn_in['bn2']}

def reference(x, src, dst, L0_gnn_lin_w, L0_gnn_lin_b, L0_gnn_weight, L0_gnn_w_ih, L0_gnn_w_hh, L0_gnn_b_ih, L0_gnn_b_hh, L1_gnn_hyperedge_weight, L1_gnn_W, L1_gnn_b, L1_gnn_gamma, L1_gnn_beta, L2_gnn_kernel, L2_gnn_kernel1, L2_gnn_kernel2, L2_gnn_gamma, L2_gnn_beta, L3_gnn_We1, L3_gnn_be1, L3_gnn_We2, L3_gnn_be2, L3_gnn_Wn1, L3_gnn_bn1, L3_gnn_Wn2, L3_gnn_bn2):
    import jax
    import jax.numpy as jnp

    def _L0_gnn_ref(x, lin_w, lin_b, weight, w_ih, w_hh, b_ih, b_hh, edge_index):
        import jax, jax.numpy as jnp
        import numpy as np
        N = 6250
        E = 37500
        D_IN = 128
        D = 128
        L = 3

        def gru_cell(m, h, w_ih, w_hh, b_ih, b_hh):
            gi = m @ w_ih.T + b_ih
            gh = h @ w_hh.T + b_hh
            ir, iz, inn = jnp.split(gi, 3, axis=-1)
            hr, hz, hn = jnp.split(gh, 3, axis=-1)
            r = jax.nn.sigmoid(ir + hr)
            z = jax.nn.sigmoid(iz + hz)
            n = jnp.tanh(inn + r * hn)
            return (1.0 - z) * n + z * h
        h = x @ lin_w.T + lin_b
        src, dst = (edge_index[0], edge_index[1])
        n_nodes = h.shape[0]
        for i in range(weight.shape[0]):
            m = h @ weight[i]
            agg = jax.ops.segment_sum(m[src], dst, num_segments=n_nodes)
            h = gru_cell(agg, h, w_ih, w_hh, b_ih, b_hh)
        return h

    def _L1_gnn_ref(x, hyperedge_index, hyperedge_weight, W, b, gamma, beta):
        import jax, jax.numpy as jnp
        import numpy as np
        N, M, E = (3125, 6250, 50000)
        F_IN, F_OUT = (128, 128)
        BN_EPS = 1e-05
        row = hyperedge_index[0]
        col = hyperedge_index[1]
        num_nodes = x.shape[0]
        num_edges = hyperedge_weight.shape[0]
        h = x @ W
        D = jax.ops.segment_sum(hyperedge_weight[col], row, num_segments=num_nodes)
        D_inv = jnp.where(D > 0, 1.0 / D, 0.0)
        B = jax.ops.segment_sum(jnp.ones_like(col, dtype=h.dtype), col, num_segments=num_edges)
        B_inv = jnp.where(B > 0, 1.0 / B, 0.0)
        e_feat = B_inv[:, None] * jax.ops.segment_sum(h[row], col, num_segments=num_edges)
        out = D_inv[:, None] * jax.ops.segment_sum(e_feat[col], row, num_segments=num_nodes)
        out = out + b
        mean = out.mean(axis=0)
        var = out.var(axis=0)
        out = gamma * (out - mean) * jax.lax.rsqrt(var + BN_EPS) + beta
        return jax.nn.relu(out)

    def _L2_gnn_ref(x, edge_index, kernel, kernel1, kernel2, gamma, beta):
        import jax, jax.numpy as jnp
        import numpy as np
        N_NODES = 6250
        D_IN = 128
        D_OUT = 128
        N_EDGES = 100000
        BN_EPS = 1e-05

        def _glorot(key, fan_in, fan_out):
            limit = np.sqrt(6.0 / (fan_in + fan_out))
            return jax.random.uniform(key, (fan_in, fan_out), jnp.float32, -limit, limit)
        N = x.shape[0]
        mean = jnp.mean(x, axis=0)
        var = jnp.var(x, axis=0)
        xn = (x - mean) * jax.lax.rsqrt(var + BN_EPS) * gamma + beta
        mapped = xn @ kernel
        s1 = jnp.tanh(jnp.sum(xn @ kernel1 * xn, axis=1))
        s2 = jnp.tanh(jnp.sum(xn @ kernel2 * xn, axis=1))
        src, dst = (edge_index[0], edge_index[1])
        e = jax.nn.leaky_relu(s1[src] + s2[dst], negative_slope=0.01)
        emax = jax.ops.segment_max(e, src, num_segments=N)
        emax = jnp.where(jnp.isfinite(emax), emax, 0.0)
        ee = jnp.exp(e - emax[src])
        denom = jax.ops.segment_sum(ee, src, num_segments=N)
        attn = ee / jnp.maximum(denom[src], 1e-16)
        out = jax.ops.segment_sum(attn[:, None] * mapped[dst], src, num_segments=N)
        return jax.nn.relu(out)

    def _L3_gnn_ref(x, edge_index, We1, be1, We2, be2, Wn1, bn1, Wn2, bn2):
        import jax, jax.numpy as jnp
        import numpy as np
        N_NODES = 3125
        N_EDGES = 50000
        D = 128

        def _mlp(h, W1, b1, W2, b2):
            return jax.nn.relu(h @ W1 + b1) @ W2 + b2
        src = edge_index[0]
        dst = edge_index[1]
        e_in = jnp.concatenate([x[src], x[dst]], axis=-1)
        edge_new = _mlp(e_in, We1, be1, We2, be2)
        agg = jax.ops.segment_sum(edge_new, dst, num_segments=x.shape[0])
        mesh_new = _mlp(jnp.concatenate([x, agg], axis=-1), Wn1, bn1, Wn2, bn2)
        return x + mesh_new
    edge_index = jnp.stack([src, dst])
    x = _layernorm(x + _L0_gnn_ref(x, L0_gnn_lin_w, L0_gnn_lin_b, L0_gnn_weight, L0_gnn_w_ih, L0_gnn_w_hh, L0_gnn_b_ih, L0_gnn_b_hh, edge_index), axis=-1)
    x = _layernorm(x + _L1_gnn_ref(x, edge_index, L1_gnn_hyperedge_weight, L1_gnn_W, L1_gnn_b, L1_gnn_gamma, L1_gnn_beta), axis=-1)
    x = _layernorm(x + _L2_gnn_ref(x, edge_index, L2_gnn_kernel, L2_gnn_kernel1, L2_gnn_kernel2, L2_gnn_gamma, L2_gnn_beta), axis=-1)
    x = _layernorm(x + _L3_gnn_ref(x, edge_index, L3_gnn_We1, L3_gnn_be1, L3_gnn_We2, L3_gnn_be2, L3_gnn_Wn1, L3_gnn_bn1, L3_gnn_Wn2, L3_gnn_bn2), axis=-1)
    return x

_drawn_inputs = setup_inputs


def setup_inputs(seed=0):
    import zlib

    import numpy as np

    out = dict(_drawn_inputs(seed))
    spreads = {'L0_gnn_lin_b': (0.0, 0.1),
     'L0_gnn_b_ih': (0.0, 0.1),
     'L0_gnn_b_hh': (0.0, 0.1),
     'L1_gnn_gamma': (1.0, 0.2),
     'L1_gnn_beta': (0.0, 0.1),
     'L2_gnn_gamma': (1.0, 0.2),
     'L2_gnn_beta': (0.0, 0.1),
     'L3_gnn_be1': (0.0, 0.1),
     'L3_gnn_be2': (0.0, 0.1),
     'L3_gnn_bn1': (0.0, 0.506),
     'L3_gnn_bn2': (0.0, 0.1)}
    factors = {'L1_gnn_b': 8.0, 'L2_gnn_kernel1': 8.0}
    for name, (base, spread) in spreads.items():
        noise = np.random.default_rng([zlib.crc32(name.encode()), seed]).standard_normal(out[name].shape)
        drawn = base * np.exp(spread * noise) if base else spread * noise
        out[name] = jnp.asarray(drawn.astype(out[name].dtype))
    for name, factor in factors.items():
        out[name] = (out[name] * factor).astype(out[name].dtype)
    return out
```

```python
from contextlib import ExitStack

import concourse.bass as bass
from concourse import mybir

F32 = mybir.dt.float32
I32 = mybir.dt.int32
I16 = mybir.dt.int16
U8 = mybir.dt.uint8
ALU = mybir.AluOpType
ACT = mybir.ActivationFunctionType
AX_X = mybir.AxisListType.X

P = 128
N = 6250
E = 106250
NB = (N + P - 1) // P
NBP = 52
NP = NBP * P
CB = 2
CN = CB * P
NODE_ITERS = NP // (2 * CN)
EC = 832
E_FULL = E // EC
E_REST = E - E_FULL * EC
CH = 8
T = -(-((E + NB * (P - 1)) // P) // (2 * CH)) * 2 * CH
PASS_ITERS = T // (2 * CH)
TP = T + 2 * CH
W = 132
SC = 16
SCATTER_ITERS = EC // (2 * SC)
PAD_NODE = 63 * P
PAD_LOCAL = 255
MASKB = 128
ST = 250
NST = N // ST
EPS = 1e-5
GRU_LAYERS = 3


class Count:
    def __init__(self, sem, base):
        self.sem, self.base = sem, base


def wait(eng, sem, value):
    if isinstance(value, int) and value <= 0:
        return
    if isinstance(sem, Count):
        eng.wait_ge(sem.sem, value + sem.base)
    else:
        eng.wait_ge(sem, value)


def turns(eng, count, body):
    body(0)
    with eng.Fori(1, count) as i:
        body(i)


def gnn(nc, d):
    ctx = ExitStack()
    with ctx:
        def sb(name, shape, dt=F32):
            return ctx.enter_context(nc.sbuf_tensor(name, shape, dt))

        def sem(name):
            return ctx.enter_context(nc.semaphore(name))

        def dram(name, shape, dt=F32):
            return nc.dram_tensor(name, shape, dt, kind="Internal").ap()

        x_nm = sb("x_nm", [P, NBP, P])
        x_fm = sb("x_fm", [P, NP])
        acc = sb("acc", [P, NBP * W])
        stage = sb("stage", [P, NBP * W])
        big = sb("big", [P, 2 * NP])
        gather_idx = [sb(f"gather_idx{k}", [P, TP], I32) for k in range(2)]
        local = [sb(f"local{k}", [P, TP]) for k in range(2)]
        block_of = [sb(f"block_of{k}", [P, T], I16) for k in range(2)]
        rows = sb("rows", [P, 2 * CH, W])
        onehot = sb("onehot", [P, 2 * CH, P])
        idx_ring = sb("idx_ring", [P, 2 * SC], I32)
        val_ring = sb("val_ring", [P, 2 * SC], I32)
        w_late = sb("w_late", [P, 10 * P])
        w_hh = sb("w_hh", [P, 3 * P])
        w_lin = sb("w_lin", [P, P])
        w_hyper = sb("w_hyper", [P, P])
        ident = sb("ident", [P, P])
        ones = sb("ones", [P, P])
        iota = sb("iota", [P, P])
        lower = sb("lower", [P, P])
        cols = sb("cols", [P, 24])
        small = sb("small", [P, 6, NBP])
        mv = sb("mv", [P, NBP, 2])
        mv_chunk = sb("mv_chunk", [P, CB, 2])
        bst = sb("bst", [P, NST, 6])
        bmv = sb("bmv", [P, 2])
        st6 = sb("st6", [P, 2, CB, 6])
        row0 = sb("row0", [1, 2 * P])
        ps = ctx.enter_context(nc.psum_tensor("ps", [P, 8, 512], F32))

        acc_nm = acc[:, :].rearrange("p (b w) -> p b w", w=W)
        stage_nm = stage[:, :].rearrange("p (b w) -> p b w", w=W)
        stage_rows = stage[:, 0:NP].rearrange("p (b f) -> p b f", f=P)
        w_comb = w_late[:, 0:9 * P].rearrange("p (l m) -> p l m", l=3)
        w_att = w_late[:, 0:3 * P]
        w_e1 = w_late[:, 3 * P:5 * P]
        w_e2 = w_late[:, 5 * P:6 * P]
        w_n1 = w_late[:, 6 * P:8 * P]
        w_n2 = w_late[:, 8 * P:9 * P]
        be1_rows = w_late[:, 9 * P:10 * P]

        edge_end = [acc[:, k * EC:(k + 1) * EC].bitcast(I32) for k in range(2)]
        tmp_int = acc[:, 2 * EC:3 * EC].bitcast(I32)
        loc_int = acc[:, 3 * EC:4 * EC].bitcast(I32)
        slot_addr = [acc[:, (4 + k) * EC:(5 + k) * EC].bitcast(I32) for k in range(2)]
        packed = [acc[:, (6 + k) * EC:(7 + k) * EC].bitcast(I32) for k in range(2)]
        mask = big[:, 0:NB * EC // 4].bitcast(U8).rearrange("p (b c) -> p b c", c=EC)
        m0 = NB * EC // 4
        blk_f = big[:, m0:m0 + EC]
        pos = x_fm[:, 0:EC]
        scan = x_fm[:, EC:3 * EC].rearrange("p (s c) -> p s c", s=2)
        ones_row = x_fm[:, 3 * EC:4 * EC]
        count_b = big[:, m0 + EC:m0 + EC + MASKB]
        base = big[:, m0 + EC + MASKB:m0 + EC + 2 * MASKB]
        diag = big[:, m0 + EC + 2 * MASKB:m0 + EC + 3 * MASKB]
        tiny = big[:, m0 + EC + 3 * MASKB:m0 + EC + 3 * MASKB + 8]
        tiny_i = big[:, m0 + EC + 3 * MASKB + 8:m0 + EC + 3 * MASKB + 16].bitcast(I32)
        tile_iota = x_fm[:, 4 * EC:4 * EC + T]
        tile_ge = x_fm[:, 4 * EC + T:4 * EC + 2 * T]
        sel_blocks = x_fm[:, 4 * EC + 2 * T:4 * EC + 2 * T + P]
        assert 4 * EC + 2 * T + P <= NP
        trash = stage[:, 16 * P:16 * P + EC - E_REST].bitcast(I32)
        fill = stage[:, 20 * P:20 * P + T].bitcast(I32)
        h0_slots = m0 + EC + 3 * MASKB + 16
        assert h0_slots + 6 * CN <= 2 * NP
        list_in = stage[:, 0:T].bitcast(I32)
        raw_w = stage[:, 0:10 * P].rearrange("p (m f) -> p m f", f=P)
        tr_w = stage[:, 10 * P:16 * P].rearrange("p (m f) -> p m f", f=P)

        edge_list = [dram(f"edge_list{k}", (P * T + EC, 1), I32) for k in range(2)]
        widths = [P, P, P, P + 1, P + 1, P + 3, P]
        table = [dram(f"table{p}", (NP, w)) for p, w in enumerate(widths)]
        degree_row = dram("degree_row", (NP, 1))

        stage_end = sem("stage_end")
        boundary = {}

        def end_stage(eng, nc_eng):
            boundary[eng] = boundary.get(eng, 0) + 1
            nc_eng.drain().then_inc(stage_end, 1)
            eng.wait_ge(stage_end, 5 * boundary[eng])

        row_landed = [sem(f"row_landed{s}") for s in range(2 * CH)]
        rows_opened = sem("rows_opened")

        made = {}

        def S(name):
            if name not in made:
                made[name] = sem(name)
            return made[name]

        NC = 2 * NODE_ITERS
        moves = {"idx_ready": TP // CH, "summed": T, "added": T, "hot_ready": T // CH + 1, "acc_zero": 1,
                 "rz_ready": NC, "nh_ready": NC, "r_ready": NC, "z_ready": NC, "n_ready": NC, "n_in": NC,
                 "h_ready": NC, "h_kept": NC, "flip_done_gru": NC, "flip_taken_gru": NC,
                 "stored_gru": 16 * NODE_ITERS}

        def Q(name, p):
            before = p
            if name == "hot_ready":
                before = sum(m != "att" for m in MODES[:p])
            return Count(S(name), moves.get(name, 0) * before)

        LISTS = [0, 0, 0, 0, 1, 1, 0]
        MODES = ["fm", "fm", "fm", "nm", "nm", "att", "edge"]

        def cslice(c):
            return bass.ds(c * CN, CN)

        def bslice(c):
            return bass.ds(c * CB, CB)

        ring_ohT = stage[:, 0:CH * P].rearrange("p (t e) -> p t e", e=P)
        ring_e = stage[:, CH * P:3 * CH * P].rearrange("p (t e) -> p t e", e=P)
        u1_rows = big[:, 0:NP]
        u2_rows = big[:, NP:2 * NP]
        q_nm = big[:, 0:NP]

        block_regs = {}

        def tile_blocks(eng, k, c):
            if eng not in block_regs:
                block_regs[eng] = [eng.alloc_register(f"block{u}") for u in range(CH)]
            eng.load(block_regs[eng], block_of[k][0:1, bass.ds(CH * c, CH)])
            return [eng.snap(r, min_val=0, max_val=NB - 1) for r in block_regs[eng]]

        def groups(w):
            per = 512 // w
            return [(g, range(g * per, min((g + 1) * per, CH))) for g in range(-(-CH // per))]

        def psum_sum(h, u, w):
            per = 512 // w
            return ps[:, h * -(-CH // per) + u // per, (u % per) * w:(u % per + 1) * w]

        def pass_pool(p, pool):
            idx_ready, summed = Q("idx_ready", p), Q("summed", p)

            def body(i):
                for h in range(2):
                    wait(pool, idx_ready, 2 * i + h + 1)
                    pool.sem_inc(rows_opened, 1)
                    if not isinstance(i, int):
                        wait(pool, summed, 2 * CH * i + CH * h - CH)
                        pool.sem_inc(rows_opened, 1)
                    for u in range(CH):
                        s = h * CH + u
                        nc.gpsimd.indirect_dma_start(
                            rows[:, s, 0:widths[p]], None, table[p][0:N, :],
                            bass.IndirectOffsetOnAxis(idx_ring[:, s:s + 1], 0),
                        ).then_inc(row_landed[s], 16)
            turns(pool, PASS_ITERS, body)

        def pass_act(p, act):
            k, mode = LISTS[p], MODES[p]
            idx_ready, summed = Q("idx_ready", p), Q("summed", p)
            for h in range(2):
                nc.scalar.copy(idx_ring[:, h * CH:(h + 1) * CH],
                               gather_idx[k][:, h * CH:(h + 1) * CH]).then_inc(idx_ready.sem, 1)

            def body(i):
                for h in range(2):
                    c = 2 * i + h
                    if mode == "att":
                        blk = tile_blocks(act, k, c)
                        for u in range(CH):
                            s = h * CH + u
                            wait(act, row_landed[s], 16 * (PASS_ITERS * p + i + 1))
                            nc.scalar.activation(onehot[:, s, :], u1_rows[:, bass.ds(blk[u] * P, P)],
                                                 ACT.Copy, scale=rows[:, s, 129:130]
                                                 ).then_inc(Q("scaled", p).sem, 1)
                    if mode == "edge":
                        for g in range(2):
                            wait(act, Q("flipped", p), 2 * c + g + 1)
                            nc.scalar.copy(ring_ohT[:, 4 * g:4 * g + 4, :].rearrange("p t e -> p (t e)"), ps[:, 4 + g, :]
                                           ).then_inc(Q("flip_copied", p).sem, 1)
                        for g in range(2):
                            wait(act, Q("edge_pre", p), 2 * c + g + 1)
                            nc.scalar.activation(ring_e[:, h * CH + 4 * g:h * CH + 4 * g + 4, :]
                                                 .rearrange("p t e -> p (t e)"), ps[:, 6 + g, :], ACT.Relu
                                                 ).then_inc(Q("edge_act", p).sem, 1)
                    wait(act, summed, CH * c + CH)
                    nc.scalar.copy(idx_ring[:, h * CH:(h + 1) * CH],
                                   gather_idx[k][:, bass.ds(CH * (c + 2), CH)]).then_inc(idx_ready.sem, 1)
            turns(act, PASS_ITERS, body)

        def pass_pe(p, pe):
            k, mode = LISTS[p], MODES[p]
            w = P if mode in ("fm", "edge") else P + 1
            hot_ready, summed, added = Q("weighted" if MODES[p] == "att" else "hot_ready", p), Q("summed", p), Q("added", p)

            def body(i):
                for h in range(2):
                    c = 2 * i + h
                    if mode == "edge":
                        blk = tile_blocks(pe, k, c)
                        wait(pe, hot_ready, c + 1)
                        for g in range(2):
                            wait(pe, Q("flip_copied", p), 2 * (c - 1) + g + 1)
                            for u in range(4):
                                last = nc.tensor.transpose(ps[:, 4 + g, u * P:(u + 1) * P],
                                                           onehot[:, h * CH + 4 * g + u, :], ident[:, :])
                            last.then_inc(Q("flipped", p).sem, 1)
                        for g in range(2):
                            wait(pe, Q("edge_act", p), 2 * (c - 1) + g + 1)
                            wait(pe, Q("flip_copied", p), 2 * c + g + 1)
                            for u in range(4):
                                s = h * CH + 4 * g + u
                                out = ps[:, 6 + g, u * P:(u + 1) * P]
                                wait(pe, row_landed[s], 16 * (PASS_ITERS * p + i + 1))
                                nc.tensor.matmul(out, ident[:, :], rows[:, s, 0:P], start=True, stop=False,
                                                 skip_group_check=True)
                                last = nc.tensor.matmul(out, ring_ohT[:, 4 * g + u, :],
                                                        q_nm[:, bass.ds(blk[4 * g + u] * P, P)],
                                                        start=False, stop=True, skip_group_check=True)
                            last.then_inc(Q("edge_pre", p).sem, 1)
                    elif mode != "att":
                        wait(pe, hot_ready, c + 1)
                    for g, tiles in groups(w):
                        wait(pe, added, CH * (c - 2) + tiles[-1] + 1)
                        if mode == "edge":
                            wait(pe, Q("edge_act", p), 2 * c + g + 1)
                        for u in tiles:
                            s = h * CH + u
                            if mode == "edge":
                                lhs, rhs = ring_e[:, s, :], onehot[:, s, :]
                            else:
                                wait(pe, row_landed[s], 16 * (PASS_ITERS * p + i + 1))
                                if mode == "fm":
                                    lhs, rhs = rows[:, s, 0:P], onehot[:, s, :]
                                elif mode == "nm":
                                    lhs, rhs = onehot[:, s, :], rows[:, s, 0:w]
                                else:
                                    wait(pe, hot_ready, CH * c + u + 1)
                                    lhs, rhs = ring_e[:, s, :], rows[:, s, 0:w]
                            nc.tensor.matmul(psum_sum(h, u, w), lhs, rhs, start=True, stop=True,
                                             skip_group_check=True).then_inc(summed.sem, 1)
            turns(pe, PASS_ITERS, body)

        def pass_dve(p, dve):
            k, mode = LISTS[p], MODES[p]
            w = P if mode in ("fm", "edge") else P + 1
            stride = P if mode in ("fm", "edge") else W
            hot_ready, summed, added = Q("weighted" if MODES[p] == "att" else "hot_ready", p), Q("summed", p), Q("added", p)
            nc.vector.memset(acc[:, :], 0.0).then_inc(Q("acc_zero", p).sem, 1)
            wait(dve, Q("acc_zero", p), 1)

            def hots(c, h):
                nc.vector.tensor_tensor(
                    onehot[:, h * CH:(h + 1) * CH, :],
                    iota[:, :].unsqueeze(1).to_broadcast([P, CH, P]),
                    local[k][:, bass.ds(CH * c, CH)].unsqueeze(2).to_broadcast([P, CH, P]),
                    ALU.is_equal).then_inc(hot_ready.sem, 1)

            if mode != "att":
                hots(0, 0)

            def body(i):
                for h in range(2):
                    c = 2 * i + h
                    blk = tile_blocks(dve, k, c)
                    if mode != "att":
                        hots(c + 1, 1 - h)
                    else:
                        for u in range(CH):
                            s = h * CH + u
                            wait(dve, Q("scaled", p), CH * c + u + 1)
                            nc.vector.scalar_tensor_tensor(
                                ring_e[:, s, :], u2_rows[:, bass.ds(blk[u] * P, P)], rows[:, s, 130:131],
                                onehot[:, s, :], ALU.mult, ALU.max).then_inc(Q("weighed", p).sem, 1)
                        for u in range(CH):
                            s = h * CH + u
                            wait(dve, Q("weighed", p), CH * c + u + 1)
                            nc.vector.scalar_tensor_tensor(
                                ring_e[:, s, :], iota[:, :], local[k][:, bass.ds(CH * c + u, 1)],
                                ring_e[:, s, :], ALU.is_equal, ALU.mult).then_inc(hot_ready.sem, 1)
                    for g, tiles in groups(w):
                        wait(dve, summed, CH * c + tiles[-1] + 1)
                        for u in tiles:
                            dst = acc[:, bass.ds(blk[u] * stride, w)]
                            wait(dve, added, CH * c + u)
                            nc.vector.tensor_tensor(dst, psum_sum(h, u, w), dst, ALU.add).then_inc(added.sem, 1)
            turns(dve, PASS_ITERS, body)

        def tslot(s):
            return ps[:, 4 + s, 0:CN]

        def flip_pe(tag, pe, src, c, s, ready):
            taken, done = (Q("flip_taken_gru", tag), Q("flip_done_gru", tag)) if isinstance(tag, int) else \
                (Count(S("flip_taken" + tag), 0), Count(S("flip_done" + tag), 0))
            wait(pe, ready, c + 1)
            wait(pe, taken, c - 1)
            for b in range(CB):
                last = nc.tensor.transpose(ps[:, 4 + s, b * P:(b + 1) * P], src[:, b * P:(b + 1) * P], ident[:, :])
            last.then_inc(done.sem, 1)

        def cut_dve(tag, dve, c, s, slot):
            wait(dve, S("flip_done" + tag), c - 1)
            nc.vector.tensor_copy(slot, x_nm[:, bslice(c), :].rearrange("p b f -> p (b f)")).then_inc(S("cut" + tag), 1)

        class Steps:
            def __init__(self, eng, name, per_chunk, base=0):
                self.eng, self.sem, self.per, self.c, self.n = eng, S(name), per_chunk, 0, 0
                self.base = base

            def chunk(self, c):
                self.c, self.n = c, 0

            def __call__(self, ins):
                self.n += 1
                ins.then_inc(self.sem, 1)
                self.eng.wait_ge(self.sem, self.c * self.per + self.n + self.base)

        chained = []

        def chain(dve):
            if not chained:
                chained.append(Steps(dve, "dve_chain", 0))
            return chained[0]

        def hold(eng):
            eng.sem_inc(S("held"), 1)

        def stats_dve(tag, dve, c, steps):
            hold(dve)
            for b in range(CB):
                nc.vector.bn_stats(st6[:, 0, b, :], x_nm[:, bass.ds(c * CB + b, 1), :]
                                   .rearrange("p b f -> p (b f)")).then_inc(steps.sem, 1)
                steps.n += 1
            dve.wait_ge(steps.sem, steps.c * steps.per + steps.n + steps.base)
            hold(dve)
            for b in range(CB):
                nc.vector.bn_aggr(mv_chunk[:, b, :], st6[:, 0, b, :]).then_inc(steps.sem, 1)
                steps.n += 1
            dve.wait_ge(steps.sem, steps.c * steps.per + steps.n + steps.base)
            nc.vector.tensor_copy(mv[:, bslice(c), :], mv_chunk[:, :, :])

        def norm_dve(tag, dve):
            one = chain(dve)
            one(nc.vector.tensor_scalar(small[:, 0, :], mv[:, :, 1], EPS, None, ALU.add))
            nc.vector.tensor_copy(small[:, 2, :], mv[:, :, 0]).then_inc(S("norm_var" + tag), 1)
            dve.wait_ge(S("norm_var" + tag), 1)
            dve.wait_ge(S("norm_std" + tag), 1)
            one(nc.vector.reciprocal(small[:, 1, :], small[:, 1, :]))

            def body(i):
                for s in range(2 * CB):
                    b = i * 2 * CB + s
                    blk = x_nm[:, bass.ds(b, 1), :].rearrange("p b f -> p (b f)")
                    nc.vector.tensor_scalar(blk, blk, small[:, 2, bass.ds(b, 1)], small[:, 1, bass.ds(b, 1)],
                                            ALU.subtract, ALU.mult).then_inc(S("normed" + tag), 1)
            turns(dve, NODE_ITERS, body)

        def norm_act(tag, act):
            act.wait_ge(S("norm_var" + tag), 1)
            nc.scalar.activation(small[:, 1, :], small[:, 0, :], ACT.Sqrt).then_inc(S("norm_std" + tag), 1)

        def store_norm_sp(tag, sp, dst):
            def body(i):
                sp.wait_ge(S("normed" + tag), (i + 1) * 2 * CB)
                sp.dma_start(dst[bass.ds(i * 2 * CN, 2 * CN), 0:P].rearrange("(b p) f -> p b f", p=P),
                             x_nm[:, bass.ds(i * 2 * CB, 2 * CB), :]).then_inc(S("stored" + tag), 16)
            turns(sp, NODE_ITERS, body)
            sp.wait_ge(S("stored" + tag), 16 * NODE_ITERS)

        def safe_inverse_dve(tag, dve):
            one = chain(dve)
            one(nc.vector.tensor_copy(small[:, 0, :], acc_nm[:, :, P]))
            one(nc.vector.tensor_scalar(small[:, 2, :], small[:, 0, :], 0.0, None, ALU.is_gt))
            one(nc.vector.tensor_tensor(small[:, 1, :], small[:, 0, :], small[:, 2, :], ALU.mult))
            one(nc.vector.tensor_scalar(small[:, 3, :], small[:, 2, :], -1.0, 1.0, ALU.mult, ALU.add))
            one(nc.vector.tensor_tensor(small[:, 1, :], small[:, 1, :], small[:, 3, :], ALU.add))
            one(nc.vector.reciprocal(small[:, 1, :], small[:, 1, :]))
            one(nc.vector.tensor_tensor(small[:, 1, :], small[:, 1, :], small[:, 2, :], ALU.mult))

        def batch_dve(tag, dve, src, gamma, beta, scale, shift):
            one = chain(dve)

            for n in range(NST):
                last = nc.vector.bn_stats(bst[:, n, :], src[:, n * ST:(n + 1) * ST])
            one(last)
            one(nc.vector.bn_aggr(bmv[:, :], bst[:, :, :].rearrange("p n s -> p (n s)")))
            nc.vector.tensor_scalar(bmv[:, 1:2], bmv[:, 1:2], EPS, None, ALU.add).then_inc(S("batch_var" + tag), 1)
            dve.wait_ge(S("batch_std" + tag), 1)
            one(nc.vector.reciprocal(scale, scale))
            one(nc.vector.tensor_tensor(scale, scale, gamma, ALU.mult))
            one(nc.vector.tensor_tensor(shift, bmv[:, 0:1], scale, ALU.mult))
            one(nc.vector.tensor_tensor(shift, beta, shift, ALU.subtract))

        def batch_act(tag, act, scale):
            act.wait_ge(S("batch_var" + tag), 1)
            nc.scalar.activation(scale, bmv[:, 1:2], ACT.Sqrt).then_inc(S("batch_std" + tag), 1)

        LIN_B, B_R, B_Z, B_IN, B_HN, HY_B, HY_G, HY_BE, AT_G, AT_BE, N1_B, SCALE, SHIFT = range(13)

        def col(j):
            return cols[:, j:j + 1]

        def vec(ap):
            return ap.rearrange("(p a) -> p a", a=1)

        def tmp(j, s):
            return big[:, NP + (2 * j + s) * CN:NP + (2 * j + s + 1) * CN]

        def tmp_h0(j, s):
            return big[:, h0_slots + (2 * j + s) * CN:h0_slots + (2 * j + s + 1) * CN]

        def tmp_acc(j, s):
            return acc[:, (2 * j + s) * CN:(2 * j + s + 1) * CN]

        block = ctx.enter_context(nc.Block())

        @block.sync
        def _(sp):
            sp.wait_ge(S("edges_padded"), 2)
            for k, name in enumerate(("dst", "src")):
                sp.dma_start(edge_end[k][0:E_FULL, :], d[name][0:E_FULL * EC]
                             .rearrange("(p c) -> p c", c=EC)).then_inc(S("edges_in"), 16)
                sp.dma_start(edge_end[k][E_FULL:E_FULL + 1, 0:E_REST], d[name][E_FULL * EC:E]
                             .rearrange("(p c) -> p c", p=1)).then_inc(S("edges_in"), 16)
            sp.dma_start(raw_w[:, 0, :], d["L0_gnn_lin_w"]).then_inc(S("weights_in"), 16)
            sp.dma_start(raw_w[:, 1:4, :], d["L0_gnn_w_ih"].rearrange("(m p) f -> p m f", p=P)).then_inc(S("weights_in"), 16)
            sp.dma_start(raw_w[:, 4:7, :], d["L0_gnn_w_hh"].rearrange("(m p) f -> p m f", p=P)).then_inc(S("weights_in"), 16)
            sp.dma_start(raw_w[:, 7:10, :], d["L0_gnn_weight"].rearrange("m p f -> p m f")).then_inc(S("weights_in"), 16)
            sp.dma_start(w_hyper[:, :], d["L1_gnn_W"]).then_inc(S("weights_in"), 16)
            for j, ap in ((LIN_B, d["L0_gnn_lin_b"]), (13, d["L0_gnn_b_ih"][0:P]), (14, d["L0_gnn_b_ih"][P:2 * P]),
                          (B_IN, d["L0_gnn_b_ih"][2 * P:3 * P]), (15, d["L0_gnn_b_hh"][0:P]),
                          (16, d["L0_gnn_b_hh"][P:2 * P]), (B_HN, d["L0_gnn_b_hh"][2 * P:3 * P]),
                          (HY_B, d["L1_gnn_b"]), (HY_G, d["L1_gnn_gamma"]), (HY_BE, d["L1_gnn_beta"]),
                          (AT_G, d["L2_gnn_gamma"]), (AT_BE, d["L2_gnn_beta"]), (N1_B, d["L3_gnn_bn1"])):
                sp.dma_start(col(j), vec(ap)).then_inc(S("vectors_in"), 16)
            sp.dma_start(row0[:, 0:P], d["L3_gnn_be2"].rearrange("(a n) -> a n", a=1)).then_inc(S("vectors_in"), 16)
            sp.dma_start(row0[:, P:2 * P], d["L3_gnn_bn2"].rearrange("(a n) -> a n", a=1)).then_inc(S("vectors_in"), 16)
            sp.wait_ge(S("x_zero"), 1)
            sp.dma_start(x_nm[:, 0:NB - 1, :], d["x"][0:(NB - 1) * P, :].rearrange("(b p) f -> p b f", p=P)).then_inc(S("x_in"), 16)
            sp.dma_start(x_nm[0:N - (NB - 1) * P, NB - 1, :], d["x"][(NB - 1) * P:N, :]).then_inc(S("x_in"), 16)
            sp.wait_ge(S("consts"), 1)
            sp.dma_start(table[3][:, P:P + 1].rearrange("(b p) f -> p (b f)", p=P), ones[:, 0:NBP],
                         allow_slow_non_contiguous=True).then_inc(S("const_columns"), 16)
            sp.dma_start(table[4][0:N, P:P + 1], d["L1_gnn_hyperedge_weight"].rearrange("(n a) -> n a", a=1),
                         allow_slow_non_contiguous=True).then_inc(S("const_columns"), 16)
            for k in range(2):
                sp.wait_ge(S("list_fill"), 1)
                sp.dma_start(edge_list[k][0:P * T, :].rearrange("(p t) a -> p (t a)", p=P),
                             fill).then_inc(S("lists_empty"), 16)
            for k in range(2):
                sp.wait_ge(S("addr_ready"), k + 1)
                sp.wait_ge(S("trash_ready"), 1)
                sp.dma_start(slot_addr[k][E_FULL:E_FULL + 1, E_REST:EC], trash[0:1, :]).then_inc(S("trash_set" + str(k)), 16)
            def h0_out(i):
                sp.wait_ge(S("h0_staged"), 2 * i + 2)
                sp.dma_start(table[0][bass.ds(i * 2 * CN, 2 * CN), :].rearrange("(b p) f -> p b f", p=P),
                             stage_rows[:, bass.ds(i * 2 * CB, 2 * CB), :]).then_inc(S("h0_stored"), 16)
            turns(sp, NODE_ITERS, h0_out)
            sp.wait_ge(S("h0_stored"), 16 * NODE_ITERS)
            sp.wait_ge(S("const_columns"), 32)
            end_stage(sp, nc.sync)
            for k in range(2):
                if k:
                    sp.wait_ge(S("list_unpacked"), 1)
                sp.dma_start(list_in, edge_list[k][0:P * T, :].rearrange("(p t) a -> p (t a)", p=P)).then_inc(S("list_in"), 16)
                sp.wait_ge(S("list_in"), 16 * (k + 1))
            end_stage(sp, nc.sync)

            for p in range(GRU_LAYERS):
                end_stage(sp, nc.sync)
                if p < GRU_LAYERS - 1:
                    def rows_out(i, p=p):
                        wait(sp, Q("flip_taken_gru", p), 2 * i + 2)
                        sp.dma_start(table[p + 1][bass.ds(i * 2 * CN, 2 * CN), :].rearrange("(b p) f -> p b f", p=P),
                                     stage_rows[:, bass.ds(i * 2 * CB, 2 * CB), :]).then_inc(Q("stored_gru", p).sem, 16)
                    turns(sp, NODE_ITERS, rows_out)
                    wait(sp, Q("stored_gru", p), 16 * NODE_ITERS)
                end_stage(sp, nc.sync)
            for ap, src in ((w_att[:, 0:P], d["L2_gnn_kernel"]), (w_att[:, P:2 * P], d["L2_gnn_kernel1"]),
                            (w_att[:, 2 * P:3 * P], d["L2_gnn_kernel2"]),
                            (w_e1[:, 0:P], d["L3_gnn_We1"][0:P, :]), (w_e1[:, P:2 * P], d["L3_gnn_We1"][P:2 * P, :]),
                            (w_e2, d["L3_gnn_We2"]), (w_n1[:, 0:P], d["L3_gnn_Wn1"][0:P, :]),
                            (w_n1[:, P:2 * P], d["L3_gnn_Wn1"][P:2 * P, :]), (w_n2, d["L3_gnn_Wn2"]),
                            (be1_rows, d["L3_gnn_be1"].rearrange("(a n) -> a n", a=1).to_broadcast([P, P]))):
                sp.dma_start(ap, src).then_inc(S("late_weights"), 16)
            store_norm_sp("_ln0", sp, table[3])
            sp.wait_ge(S("late_weights"), 160)
            end_stage(sp, nc.sync)
            end_stage(sp, nc.sync)
            sp.wait_ge(S("degree_ready"), 1)
            sp.dma_start(degree_row.rearrange("(b p) a -> p (b a)", p=P), small[:, 4, :],
                         allow_slow_non_contiguous=True).then_inc(S("degree_out"), 16)

            def hyper_out(i):
                sp.wait_ge(S("hyper_scaled"), (i + 1) * 2 * CB)
                sp.dma_start(table[4][bass.ds(i * 2 * CN, 2 * CN), 0:P].rearrange("(b p) f -> p b f", p=P),
                             stage_rows[:, bass.ds(i * 2 * CB, 2 * CB), :]).then_inc(S("hyper_stored"), 16)
            turns(sp, NODE_ITERS, hyper_out)
            sp.wait_ge(S("hyper_stored"), 16 * NODE_ITERS)
            sp.wait_ge(S("degree_out"), 16)
            end_stage(sp, nc.sync)
            end_stage(sp, nc.sync)
            end_stage(sp, nc.sync)
            end_stage(sp, nc.sync)
            end_stage(sp, nc.sync)
            end_stage(sp, nc.sync)
            end_stage(sp, nc.sync)
            sp.wait_ge(S("score_cols"), 1)

            def att_out(i):
                sp.dma_start(table[5][bass.ds(i * 2 * CN, 2 * CN), :].rearrange("(b p) f -> p b f", p=P),
                             stage_nm[:, bass.ds(i * 2 * CB, 2 * CB), 0:P + 3]).then_inc(S("att_stored"), 16)
            turns(sp, NODE_ITERS, att_out)
            sp.wait_ge(S("att_stored"), 16 * NODE_ITERS)
            end_stage(sp, nc.sync)
            end_stage(sp, nc.sync)
            end_stage(sp, nc.sync)
            end_stage(sp, nc.sync)

            def edge_out(i):
                sp.wait_ge(S("p_staged"), 2 * i + 2)
                sp.dma_start(table[6][bass.ds(i * 2 * CN, 2 * CN), :].rearrange("(b p) f -> p b f", p=P),
                             stage_rows[:, bass.ds(i * 2 * CB, 2 * CB), :]).then_inc(S("p_stored"), 16)
            turns(sp, NODE_ITERS, edge_out)
            sp.wait_ge(S("p_stored"), 16 * NODE_ITERS)
            end_stage(sp, nc.sync)
            end_stage(sp, nc.sync)
            sp.dma_start(stage[0:1, 0:NP], degree_row.rearrange("(a n) o -> a (n o)", a=1)).then_inc(S("degree_in"), 16)
            end_stage(sp, nc.sync)
            full = NB - 1
            for n in range(full // (2 * CB)):
                sp.wait_ge(S("normed_ln3"), (n + 1) * 2 * CB)
                sp.dma_start(d["out"][n * 2 * CN:(n + 1) * 2 * CN, :].rearrange("(b p) f -> p b f", p=P),
                             x_nm[:, n * 2 * CB:(n + 1) * 2 * CB, :]).then_inc(S("out_stored"), 16)
            sp.wait_ge(S("normed_ln3"), NB)
            sp.dma_start(d["out"][full * P:N, :], x_nm[0:N - full * P, full, :]).then_inc(S("out_stored"), 16)
            sp.wait_ge(S("out_stored"), 16 * (full // (2 * CB) + 1))
            end_stage(sp, nc.sync)

        @block.gpsimd
        def _(pool):
            step = Steps(pool, "const_steps", 0)
            step(nc.gpsimd.memset(ones[:, :], 1.0))
            step(nc.gpsimd.memset(ident[:, :], 0.0))
            step(nc.gpsimd.affine_select(out=ident[:, :], in_=ident[:, :], compare_op=ALU.not_equal, fill=1.0,
                                         base=0, pattern=[[-1, P]], channel_multiplier=1))
            step(nc.gpsimd.affine_select(out=lower[:, :], in_=ones[:, :], compare_op=ALU.is_ge, fill=0.0,
                                         base=-1, pattern=[[1, P]], channel_multiplier=-1))
            step(nc.gpsimd.affine_select(out=sel_blocks, in_=ones[:, :], compare_op=ALU.is_ge, fill=0.0,
                                         base=-1, pattern=[[0, P]], channel_multiplier=1))
            step(nc.gpsimd.affine_select(out=sel_blocks, in_=sel_blocks, compare_op=ALU.is_ge, fill=0.0,
                                         base=NB - 1, pattern=[[0, P]], channel_multiplier=-1))
            step(nc.gpsimd.iota(iota[:, :], pattern=[[1, P]], base=0, channel_multiplier=0,
                                allow_small_or_imprecise_dtypes=True))
            step(nc.gpsimd.iota(tile_iota, pattern=[[1, T]], base=0, channel_multiplier=0,
                                allow_small_or_imprecise_dtypes=True))
            nc.gpsimd.memset(rows[:, :, :], 0.0).then_inc(S("consts"), 1)
            nc.gpsimd.iota(trash, pattern=[[1, EC - E_REST]], base=P * T, channel_multiplier=0).then_inc(S("trash_ready"), 1)
            pool.wait_ge(S("lists_empty"), 32)
            for k in range(2):
                def body(i, k=k):
                    for h in range(2):
                        pool.wait_ge(S("ring_filled"), 2 * (SCATTER_ITERS * k + i) + h + 1)
                        pool.sem_inc(rows_opened, 1)
                        for u in range(SC):
                            s = h * SC + u
                            nc.gpsimd.indirect_dma_start(
                                edge_list[k], bass.IndirectOffsetOnAxis(idx_ring[:, s:s + 1], 0),
                                val_ring[:, s:s + 1], None).then_inc(S(f"scattered{h}"), 16)
                with pool.Fori(0, SCATTER_ITERS) as i:
                    body(i)
            for h in range(2):
                pool.wait_ge(S(f"scattered{h}"), 16 * SC * 2 * SCATTER_ITERS)
            end_stage(pool, nc.gpsimd)
            end_stage(pool, nc.gpsimd)
            follow = [1, 1, 1 + 1, 1, 5 + 1, 3, 2]
            for p in range(7):
                pass_pool(p, pool)
                end_stage(pool, nc.gpsimd)
                for _ in range(follow[p]):
                    end_stage(pool, nc.gpsimd)

        @block.scalar
        def _(act):
            for k in range(2):
                act.wait_ge(S("addr_ready"), k + 1)
                act.wait_ge(S("trash_set" + str(k)), 16)

                def body(i, k=k, first=False):
                    for h in range(2):
                        if not first:
                            act.wait_ge(S(f"scattered{h}"), 16 * SC * (SCATTER_ITERS * k + i))
                        c = 2 * i + h
                        nc.scalar.copy(idx_ring[:, h * SC:(h + 1) * SC], slot_addr[k][:, bass.ds(SC * c, SC)])\
                            .then_inc(S("ring_idx"), 1)
                        act.wait_ge(S("ring_idx"), 2 * SCATTER_ITERS * k + c + 1)
                        nc.scalar.copy(val_ring[:, h * SC:(h + 1) * SC], packed[k][:, bass.ds(SC * c, SC)])\
                            .then_inc(S("ring_filled"), 1)
                body(0, first=(k == 0))
                with act.Fori(1, SCATTER_ITERS) as i:
                    body(i)
            end_stage(act, nc.scalar)
            end_stage(act, nc.scalar)

            for p in range(GRU_LAYERS):
                pass_act(p, act)
                end_stage(act, nc.scalar)

                def keep(c, s, p=p):
                    wait(act, Q("h_ready", p), c + 1)
                    nc.scalar.copy(x_fm[:, cslice(c)], tmp(6, s)).then_inc(Q("h_kept", p).sem, 1)
                    wait(act, Q("flip_done_gru", p), c + 1)
                    nc.scalar.copy(stage_rows[:, bslice(c), :].rearrange("p b f -> p (b f)"),
                                   tslot(s)).then_inc(Q("flip_taken_gru", p).sem, 1)

                def gates_all(i, p=p):
                    for s in range(2):
                        c = 2 * i + s
                        wait(act, Q("rz_ready", p), c + 1)
                        wait(act, Q("n_in", p), c - 1)
                        nc.scalar.activation(tmp(0, s), ps[:, s, 0:CN], ACT.Sigmoid, bias=col(B_R)).then_inc(Q("r_ready", p).sem, 1)
                        wait(act, Q("h_ready", p), c - 1)
                        nc.scalar.activation(tmp(1, s), ps[:, s, CN:2 * CN], ACT.Sigmoid, bias=col(B_Z)).then_inc(Q("z_ready", p).sem, 1)
                        wait(act, Q("n_in", p), c + 1)
                        nc.scalar.activation(tmp(3, s), tmp(2, s), ACT.Tanh, bias=col(B_IN)).then_inc(Q("n_ready", p).sem, 1)
                        if p < GRU_LAYERS - 1 and not (isinstance(i, int) and s == 0):
                            keep(c - 1, 1 - s)
                turns(act, NODE_ITERS, gates_all)
                if p < GRU_LAYERS - 1:
                    keep(2 * NODE_ITERS - 1, 1)
                end_stage(act, nc.scalar)
            norm_act("_ln0", act)
            end_stage(act, nc.scalar)
            pass_act(3, act)
            end_stage(act, nc.scalar)
            end_stage(act, nc.scalar)
            pass_act(4, act)
            end_stage(act, nc.scalar)

            def hyper_product(i):
                for s in range(2):
                    c = 2 * i + s
                    act.wait_ge(S("flip_done_hy"), c + 1)
                    wait(act, S("hy_product"), c - 1)
                    nc.scalar.copy(tmp(1, s), tslot(s)).then_inc(S("flip_taken_hy"), 1)
                    act.wait_ge(S("hy_product"), c + 1)
                    nc.scalar.activation(big[:, cslice(c)], ps[:, s, 0:CN], ACT.Identity, bias=col(HY_B))\
                        .then_inc(S("hy_out"), 1)
            turns(act, NODE_ITERS, hyper_product)
            batch_act("_hy", act, col(SCALE))
            end_stage(act, nc.scalar)

            def hyper_relu(i):
                for s in range(2):
                    c = 2 * i + s
                    wait(act, S("flip_done_hr"), c - 1)
                    nc.scalar.activation(tmp(0, s), big[:, cslice(c)], ACT.Relu,
                                         bias=col(SHIFT), scale=col(SCALE)).then_inc(S("hy_relu"), 1)
            turns(act, NODE_ITERS, hyper_relu)
            end_stage(act, nc.scalar)
            norm_act("_ln1", act)
            end_stage(act, nc.scalar)

            def copy_fm(tag):
                def body(i):
                    for s in range(2):
                        c = 2 * i + s
                        act.wait_ge(S("flip_done" + tag), c + 1)
                        nc.scalar.copy(x_fm[:, cslice(c)], tslot(s)).then_inc(S("flip_taken" + tag), 1)
                turns(act, NODE_ITERS, body)

            copy_fm("_x2")
            batch_act("_at", act, col(SCALE))
            end_stage(act, nc.scalar)

            def scores(i):
                for s in range(2):
                    c = 2 * i + s
                    act.wait_ge(S("s_ready"), c + 1)
                    nc.scalar.activation(u1_rows[:, cslice(c)], ps[:, 2 + s, 0:CN], ACT.Tanh).then_inc(S("act_sc"), 1)
                    nc.scalar.activation(small[:, 4, bslice(c)], ps[:, 2 + s, CN:CN + CB], ACT.Tanh).then_inc(S("act_sc"), 1)
                    nc.scalar.copy(stage_nm[:, bslice(c), 0:P],
                                   tslot(s).rearrange("p (b f) -> p b f", f=P)).then_inc(S("s_taken"), 1)
            turns(act, NODE_ITERS, scores)
            act.wait_ge(S("act_sc"), 4 * NODE_ITERS)
            nc.scalar.activation(u2_rows, u1_rows, ACT.Exp, scale=0.01).then_inc(S("act_exp"), 1)
            nc.scalar.activation(stage_nm[:, :, P + 1], small[:, 4, :], ACT.Exp).then_inc(S("act_exp"), 1)
            nc.scalar.activation(stage_nm[:, :, P + 2], small[:, 4, :], ACT.Exp, scale=0.01).then_inc(S("act_exp"), 1)
            act.wait_ge(S("act_exp"), 3)
            nc.scalar.activation(u1_rows, u1_rows, ACT.Exp).then_inc(S("act_exp"), 1)
            end_stage(act, nc.scalar)
            end_stage(act, nc.scalar)
            pass_act(5, act)
            end_stage(act, nc.scalar)

            def att_relu(i):
                for s in range(2 * CB):
                    b = i * 2 * CB + s
                    if s == 0 and not isinstance(i, int):
                        act.wait_ge(S("at_added"), 2 * i)
                    if s == 0 and isinstance(i, int):
                        act.wait_ge(S("inverse_done_at"), 1)
                    nc.scalar.activation(x_fm[:, s * P:(s + 1) * P], acc_nm[:, bass.ds(b, 1), 0:P]
                                         .rearrange("p b f -> p (b f)"), ACT.Relu,
                                         scale=small[:, 1, bass.ds(b, 1)]).then_inc(S("at_relu"), 1)
            turns(act, NODE_ITERS, att_relu)
            end_stage(act, nc.scalar)
            norm_act("_ln2", act)
            end_stage(act, nc.scalar)

            def edge_halves(i):
                for s in range(2):
                    c = 2 * i + s
                    act.wait_ge(S("flip_done_x3"), c + 1)
                    wait(act, S("q_taken"), c - 1)
                    nc.scalar.copy(tmp(1, s), tslot(s)).then_inc(S("flip_taken_x3"), 1)
                    act.wait_ge(S("pq_ready"), c + 1)
                    nc.scalar.copy(stage_rows[:, bslice(c), :],
                                   ps[:, s, :].rearrange("p (b h f) -> p b h f", b=CB, h=2)[:, :, 0, :]
                                   ).then_inc(S("p_staged"), 1)
            turns(act, NODE_ITERS, edge_halves)
            end_stage(act, nc.scalar)
            pass_act(6, act)
            end_stage(act, nc.scalar)

            def node_mlp(i):
                for s in range(2):
                    c = 2 * i + s
                    act.wait_ge(S("agg_ready"), c + 1)
                    wait(act, S("hid_ready"), c - 1)
                    nc.scalar.copy(tmp(0, s), ps[:, s, 0:CN]).then_inc(S("agg_copied"), 1)
                    act.wait_ge(S("hid_ready"), c + 1)
                    wait(act, S("mesh_ready"), c - 1)
                    nc.scalar.activation(tmp(1, s), ps[:, 2 + s, 0:CN], ACT.Relu, bias=col(N1_B)).then_inc(S("hid_copied"), 1)
            turns(act, NODE_ITERS, node_mlp)
            end_stage(act, nc.scalar)
            norm_act("_ln3", act)
            end_stage(act, nc.scalar)

        @block.tensor
        def _(pe):
            pe.wait_ge(S("consts"), 1)
            for k in range(2):
                pe.wait_ge(S("counted"), k + 1)
                nc.tensor.matmul(ps[:, 0, 0:1], count_b, ones[:, 0:1], start=True, stop=True).then_inc(S("totals"), 1)
                pe.wait_ge(S("tiles_b"), k + 1)
                nc.tensor.matmul(ps[:, 1, 0:1], lower[:, :], tiny[:, 2:3], start=True, stop=True).then_inc(S("bases"), 1)
                pe.wait_ge(S("diag_ready"), k + 1)
                nc.tensor.matmul(ps[:, 2, 0:MASKB], lower[:, :], count_b, start=True, stop=False)
                nc.tensor.matmul(ps[:, 2, 0:MASKB], ones[:, :], diag, start=False, stop=True).then_inc(S("places"), 1)
                for j in range(2):
                    last = nc.tensor.matmul(ps[:, 3 + j, 0:T // 2], sel_blocks,
                                            tile_ge[:, j * (T // 2):(j + 1) * (T // 2)], start=True, stop=True)
                last.then_inc(S("tile_blocks"), 1)
                if k == 0:
                    pe.wait_ge(S("weights_in"), 80)
                    for j in range(10):
                        last = nc.tensor.transpose(ps[:, 5 + j // 4, (j % 4) * P:(j % 4 + 1) * P], raw_w[:, j, :],
                                                   ident[:, :])
                    last.then_inc(S("w_flipped"), 1)
                    pe.wait_ge(S("w_copied"), 1)
                    for l in range(GRU_LAYERS):
                        last = nc.tensor.matmul(ps[:, 5 + l, 0:3 * P], tr_w[:, 3 + l, :],
                                                tr_w[:, 0:3, :].rearrange("p m f -> p (m f)"), start=True, stop=True)
                    last.then_inc(S("w_combined"), 1)
            def h0(i):
                for s in range(2):
                    c = 2 * i + s
                    flip_pe("_h0x", pe, tmp_h0(0, s), c, s, S("cut_h0x"))
                    pe.wait_ge(S("flip_taken_h0x"), c + 1)
                    nc.tensor.matmul(ps[:, s, 0:CN], w_lin[:, :], tmp_h0(1, s), start=True, stop=True)\
                        .then_inc(S("h0_product"), 1)
                    pe.wait_ge(S("h0_ready"), c + 1)
                    for b in range(CB):
                        last = nc.tensor.transpose(ps[:, 6 + s, b * P:(b + 1) * P],
                                                   tmp_h0(2, s)[:, b * P:(b + 1) * P], ident[:, :])
                    last.then_inc(S("h0_rows"), 1)
            turns(pe, NODE_ITERS, h0)
            end_stage(pe, nc.tensor)
            end_stage(pe, nc.tensor)

            for p in range(GRU_LAYERS):
                pass_pe(p, pe)
                end_stage(pe, nc.tensor)

                def flip_new(c, s, p=p):
                    flip_pe(p, pe, tmp(6, s), c, s, Q("h_ready", p))

                def gru(i, p=p):
                    for s in range(2):
                        c = 2 * i + s
                        wait(pe, Q("z_ready", p), c - 1)
                        for j in range(2):
                            nc.tensor.matmul(ps[:, s, j * CN:(j + 1) * CN], w_comb[:, p, j * P:(j + 1) * P],
                                             acc[:, cslice(c)], start=True, stop=False)
                            last = nc.tensor.matmul(ps[:, s, j * CN:(j + 1) * CN], w_hh[:, j * P:(j + 1) * P],
                                                    x_fm[:, cslice(c)], start=False, stop=True)
                        last.then_inc(Q("rz_ready", p).sem, 1)
                        wait(pe, Q("n_in", p), c - 1)
                        nc.tensor.matmul(ps[:, 2 + s, 0:CN], w_comb[:, p, 2 * P:3 * P], acc[:, cslice(c)],
                                         start=True, stop=True)
                        nc.tensor.matmul(ps[:, 2 + s, CN:2 * CN], w_hh[:, 2 * P:3 * P], x_fm[:, cslice(c)],
                                         start=True, stop=True).then_inc(Q("nh_ready", p).sem, 1)
                        if not (isinstance(i, int) and s == 0):
                            flip_new(c - 1, 1 - s)
                turns(pe, NODE_ITERS, gru)
                flip_new(2 * NODE_ITERS - 1, 1)
                end_stage(pe, nc.tensor)
            end_stage(pe, nc.tensor)
            pass_pe(3, pe)
            end_stage(pe, nc.tensor)
            end_stage(pe, nc.tensor)
            pass_pe(4, pe)
            end_stage(pe, nc.tensor)

            def hyper_product(i):
                for s in range(2):
                    c = 2 * i + s
                    flip_pe("_hy", pe, tmp(0, s), c, s, S("hy_scaled"))
                    pe.wait_ge(S("flip_taken_hy"), c + 1)
                    wait(pe, S("hy_out"), c - 1)
                    nc.tensor.matmul(ps[:, s, 0:CN], w_hyper[:, :], tmp(1, s), start=True, stop=True).then_inc(S("hy_product"), 1)
            turns(pe, NODE_ITERS, hyper_product)
            end_stage(pe, nc.tensor)

            def hyper_rows(i):
                for s in range(2):
                    c = 2 * i + s
                    flip_pe("_hr", pe, tmp(0, s), c, s, S("hy_relu"))
            turns(pe, NODE_ITERS, hyper_rows)
            end_stage(pe, nc.tensor)
            end_stage(pe, nc.tensor)

            def to_fm(i):
                for s in range(2):
                    c = 2 * i + s
                    flip_pe("_x2", pe, tmp(0, s), c, s, S("cut_x2"))
            turns(pe, NODE_ITERS, to_fm)
            end_stage(pe, nc.tensor)

            def scores(i):
                for s in range(2):
                    c = 2 * i + s
                    pe.wait_ge(S("xn_ready"), c + 1)
                    for j in range(2):
                        last = nc.tensor.matmul(ps[:, s, j * CN:(j + 1) * CN], w_att[:, (1 + j) * P:(2 + j) * P],
                                                tmp_acc(0, s), start=True, stop=True)
                    last.then_inc(S("sc_ready"), 1)
                    wait(pe, S("s_taken"), c - 1)
                    for b in range(CB):
                        nc.tensor.matmul(ps[:, 4 + s, b * P:(b + 1) * P], tmp_acc(0, s)[:, b * P:(b + 1) * P],
                                         w_att[:, 0:P], start=True, stop=True)
                    pe.wait_ge(S("sc_prod"), c + 1)
                    nc.tensor.matmul(ps[:, 2 + s, 0:CN], ones[:, :], tmp_acc(1, s), start=True, stop=True)
                    for b in range(CB):
                        last = nc.tensor.matmul(ps[:, 2 + s, CN + b:CN + b + 1],
                                                tmp_acc(2, s)[:, b * P:(b + 1) * P], ones[:, 0:1],
                                                start=True, stop=True)
                    last.then_inc(S("s_ready"), 1)
            turns(pe, NODE_ITERS, scores)
            end_stage(pe, nc.tensor)
            end_stage(pe, nc.tensor)
            pass_pe(5, pe)
            end_stage(pe, nc.tensor)
            end_stage(pe, nc.tensor)
            end_stage(pe, nc.tensor)

            def edge_halves(i):
                for s in range(2):
                    c = 2 * i + s
                    flip_pe("_x3", pe, tmp(0, s), c, s, S("cut_x3"))
                    pe.wait_ge(S("flip_taken_x3"), c + 1)
                    wait(pe, S("p_staged"), c - 1)
                    wait(pe, S("q_taken"), c - 1)
                    for b in range(CB):
                        last = nc.tensor.matmul(ps[:, s, b * CN:(b + 1) * CN], tmp(1, s)[:, b * P:(b + 1) * P],
                                                w_e1, start=True, stop=True)
                    last.then_inc(S("pq_ready"), 1)
            turns(pe, NODE_ITERS, edge_halves)
            end_stage(pe, nc.tensor)
            pass_pe(6, pe)
            end_stage(pe, nc.tensor)
            pe.wait_ge(S("degree_in"), 16)

            def node_mlp(i):
                for s in range(2):
                    c = 2 * i + s
                    wait(pe, S("agg_copied"), c - 1)
                    nc.tensor.matmul(ps[:, s, 0:CN], w_e2, acc[:, cslice(c)], start=True, stop=False)
                    nc.tensor.matmul(ps[:, s, 0:CN], row0[0:1, 0:P], stage[0:1, cslice(c)], start=False, stop=True)\
                        .then_inc(S("agg_ready"), 1)
                    wait(pe, S("hid_copied"), c - 1)
                    nc.tensor.matmul(ps[:, 2 + s, 0:CN], w_n1[:, 0:P], x_fm[:, cslice(c)], start=True, stop=False)
                    pe.wait_ge(S("agg_copied"), c + 1)
                    nc.tensor.matmul(ps[:, 2 + s, 0:CN], w_n1[:, P:2 * P], tmp(0, s), start=False, stop=True)\
                        .then_inc(S("hid_ready"), 1)
                    pe.wait_ge(S("hid_copied"), c + 1)
                    wait(pe, S("mesh_added"), c - 1)
                    for b in range(CB):
                        nc.tensor.matmul(ps[:, 4 + s, b * P:(b + 1) * P], tmp(1, s)[:, b * P:(b + 1) * P], w_n2,
                                         start=True, stop=False)
                        last = nc.tensor.matmul(ps[:, 4 + s, b * P:(b + 1) * P], ones[0:1, :], row0[0:1, P:2 * P],
                                                start=False, stop=True)
                    last.then_inc(S("mesh_ready"), 1)
            turns(pe, NODE_ITERS, node_mlp)
            end_stage(pe, nc.tensor)
            end_stage(pe, nc.tensor)

        @block.vector
        def _(dve):
            nc.vector.memset(edge_end[0], PAD_NODE).then_inc(S("edges_padded"), 1)
            nc.vector.memset(edge_end[1], PAD_NODE).then_inc(S("edges_padded"), 1)
            nc.vector.memset(fill, PAD_LOCAL).then_inc(S("list_fill"), 1)
            nc.vector.memset(x_nm[:, :, :], 0.0).then_inc(S("x_zero"), 1)
            step = chain(dve)
            step(nc.vector.memset(ones_row, 1.0))
            nc.vector.memset(small[:, :, :], 0.0)
            step(nc.vector.memset(count_b, 0.0))
            dve.wait_ge(S("consts"), 1)
            dve.wait_ge(S("edges_in"), 64)
            for k in range(2):
                key, other = edge_end[k], edge_end[1 - k]
                step(nc.vector.tensor_scalar(tmp_int, key, 7, None, ALU.logical_shift_right))
                step(nc.vector.tensor_copy(blk_f, tmp_int))
                step(nc.vector.tensor_scalar(loc_int, key, P - 1, None, ALU.bitwise_and))
                step(nc.vector.scalar_tensor_tensor(packed[k], other, 256.0, loc_int, ALU.mult, ALU.add))
                with dve.Fori(0, NB) as b:
                    nc.vector.tensor_scalar(mask[:, bass.ds(b, 1), :].rearrange("p b c -> p (b c)"), blk_f,
                                            iota[:, bass.ds(b, 1)], None, ALU.is_equal, ALU.add,
                                            accum_out=count_b[:, bass.ds(b, 1)]).then_inc(S("masked"), 1)
                dve.wait_ge(S("masked"), NB * (k + 1))
                dve.sem_inc(S("counted"), 1)
                dve.wait_ge(S("totals"), k + 1)
                step(nc.vector.tensor_scalar(tiny_i[:, 0:1], ps[:, 0, 0:1], float(P - 1), None, ALU.add))
                step(nc.vector.tensor_scalar(tiny_i[:, 1:2], tiny_i[:, 0:1], 7, None, ALU.logical_shift_right))
                nc.vector.tensor_copy(tiny[:, 2:3], tiny_i[:, 1:2]).then_inc(S("tiles_b"), 1)
                dve.wait_ge(S("bases"), k + 1)
                step(nc.vector.tensor_copy(tiny[:, 3:4], ps[:, 1, 0:1]))
                step(nc.vector.tensor_scalar(diag, ident[:, :], tiny[:, 3:4], float(P), ALU.mult, ALU.mult))
                nc.vector.tensor_scalar(tile_ge, tile_iota, tiny[:, 3:4], None, ALU.is_ge).then_inc(S("diag_ready"), 1)
                dve.wait_ge(S("places"), k + 1)
                step(nc.vector.tensor_copy(base, ps[:, 2, 0:MASKB]))
                dve.wait_ge(S("tile_blocks"), k + 1)
                for j in range(2):
                    nc.vector.tensor_copy(block_of[k][:, j * (T // 2):(j + 1) * (T // 2)], ps[:, 3 + j, 0:T // 2])
                step(nc.vector.memset(pos, 0.0))
                with dve.Fori(0, NB) as b:
                    m = mask[:, bass.ds(b, 1), :].rearrange("p b c -> p (b c)")
                    nc.vector.tensor_tensor_scan(scan[:, 0, :], ones_row, m, base[:, bass.ds(b, 1)],
                                                 ALU.mult, ALU.add).then_inc(S("scanned"), 1)
                    dve.wait_ge(S("scanned"), 3 * (NB * k + b) + 1)
                    nc.vector.tensor_tensor(scan[:, 1, :], scan[:, 0, :], m, ALU.mult).then_inc(S("scanned"), 1)
                    dve.wait_ge(S("scanned"), 3 * (NB * k + b) + 2)
                    nc.vector.tensor_tensor(pos, pos, scan[:, 1, :], ALU.add).then_inc(S("scanned"), 1)
                dve.wait_ge(S("scanned"), 3 * NB * (k + 1))
                step(nc.vector.tensor_scalar(tmp_int, pos, -1.0, None, ALU.add))
                step(nc.vector.tensor_scalar(loc_int, tmp_int, P - 1, None, ALU.bitwise_and))
                step(nc.vector.tensor_scalar(tmp_int, tmp_int, 7, None, ALU.arith_shift_right))
                nc.vector.scalar_tensor_tensor(slot_addr[k], loc_int, float(T), tmp_int, ALU.mult, ALU.add)\
                    .then_inc(S("addr_ready"), 1)
                if k == 0:
                    dve.wait_ge(S("w_flipped"), 1)
                    nc.vector.tensor_copy(w_lin[:, :], ps[:, 5, 0:P])
                    nc.vector.tensor_copy(tr_w[:, 0:3, :].rearrange("p m f -> p (m f)"), ps[:, 5, P:4 * P])
                    nc.vector.tensor_copy(w_hh[:, :], ps[:, 6, 0:3 * P])
                    nc.vector.tensor_copy(tr_w[:, 3, :], ps[:, 6, 3 * P:4 * P])
                    nc.vector.tensor_copy(tr_w[:, 4:6, :].rearrange("p m f -> p (m f)"), ps[:, 7, 0:2 * P])\
                        .then_inc(S("w_copied"), 1)
                    dve.wait_ge(S("w_combined"), 1)
                    for l in range(GRU_LAYERS):
                        nc.vector.tensor_copy(w_comb[:, l, :], ps[:, 5 + l, 0:3 * P])
            dve.wait_ge(S("vectors_in"), 16 * 15)
            nc.vector.tensor_tensor(col(B_R), col(13), col(15), ALU.add)
            step(nc.vector.tensor_tensor(col(B_Z), col(14), col(16), ALU.add))
            dve.wait_ge(S("x_in"), 32)
            dve.wait_ge(S("lists_empty"), 32)
            dve.wait_ge(S("trash_set1"), 16)

            def h0(i):
                for s in range(2):
                    c = 2 * i + s
                    cut_dve("_h0x", dve, c, s, tmp_h0(0, s))
                    dve.wait_ge(S("flip_done_h0x"), c + 1)
                    nc.vector.tensor_copy(tmp_h0(1, s), tslot(s)).then_inc(S("flip_taken_h0x"), 1)
                    dve.wait_ge(S("h0_product"), c + 1)
                    nc.vector.tensor_scalar(x_fm[:, cslice(c)], ps[:, s, 0:CN], col(LIN_B), None, ALU.add)
                    nc.vector.tensor_scalar(tmp_h0(2, s), ps[:, s, 0:CN], col(LIN_B), None, ALU.add)\
                        .then_inc(S("h0_ready"), 1)
                    dve.wait_ge(S("h0_rows"), c + 1)
                    nc.vector.tensor_copy(stage_rows[:, bslice(c), :].rearrange("p b f -> p (b f)"), ps[:, 6 + s, 0:CN])\
                        .then_inc(S("h0_staged"), 1)
            turns(dve, NODE_ITERS, h0)
            end_stage(dve, nc.vector)

            step = chain(dve)
            for k in range(2):
                dve.wait_ge(S("list_in"), 16 * (k + 1))
                nc.vector.memset(gather_idx[k][:, T:TP], 0)
                nc.vector.memset(local[k][:, T:TP], float(PAD_LOCAL))
                nc.vector.tensor_scalar(gather_idx[k][:, 0:T], list_in, 8, None, ALU.logical_shift_right)
                step(nc.vector.tensor_scalar(acc[:, 0:T].bitcast(I32), list_in,
                                             255, None, ALU.bitwise_and))
                nc.vector.tensor_copy(local[k][:, 0:T], acc[:, 0:T].bitcast(I32)).then_inc(S("list_unpacked"), 1)
                dve.wait_ge(S("list_unpacked"), k + 1)
            end_stage(dve, nc.vector)

            for p in range(GRU_LAYERS):
                pass_dve(p, dve)
                end_stage(dve, nc.vector)
                last_layer = p == GRU_LAYERS - 1
                steps = Steps(dve, "gru_steps", 3, 3 * NC * p)
                stat = Steps(dve, "gru_stats", 2 * CB)

                def residual(c, s, p=p, stat=stat):
                    stat.chunk(c)
                    blk = x_nm[:, bslice(c), :].rearrange("p b f -> p (b f)")
                    wait(dve, Q("flip_done_gru", p), c + 1)
                    nc.vector.tensor_tensor(blk, blk, tslot(s), ALU.add).then_inc(Q("flip_taken_gru", p).sem, 1)
                    wait(dve, Q("flip_taken_gru", p), c + 1)
                    stats_dve("", dve, c, stat)

                def gru(i, p=p, steps=steps, last_layer=last_layer):
                    for s in range(2):
                        c = 2 * i + s
                        steps.chunk(c)
                        wait(dve, Q("nh_ready", p), c + 1)
                        wait(dve, Q("r_ready", p), c + 1)
                        steps(nc.vector.scalar_tensor_tensor(tmp(4, s), ps[:, 2 + s, CN:2 * CN], col(B_HN),
                                                             tmp(0, s), ALU.add, ALU.mult))
                        nc.vector.tensor_tensor(tmp(2, s), tmp(4, s), ps[:, 2 + s, 0:CN], ALU.add)\
                            .then_inc(Q("n_in", p).sem, 1)
                        if last_layer and not (isinstance(i, int) and s == 0):
                            residual(c - 1, 1 - s)
                        wait(dve, Q("n_ready", p), c + 1)
                        steps(nc.vector.tensor_tensor(tmp(5, s), x_fm[:, cslice(c)], tmp(3, s), ALU.subtract))
                        steps(nc.vector.tensor_tensor(tmp(5, s), tmp(5, s), tmp(1, s), ALU.mult))
                        wait(dve, Q("flip_done_gru", p), c - 1)
                        if not last_layer:
                            wait(dve, Q("h_kept", p), c - 1)
                        nc.vector.tensor_tensor(tmp(6, s), tmp(5, s), tmp(3, s), ALU.add).then_inc(Q("h_ready", p).sem, 1)
                turns(dve, NODE_ITERS, gru)
                if last_layer:
                    residual(2 * NODE_ITERS - 1, 1)
                end_stage(dve, nc.vector)
            norm_dve("_ln0", dve)
            end_stage(dve, nc.vector)
            pass_dve(3, dve)
            end_stage(dve, nc.vector)

            nc.vector.tensor_copy(small[:, 4, :], acc_nm[:, :, P]).then_inc(S("degree_ready"), 1)
            safe_inverse_dve("_b", dve)

            def hyper_scale(i):
                for s in range(2 * CB):
                    b = i * 2 * CB + s
                    nc.vector.tensor_scalar(stage_rows[:, bass.ds(b, 1), :].rearrange("p b f -> p (b f)"),
                                            acc_nm[:, bass.ds(b, 1), 0:P].rearrange("p b f -> p (b f)"),
                                            small[:, 1, bass.ds(b, 1)], None, ALU.mult).then_inc(S("hyper_scaled"), 1)
            turns(dve, NODE_ITERS, hyper_scale)
            end_stage(dve, nc.vector)
            pass_dve(4, dve)
            end_stage(dve, nc.vector)

            safe_inverse_dve("_d", dve)

            def node_scale(i):
                for s in range(2):
                    c = 2 * i + s
                    wait(dve, S("flip_done_hy"), c - 1)
                    for b in range(CB):
                        last = nc.vector.tensor_scalar(tmp(0, s)[:, b * P:(b + 1) * P],
                                                       acc_nm[:, bass.ds(c * CB + b, 1), 0:P].rearrange("p b f -> p (b f)"),
                                                       small[:, 1, bass.ds(c * CB + b, 1)], None, ALU.mult)
                    last.then_inc(S("hy_scaled"), 1)
            turns(dve, NODE_ITERS, node_scale)
            dve.wait_ge(S("hy_out"), 2 * NODE_ITERS)
            batch_dve("_hy", dve, big, col(HY_G), col(HY_BE), col(SCALE), col(SHIFT))
            end_stage(dve, nc.vector)

            stat = Steps(dve, "hr_steps", 2 * CB)

            def hyper_residual(i):
                for s in range(2):
                    c = 2 * i + s
                    stat.chunk(c)
                    blk = x_nm[:, bslice(c), :].rearrange("p b f -> p (b f)")
                    dve.wait_ge(S("flip_done_hr"), c + 1)
                    nc.vector.tensor_tensor(blk, blk, tslot(s), ALU.add).then_inc(S("flip_taken_hr"), 1)
                    dve.wait_ge(S("flip_taken_hr"), c + 1)
                    stats_dve("", dve, c, stat)
            turns(dve, NODE_ITERS, hyper_residual)
            end_stage(dve, nc.vector)
            norm_dve("_ln1", dve)
            end_stage(dve, nc.vector)

            def cut_x2(i):
                for s in range(2):
                    cut_dve("_x2", dve, 2 * i + s, s, tmp(0, s))
            turns(dve, NODE_ITERS, cut_x2)
            dve.wait_ge(S("flip_taken_x2"), 2 * NODE_ITERS)
            batch_dve("_at", dve, x_fm, col(AT_G), col(AT_BE), col(SCALE), col(SHIFT))
            end_stage(dve, nc.vector)

            nc.vector.memset(stage_nm[:, :, P], 1.0)

            def scores(i):
                for s in range(2):
                    c = 2 * i + s
                    wait(dve, S("s_ready"), c - 1)
                    nc.vector.tensor_scalar(tmp_acc(0, s), x_fm[:, cslice(c)], col(SCALE), col(SHIFT), ALU.mult, ALU.add)\
                        .then_inc(S("xn_ready"), 1)
                    dve.wait_ge(S("xn_ready"), c + 1)
                    dve.wait_ge(S("sc_ready"), c + 1)
                    nc.vector.tensor_tensor(tmp_acc(1, s), ps[:, s, 0:CN], tmp_acc(0, s), ALU.mult)
                    nc.vector.tensor_tensor(tmp_acc(2, s), ps[:, s, CN:2 * CN], tmp_acc(0, s), ALU.mult)\
                        .then_inc(S("sc_prod"), 1)
            turns(dve, NODE_ITERS, scores)
            end_stage(dve, nc.vector)
            dve.sem_inc(S("score_cols"), 1)
            end_stage(dve, nc.vector)
            pass_dve(5, dve)
            end_stage(dve, nc.vector)

            one = chain(dve)
            one(nc.vector.tensor_scalar(small[:, 0, :], acc_nm[:, :, P], 1e-16, None, ALU.max))
            nc.vector.reciprocal(small[:, 1, :], small[:, 0, :]).then_inc(S("inverse_done_at"), 1)
            stat2 = Steps(dve, "at_stats", 2 * CB)

            def att_residual(i):
                for s in range(2):
                    c = 2 * i + s
                    stat2.chunk(c)
                    blk = x_nm[:, bslice(c), :].rearrange("p b f -> p (b f)")
                    dve.wait_ge(S("at_relu"), (c + 1) * CB)
                    nc.vector.tensor_tensor(blk, blk, x_fm[:, s * CN:(s + 1) * CN], ALU.add).then_inc(S("at_added"), 1)
                    dve.wait_ge(S("at_added"), c + 1)
                    stats_dve("", dve, c, stat2)
            turns(dve, NODE_ITERS, att_residual)
            end_stage(dve, nc.vector)
            norm_dve("_ln2", dve)
            end_stage(dve, nc.vector)

            def edge_halves(i):
                for s in range(2):
                    c = 2 * i + s
                    cut_dve("_x3", dve, c, s, tmp(0, s))
                    dve.wait_ge(S("flip_taken_x3"), c + 1)
                    nc.vector.tensor_copy(x_fm[:, cslice(c)], tmp(1, s))
                    dve.wait_ge(S("p_staged"), c + 1)
                    nc.vector.tensor_tensor(q_nm[:, cslice(c)].rearrange("p (b f) -> p b f", b=CB),
                                            ps[:, s, :].rearrange("p (b h f) -> p b h f", b=CB, h=2)[:, :, 1, :],
                                            be1_rows.unsqueeze(1).to_broadcast([P, CB, P]), ALU.add)\
                        .then_inc(S("q_taken"), 1)
            turns(dve, NODE_ITERS, edge_halves)
            end_stage(dve, nc.vector)
            pass_dve(6, dve)
            end_stage(dve, nc.vector)

            stat3 = Steps(dve, "mesh_stats", 2 * CB)

            def mesh_residual(i):
                for s in range(2):
                    c = 2 * i + s
                    stat3.chunk(c)
                    blk = x_nm[:, bslice(c), :].rearrange("p b f -> p (b f)")
                    dve.wait_ge(S("mesh_ready"), c + 1)
                    nc.vector.scalar_tensor_tensor(blk, blk, 2.0, ps[:, 4 + s, 0:CN], ALU.mult, ALU.add)\
                        .then_inc(S("mesh_added"), 1)
                    dve.wait_ge(S("mesh_added"), c + 1)
                    stats_dve("", dve, c, stat3)
            turns(dve, NODE_ITERS, mesh_residual)
            end_stage(dve, nc.vector)
            norm_dve("_ln3", dve)
            end_stage(dve, nc.vector)


_INS = ["x", "src", "dst", "L0_gnn_lin_w", "L0_gnn_lin_b", "L0_gnn_weight", "L0_gnn_w_ih", "L0_gnn_w_hh",
        "L0_gnn_b_ih", "L0_gnn_b_hh", "L1_gnn_hyperedge_weight", "L1_gnn_W", "L1_gnn_b", "L1_gnn_gamma",
        "L1_gnn_beta", "L2_gnn_kernel", "L2_gnn_kernel1", "L2_gnn_kernel2", "L2_gnn_gamma", "L2_gnn_beta",
        "L3_gnn_We1", "L3_gnn_be1", "L3_gnn_We2", "L3_gnn_be2", "L3_gnn_Wn1", "L3_gnn_bn1", "L3_gnn_Wn2",
        "L3_gnn_bn2"]


def kernel(**inputs):
    import numpy as np
    import concourse.bacc as bacc
    from concourse.bass_utils import run_bass_kernel_spmd

    nc = bacc.Bacc("TRN2", target_bir_lowering=False, num_devices=1)
    arrays = {name: np.ascontiguousarray(inputs[name]) for name in _INS}
    d = {name: nc.dram_tensor(name, a.shape, mybir.dt.from_np(a.dtype), kind="ExternalInput").ap()
         for name, a in arrays.items()}
    d["out"] = nc.dram_tensor("out", (N, P), F32, kind="ExternalOutput").ap()
    gnn(nc, d)
    return run_bass_kernel_spmd(nc, [arrays], core_ids=[0]).results[0]["out"]
```

```python
from contextlib import ExitStack

import concourse.bass as bass
from concourse import mybir

F32 = mybir.dt.float32
F16 = mybir.dt.float16
I32 = mybir.dt.int32
I16 = mybir.dt.int16
U8 = mybir.dt.uint8
ALU = mybir.AluOpType
ACT = mybir.ActivationFunctionType
AX_X = mybir.AxisListType.X

P = 128
N = 6250
E = 106250
NB = (N + P - 1) // P
NB1 = NB + 1
NBP = 52
NP = NBP * P
CB = 2
CN = CB * P
NODE_ITERS = NP // (2 * CN)
EC = 832
E_FULL = E // EC
E_REST = E - E_FULL * EC
CH = 8
T = -(-((E + NB * (P - 1)) // P) // (2 * CH)) * 2 * CH
PASS_ITERS = T // (2 * CH)
TP = T + 2 * CH
assert TP == -(-T // P) * P
W = 132
SC = 16
SCATTER_ITERS = EC // (2 * SC)
EDGE_TILES = P * EC // P
PAD_NODE = NB * P
NODE_BITS = 13
TG = -(-T // P)
LOW_BITS = 11
BUILD = 4
MASKB = 128
ST = 250
NST = N // ST
EPS = 1e-5
GRU_LAYERS = 3


class Count:
    def __init__(self, sem, base):
        self.sem, self.base = sem, base


def wait(eng, sem, value):
    if isinstance(value, int) and value <= 0:
        return
    if isinstance(sem, Count):
        eng.wait_ge(sem.sem, value + sem.base)
    else:
        eng.wait_ge(sem, value)


def turns(eng, count, body, peeled=1):
    for i in range(peeled):
        body(i)
    with eng.Fori(peeled, count) as i:
        body(i)


def gnn(nc, d):
    ctx = ExitStack()
    with ctx:
        def sb(name, shape, dt=F32):
            return ctx.enter_context(nc.sbuf_tensor(name, shape, dt))

        def sem(name):
            return ctx.enter_context(nc.semaphore(name))

        def dram(name, shape, dt=F32):
            return nc.dram_tensor(name, shape, dt, kind="Internal").ap()

        x_nm = sb("x_nm", [P, NBP, P])
        x_fm = sb("x_fm", [P, NP])
        acc = sb("acc", [P, NBP * W])
        stage = sb("stage", [P, NBP * W])
        big = sb("big", [P, 2 * NP])
        gather_idx = [sb(f"gather_idx{k}", [P, TP], I32) for k in range(2)]
        local = [sb(f"local{k}", [P, TP]) for k in range(2)]
        block_of = [sb(f"block_of{k}", [P, T], I16) for k in range(2)]
        rows = sb("rows", [P, 2 * CH, W])
        onehot = sb("onehot", [P, 2 * CH, P])
        idx_ring = sb("idx_ring", [P, 2 * SC], I32)
        val_ring = sb("val_ring", [P, 2 * SC], I32)
        w_late = sb("w_late", [P, 10 * P])
        w_hh = sb("w_hh", [P, 3 * P])
        w_lin = sb("w_lin", [P, P])
        w_hyper = sb("w_hyper", [P, P])
        ident = sb("ident", [P, P])
        ones = sb("ones", [P, P])
        iota = sb("iota", [P, P])
        lower = sb("lower", [P, P])
        sel_blocks = sb("sel_blocks", [P, P])
        step_down = sb("step_down", [P, P])
        tile_iota = sb("tile_iota", [P, TP], F16)
        block_no = sb("block_no", [P, PASS_ITERS])
        cols = sb("cols", [P, 24])
        small = sb("small", [P, 6, NBP])
        mv = sb("mv", [P, NBP, 2])
        mv_chunk = sb("mv_chunk", [P, CB, 2])
        bst = sb("bst", [P, NST, 6])
        bmv = sb("bmv", [P, 2])
        st6 = sb("st6", [P, 2, CB, 6])
        row0 = sb("row0", [1, 2 * P])
        ps = ctx.enter_context(nc.psum_tensor("ps", [P, 8, 512], F32))

        acc_nm = acc[:, :].rearrange("p (b w) -> p b w", w=W)
        stage_nm = stage[:, :].rearrange("p (b w) -> p b w", w=W)
        stage_rows = stage[:, 0:NP].rearrange("p (b f) -> p b f", f=P)
        w_comb = w_late[:, 0:9 * P].rearrange("p (l m) -> p l m", l=3)
        w_att = w_late[:, 0:3 * P]
        w_e1 = w_late[:, 3 * P:5 * P]
        w_e2 = w_late[:, 5 * P:6 * P]
        w_n1 = w_late[:, 6 * P:8 * P]
        w_n2 = w_late[:, 8 * P:9 * P]
        be1_rows = w_late[:, 9 * P:10 * P]

        dst_e, src_e, int_a, int_b, next_e, packed, slot_addr = [
            acc[:, k * EC:(k + 1) * EC].bitcast(I32) for k in range(7)]
        blk0 = acc[:, 7 * EC:8 * EC]
        blk1, pos1, hi1, lo1, row1, tile1 = [big[:, k * T:(k + 1) * T] for k in range(6)]
        next_blk = big[:, 6 * T:6 * T + EC]
        assert 6 * T + EC <= NP and 8 * EC <= NBP * W
        h = NP + 14 * CN
        scan, prod, ones_row = [big[:, h + k * EC:h + (k + 1) * EC] for k in range(3)]
        mask = big[:, h + 3 * EC:h + 3 * EC + EC // 4].bitcast(U8)
        h += 3 * EC + EC // 4
        count_b, base = big[:, h:h + MASKB], big[:, h + MASKB:h + 2 * MASKB]
        tiny = big[:, h + 2 * MASKB:h + 2 * MASKB + 16]
        tiny_i = big[:, h + 2 * MASKB + 16:h + 2 * MASKB + 24].bitcast(I32)
        assert h + 2 * MASKB + 24 <= 2 * NP and 6 * T <= NP
        diag = scan[:, 0:MASKB]
        tile_ge = big[:, NP + 6 * CN:NP + 6 * CN + TP]
        pos0 = next_blk
        pair_rows, pair_a, pair_b = [acc[:, 4 * EC + k * TP:4 * EC + (k + 1) * TP].bitcast(I32)
                                     .rearrange("p (g e) -> p g e", g=TG) for k in range(3)]
        pair_f = big[:, NP + 6 * CN + TP:NP + 6 * CN + 2 * TP].rearrange("p (g e) -> p g e", g=TG)
        assert 4 * EC + 3 * TP <= NBP * W and 6 * CN + 2 * TP <= 14 * CN
        pair_idx = sb("pair_idx", [P, TG], I32)
        pair_blk = sb("pair_blk", [P, TG])
        flag = sb("flag", [P, 1], I32)
        h = NP + 14 * CN
        hot_tile = [big[:, a:a + BUILD * T // 2].bitcast(F16).rearrange("p (m t) -> p m t", m=BUILD)
                    for a in (0, h)]
        h += BUILD * T // 2
        hot_row = [big[:, h + n * BUILD * P:h + (n + 1) * BUILD * P].bitcast(F16)
                   .rearrange("p (m a r) -> p m a r", m=BUILD, a=2) for n in range(2)]
        assert h + 2 * BUILD * P <= 2 * NP
        raw_w = stage[:, 0:10 * P].rearrange("p (m f) -> p m f", f=P)
        tr_w = stage[:, 10 * P:16 * P].rearrange("p (m f) -> p m f", f=P)

        edges = dram("edges", (P * EC, 1), I32)
        widths = [P, P, P, P + 1, P + 1, P + 3, P]
        table = [dram(f"table{p}", (NP, w)) for p, w in enumerate(widths)]
        degree_row = dram("degree_row", (NP, 1))

        stage_end = sem("stage_end")
        boundary = {}

        def end_stage(eng, nc_eng):
            boundary[eng] = boundary.get(eng, 0) + 1
            nc_eng.drain().then_inc(stage_end, 1)
            eng.wait_ge(stage_end, 5 * boundary[eng])

        row_landed = [sem(f"row_landed{s}") for s in range(2 * CH)]
        rows_opened = sem("rows_opened")

        made = {}

        def S(name):
            if name not in made:
                made[name] = sem(name)
            return made[name]

        NC = 2 * NODE_ITERS
        moves = {"idx_ready": TP // CH, "summed": T, "added": T, "hot_ready": T // CH + 1, "acc_zero": 1,
                 "rz_ready": NC, "nh_ready": NC, "r_ready": NC, "z_ready": NC, "n_ready": NC, "n_in": NC,
                 "h_ready": NC, "h_kept": NC, "flip_done_gru": NC, "flip_taken_gru": NC,
                 "stored_gru": 16 * NODE_ITERS}

        def Q(name, p):
            before = p
            if name == "hot_ready":
                before = sum(m != "att" for m in MODES[:p])
            return Count(S(name), moves.get(name, 0) * before)

        LISTS = [0, 0, 0, 0, 1, 1, 0]
        MODES = ["fm", "fm", "fm", "nm", "nm", "att", "edge"]

        def cslice(c):
            return bass.ds(c * CN, CN)

        def bslice(c):
            return bass.ds(c * CB, CB)

        ring_ohT = stage[:, 0:CH * P].rearrange("p (t e) -> p t e", e=P)
        ring_e = stage[:, CH * P:3 * CH * P].rearrange("p (t e) -> p t e", e=P)
        u1_rows = big[:, 0:NP]
        u2_rows = big[:, NP:2 * NP]
        q_nm = big[:, 0:NP]

        block_regs = {}

        def tile_blocks(eng, k, c):
            if eng not in block_regs:
                block_regs[eng] = [eng.alloc_register(f"block{u}") for u in range(CH)]
            eng.load(block_regs[eng], block_of[k][0:1, bass.ds(CH * c, CH)])
            return [eng.snap(r, min_val=0, max_val=NB - 1) for r in block_regs[eng]]

        def groups(w):
            per = 512 // w
            return [(g, range(g * per, min((g + 1) * per, CH))) for g in range(-(-CH // per))]

        def psum_sum(h, u, w):
            per = 512 // w
            return ps[:, h * -(-CH // per) + u // per, (u % per) * w:(u % per + 1) * w]

        def pass_pool(p, pool):
            idx_ready, summed = Q("idx_ready", p), Q("summed", p)

            def body(i):
                for h in range(2):
                    wait(pool, idx_ready, 2 * i + h + 1)
                    pool.sem_inc(rows_opened, 1)
                    if not isinstance(i, int):
                        wait(pool, summed, 2 * CH * i + CH * h - CH)
                        pool.sem_inc(rows_opened, 1)
                    for u in range(CH):
                        s = h * CH + u
                        nc.gpsimd.indirect_dma_start(
                            rows[:, s, 0:widths[p]], None, table[p][0:N, :],
                            bass.IndirectOffsetOnAxis(idx_ring[:, s:s + 1], 0),
                        ).then_inc(row_landed[s], 16)
            turns(pool, PASS_ITERS, body)

        def pass_act(p, act):
            k, mode = LISTS[p], MODES[p]
            idx_ready, summed = Q("idx_ready", p), Q("summed", p)
            for h in range(2):
                nc.scalar.copy(idx_ring[:, h * CH:(h + 1) * CH],
                               gather_idx[k][:, h * CH:(h + 1) * CH]).then_inc(idx_ready.sem, 1)

            def body(i):
                for h in range(2):
                    c = 2 * i + h
                    if mode == "att":
                        blk = tile_blocks(act, k, c)
                        for u in range(CH):
                            s = h * CH + u
                            wait(act, row_landed[s], 16 * (PASS_ITERS * p + i + 1))
                            nc.scalar.activation(onehot[:, s, :], u1_rows[:, bass.ds(blk[u] * P, P)],
                                                 ACT.Copy, scale=rows[:, s, 129:130]
                                                 ).then_inc(Q("scaled", p).sem, 1)
                    if mode == "edge":
                        for g in range(2):
                            wait(act, Q("flipped", p), 2 * c + g + 1)
                            nc.scalar.copy(ring_ohT[:, 4 * g:4 * g + 4, :].rearrange("p t e -> p (t e)"), ps[:, 4 + g, :]
                                           ).then_inc(Q("flip_copied", p).sem, 1)
                        for g in range(2):
                            wait(act, Q("edge_pre", p), 2 * c + g + 1)
                            nc.scalar.activation(ring_e[:, h * CH + 4 * g:h * CH + 4 * g + 4, :]
                                                 .rearrange("p t e -> p (t e)"), ps[:, 6 + g, :], ACT.Relu
                                                 ).then_inc(Q("edge_act", p).sem, 1)
                    wait(act, summed, CH * c + CH)
                    nc.scalar.copy(idx_ring[:, h * CH:(h + 1) * CH],
                                   gather_idx[k][:, bass.ds(CH * (c + 2), CH)]).then_inc(idx_ready.sem, 1)
            turns(act, PASS_ITERS, body)

        def bases_pe(pe):
            pe.wait_ge(S("counted"), 2)
            nc.tensor.matmul(ps[:, 4, 0:1], count_b, ones[:, 0:1], start=True, stop=True).then_inc(S("totals"), 1)
            pe.wait_ge(S("tiles_b"), 1)
            nc.tensor.matmul(ps[:, 5, 0:1], lower[:, :], tiny[:, 2:3], start=True, stop=True).then_inc(S("bases"), 1)
            pe.wait_ge(S("diag_ready"), 1)
            nc.tensor.matmul(ps[:, 6, 0:MASKB], lower[:, :], count_b, start=True, stop=False)
            nc.tensor.matmul(ps[:, 6, 0:MASKB], ones[:, :], diag, start=False, stop=True)
            for j in range(2):
                last = nc.tensor.matmul(ps[:, 7 - 3 * j, 0:T // 2], sel_blocks[:, :],
                                        tile_ge[:, j * (T // 2):(j + 1) * (T // 2)], start=True, stop=True)
            last.then_inc(S("places"), 1)

        def bases_dve(dve):
            step = chain(dve)
            dve.sem_inc(S("counted"), 1)
            dve.wait_ge(S("totals"), 2)
            step(nc.vector.tensor_scalar(tiny_i[:, 0:1], ps[:, 4, 0:1], float(P - 1), None, ALU.add))
            step(nc.vector.tensor_scalar(tiny_i[:, 1:2], tiny_i[:, 0:1], 7, None, ALU.logical_shift_right))
            nc.vector.tensor_copy(tiny[:, 2:3], tiny_i[:, 1:2]).then_inc(S("tiles_b"), 1)
            dve.wait_ge(S("bases"), 2)
            step(nc.vector.tensor_copy(tiny[:, 3:4], ps[:, 5, 0:1]))
            step(nc.vector.tensor_scalar(diag, ident[:, :], tiny[:, 3:4], float(P), ALU.mult, ALU.mult))
            nc.vector.tensor_scalar(tile_ge, tile_iota[:, :], tiny[:, 3:4], None, ALU.is_ge).then_inc(S("diag_ready"), 1)
            dve.wait_ge(S("places"), 1)
            for j in range(2):
                nc.vector.tensor_copy(block_of[1][:, j * (T // 2):(j + 1) * (T // 2)], ps[:, 7 - 3 * j, 0:T // 2])
            step(nc.vector.tensor_copy(base, ps[:, 6, 0:MASKB]))

        def places_dve(dve):
            step = chain(dve)
            a, b = scan[:, 0:EC].bitcast(I32), prod[:, 0:EC].bitcast(I32)
            step(nc.vector.tensor_scalar(a, pos1[:, 0:EC], -1.0, None, ALU.add))
            step(nc.vector.tensor_scalar(b, a, P - 1, None, ALU.bitwise_and))
            nc.vector.tensor_copy(row1[:, 0:EC], b)
            step(nc.vector.memset(row1[:, EC:T], -1.0))
            step(nc.vector.tensor_scalar(b, a, 7, None, ALU.arith_shift_right))
            nc.vector.tensor_copy(tile1[:, 0:EC], b)
            step(nc.vector.memset(tile1[:, EC:T], -1.0))

        def list1_dve(p, dve, i, h):
            if p == 0 and h == 0:
                blk = block_no[:, bass.ds(i, 1)]
                ranks = Steps(dve, "rank_steps", 4)
                ranks.chunk(i)
                ranks(nc.vector.tensor_scalar(mask, blk1[:, 0:EC], blk, None, ALU.is_equal, ALU.add,
                                              accum_out=count_b[:, bass.ds(i, 1)]))
                ranks(nc.vector.tensor_tensor_scan(scan, ones_row, mask, 0.0, ALU.mult, ALU.add))
                ranks(nc.vector.tensor_tensor(prod, scan, mask, ALU.mult))
                ranks(nc.vector.tensor_tensor(pos1[:, 0:EC], pos1[:, 0:EC], prod, ALU.add))
            if p == 1 and h == 0:
                places = Steps(dve, "place_steps", 2)
                places.chunk(i)
                places(nc.vector.tensor_scalar(prod, blk1[:, 0:EC], block_no[:, bass.ds(i, 1)],
                                               base[:, bass.ds(i, 1)], ALU.is_equal, ALU.mult))
                places(nc.vector.tensor_tensor(pos1[:, 0:EC], pos1[:, 0:EC], prod, ALU.add))
            if p in (2, 3):
                turn = 2 * (PASS_ITERS * (p - 2) + i) + h
                wait(dve, S("built"), turn - 1)
                for m in range(BUILD):
                    one_col = bass.ds(BUILD * turn + m, 1)
                    nc.vector.tensor_scalar(hot_tile[h][:, m, :], tile_iota[:, 0:T], tile1[:, one_col], None,
                                            ALU.is_equal)
                    for a, value in enumerate((hi1, lo1)):
                        last = nc.vector.tensor_scalar(hot_row[h][:, m, a, :], tile_iota[:, 0:P], row1[:, one_col],
                                                       value[:, one_col], ALU.is_equal, ALU.mult)
                last.then_inc(S("hot_cols"), 1)

        def list1_pe(p, pe, i, h):
            if p not in (2, 3):
                return
            turn = 2 * (PASS_ITERS * (p - 2) + i) + h
            pe.wait_ge(S("hot_cols"), turn + 1)
            for m in range(BUILD):
                for a in range(2):
                    first = p == 2 and h == 0 and m == 0 and a == 0 and isinstance(i, int)
                    for j in range(2):
                        last = nc.tensor.matmul(ps[:, 6 + j, 0:T // 2], hot_row[h][:, m, a, :],
                                                hot_tile[h][:, m, j * (T // 2):(j + 1) * (T // 2)],
                                                start=first, stop=True, skip_group_check=True)
            last.then_inc(S("built"), 1)

        def unpack1_dve(dve):
            step = chain(dve)
            v, a, b = [stage[:, NP - (k + 1) * T:NP - k * T] for k in range(3)]
            v_i, a_i, b_i = [t.bitcast(I32) for t in (v, a, b)]
            for j in range(2):
                last = nc.vector.tensor_scalar(v_i[:, j * (T // 2):(j + 1) * (T // 2)], ps[:, 6 + j, 0:T // 2],
                                               float(1 << LOW_BITS), None, ALU.mult)
            step(last)
            step(nc.vector.tensor_scalar(a_i, v_i, -1.0, 0.0, ALU.add, ALU.max))
            nc.vector.tensor_scalar(b, v_i, 0.0, float(P), ALU.is_equal, ALU.mult)
            nc.vector.memset(gather_idx[1][:, T:TP], 0)
            nc.vector.memset(local[1][:, T:TP], float(P))
            step(nc.vector.tensor_scalar(gather_idx[1][:, 0:T], a_i, 7, None, ALU.logical_shift_right))
            step(nc.vector.tensor_scalar(v_i, a_i, P - 1, None, ALU.bitwise_and))
            step(nc.vector.tensor_tensor(local[1][:, 0:T], v_i, b, ALU.add))

        def pass_pe(p, pe):
            k, mode = LISTS[p], MODES[p]
            if p == 1:
                bases_pe(pe)
            w = P if mode in ("fm", "edge") else P + 1
            hot_ready, summed, added = Q("weighted" if MODES[p] == "att" else "hot_ready", p), Q("summed", p), Q("added", p)

            def body(i):
                for h in range(2):
                    c = 2 * i + h
                    if mode == "edge":
                        blk = tile_blocks(pe, k, c)
                        wait(pe, hot_ready, c + 1)
                        for g in range(2):
                            wait(pe, Q("flip_copied", p), 2 * (c - 1) + g + 1)
                            for u in range(4):
                                last = nc.tensor.transpose(ps[:, 4 + g, u * P:(u + 1) * P],
                                                           onehot[:, h * CH + 4 * g + u, :], ident[:, :])
                            last.then_inc(Q("flipped", p).sem, 1)
                        for g in range(2):
                            wait(pe, Q("edge_act", p), 2 * (c - 1) + g + 1)
                            wait(pe, Q("flip_copied", p), 2 * c + g + 1)
                            for u in range(4):
                                s = h * CH + 4 * g + u
                                out = ps[:, 6 + g, u * P:(u + 1) * P]
                                wait(pe, row_landed[s], 16 * (PASS_ITERS * p + i + 1))
                                nc.tensor.matmul(out, ident[:, :], rows[:, s, 0:P], start=True, stop=False,
                                                 skip_group_check=True)
                                last = nc.tensor.matmul(out, ring_ohT[:, 4 * g + u, :],
                                                        q_nm[:, bass.ds(blk[4 * g + u] * P, P)],
                                                        start=False, stop=True, skip_group_check=True)
                            last.then_inc(Q("edge_pre", p).sem, 1)
                    elif mode != "att":
                        wait(pe, hot_ready, c + 1)
                    for g, tiles in groups(w):
                        wait(pe, added, CH * (c - 2) + tiles[-1] + 1)
                        if mode == "edge":
                            wait(pe, Q("edge_act", p), 2 * c + g + 1)
                        for u in tiles:
                            s = h * CH + u
                            if mode == "edge":
                                lhs, rhs = ring_e[:, s, :], onehot[:, s, :]
                            else:
                                wait(pe, row_landed[s], 16 * (PASS_ITERS * p + i + 1))
                                if mode == "fm":
                                    lhs, rhs = rows[:, s, 0:P], onehot[:, s, :]
                                elif mode == "nm":
                                    lhs, rhs = onehot[:, s, :], rows[:, s, 0:w]
                                else:
                                    wait(pe, hot_ready, CH * c + u + 1)
                                    lhs, rhs = ring_e[:, s, :], rows[:, s, 0:w]
                            nc.tensor.matmul(psum_sum(h, u, w), lhs, rhs, start=True, stop=True,
                                             skip_group_check=True).then_inc(summed.sem, 1)
                    list1_pe(p, pe, i, h)
            turns(pe, PASS_ITERS, body)

        def pass_dve(p, dve):
            k, mode = LISTS[p], MODES[p]
            w = P if mode in ("fm", "edge") else P + 1
            stride = P if mode in ("fm", "edge") else W
            hot_ready, summed, added = Q("weighted" if MODES[p] == "att" else "hot_ready", p), Q("summed", p), Q("added", p)
            nc.vector.memset(acc[:, :], 0.0).then_inc(Q("acc_zero", p).sem, 1)
            wait(dve, Q("acc_zero", p), 1)

            def hots(c, h):
                nc.vector.tensor_tensor(
                    onehot[:, h * CH:(h + 1) * CH, :],
                    iota[:, :].unsqueeze(1).to_broadcast([P, CH, P]),
                    local[k][:, bass.ds(CH * c, CH)].unsqueeze(2).to_broadcast([P, CH, P]),
                    ALU.is_equal).then_inc(hot_ready.sem, 1)

            if mode != "att":
                hots(0, 0)
            if p == 1:
                bases_dve(dve)
            if p == 2:
                places_dve(dve)

            def body(i):
                for h in range(2):
                    c = 2 * i + h
                    blk = tile_blocks(dve, k, c)
                    if mode != "att":
                        hots(c + 1, 1 - h)
                        list1_dve(p, dve, i, h)
                    else:
                        for u in range(CH):
                            s = h * CH + u
                            wait(dve, Q("scaled", p), CH * c + u + 1)
                            nc.vector.scalar_tensor_tensor(
                                ring_e[:, s, :], u2_rows[:, bass.ds(blk[u] * P, P)], rows[:, s, 130:131],
                                onehot[:, s, :], ALU.mult, ALU.max).then_inc(Q("weighed", p).sem, 1)
                        for u in range(CH):
                            s = h * CH + u
                            wait(dve, Q("weighed", p), CH * c + u + 1)
                            nc.vector.scalar_tensor_tensor(
                                ring_e[:, s, :], iota[:, :], local[k][:, bass.ds(CH * c + u, 1)],
                                ring_e[:, s, :], ALU.is_equal, ALU.mult).then_inc(hot_ready.sem, 1)
                    for g, tiles in groups(w):
                        wait(dve, summed, CH * c + tiles[-1] + 1)
                        for u in tiles:
                            dst = acc[:, bass.ds(blk[u] * stride, w)]
                            wait(dve, added, CH * c + u)
                            nc.vector.tensor_tensor(dst, psum_sum(h, u, w), dst, ALU.add).then_inc(added.sem, 1)
            turns(dve, PASS_ITERS, body)

        def tslot(s):
            return ps[:, 4 + s, 0:CN]

        def flip_pe(tag, pe, src, c, s, ready):
            taken, done = (Q("flip_taken_gru", tag), Q("flip_done_gru", tag)) if isinstance(tag, int) else \
                (Count(S("flip_taken" + tag), 0), Count(S("flip_done" + tag), 0))
            wait(pe, ready, c + 1)
            wait(pe, taken, c - 1)
            for b in range(CB):
                last = nc.tensor.transpose(ps[:, 4 + s, b * P:(b + 1) * P], src[:, b * P:(b + 1) * P], ident[:, :])
            last.then_inc(done.sem, 1)

        def cut_dve(tag, dve, c, s, slot):
            wait(dve, S("flip_done" + tag), c - 1)
            nc.vector.tensor_copy(slot, x_nm[:, bslice(c), :].rearrange("p b f -> p (b f)")).then_inc(S("cut" + tag), 1)

        class Steps:
            def __init__(self, eng, name, per_chunk, base=0):
                self.eng, self.sem, self.per, self.c, self.n = eng, S(name), per_chunk, 0, 0
                self.base = base

            def chunk(self, c):
                self.c, self.n = c, 0

            def __call__(self, ins):
                self.n += 1
                ins.then_inc(self.sem, 1)
                self.eng.wait_ge(self.sem, self.c * self.per + self.n + self.base)

        chained = []

        def chain(dve):
            if not chained:
                chained.append(Steps(dve, "dve_chain", 0))
            return chained[0]

        def hold(eng):
            eng.sem_inc(S("held"), 1)

        def stats_dve(tag, dve, c, steps):
            hold(dve)
            for b in range(CB):
                nc.vector.bn_stats(st6[:, 0, b, :], x_nm[:, bass.ds(c * CB + b, 1), :]
                                   .rearrange("p b f -> p (b f)")).then_inc(steps.sem, 1)
                steps.n += 1
            dve.wait_ge(steps.sem, steps.c * steps.per + steps.n + steps.base)
            hold(dve)
            for b in range(CB):
                nc.vector.bn_aggr(mv_chunk[:, b, :], st6[:, 0, b, :]).then_inc(steps.sem, 1)
                steps.n += 1
            dve.wait_ge(steps.sem, steps.c * steps.per + steps.n + steps.base)
            nc.vector.tensor_copy(mv[:, bslice(c), :], mv_chunk[:, :, :])

        def norm_dve(n, dve):
            one = chain(dve)
            one(nc.vector.tensor_scalar(small[:, 0, :], mv[:, :, 1], EPS, None, ALU.add))
            nc.vector.tensor_copy(small[:, 2, :], mv[:, :, 0]).then_inc(S("norm_var"), 1)
            dve.wait_ge(S("norm_var"), n + 1)
            dve.wait_ge(S("norm_std"), n + 1)
            one(nc.vector.reciprocal(small[:, 1, :], small[:, 1, :]))

            def body(i):
                for s in range(2 * CB):
                    b = i * 2 * CB + s
                    blk = x_nm[:, bass.ds(b, 1), :].rearrange("p b f -> p (b f)")
                    nc.vector.tensor_scalar(blk, blk, small[:, 2, bass.ds(b, 1)], small[:, 1, bass.ds(b, 1)],
                                            ALU.subtract, ALU.mult).then_inc(S("normed"), 1)
            turns(dve, NODE_ITERS, body)

        def norm_act(n, act):
            act.wait_ge(S("norm_var"), n + 1)
            nc.scalar.activation(small[:, 1, :], small[:, 0, :], ACT.Sqrt).then_inc(S("norm_std"), 1)

        def store_norm_sp(sp, dst):
            def body(i):
                sp.wait_ge(S("normed"), (i + 1) * 2 * CB)
                sp.dma_start(dst[bass.ds(i * 2 * CN, 2 * CN), 0:P].rearrange("(b p) f -> p b f", p=P),
                             x_nm[:, bass.ds(i * 2 * CB, 2 * CB), :]).then_inc(S("norm_stored"), 16)
            turns(sp, NODE_ITERS, body)
            sp.wait_ge(S("norm_stored"), 16 * NODE_ITERS)

        def safe_inverse_dve(tag, dve):
            one = chain(dve)
            one(nc.vector.tensor_copy(small[:, 0, :], acc_nm[:, :, P]))
            one(nc.vector.tensor_scalar(small[:, 2, :], small[:, 0, :], 0.0, None, ALU.is_gt))
            one(nc.vector.tensor_tensor(small[:, 1, :], small[:, 0, :], small[:, 2, :], ALU.mult))
            one(nc.vector.tensor_scalar(small[:, 3, :], small[:, 2, :], -1.0, 1.0, ALU.mult, ALU.add))
            one(nc.vector.tensor_tensor(small[:, 1, :], small[:, 1, :], small[:, 3, :], ALU.add))
            one(nc.vector.reciprocal(small[:, 1, :], small[:, 1, :]))
            one(nc.vector.tensor_tensor(small[:, 1, :], small[:, 1, :], small[:, 2, :], ALU.mult))

        def batch_dve(n_done, dve, src, gamma, beta, scale, shift):
            one = chain(dve)

            for n in range(NST):
                last = nc.vector.bn_stats(bst[:, n, :], src[:, n * ST:(n + 1) * ST])
            one(last)
            one(nc.vector.bn_aggr(bmv[:, :], bst[:, :, :].rearrange("p n s -> p (n s)")))
            nc.vector.tensor_scalar(bmv[:, 1:2], bmv[:, 1:2], EPS, None, ALU.add).then_inc(S("batch_var"), 1)
            dve.wait_ge(S("batch_std"), n_done + 1)
            one(nc.vector.reciprocal(scale, scale))
            one(nc.vector.tensor_tensor(scale, scale, gamma, ALU.mult))
            one(nc.vector.tensor_tensor(shift, bmv[:, 0:1], scale, ALU.mult))
            one(nc.vector.tensor_tensor(shift, beta, shift, ALU.subtract))

        def batch_act(n_done, act, scale):
            act.wait_ge(S("batch_var"), n_done + 1)
            nc.scalar.activation(scale, bmv[:, 1:2], ACT.Sqrt).then_inc(S("batch_std"), 1)

        real_block = sb("real_block", [P, 1])

        LIN_B, B_R, B_Z, B_IN, B_HN, HY_B, HY_G, HY_BE, AT_G, AT_BE, N1_B, SCALE, SHIFT = range(13)

        def col(j):
            return cols[:, j:j + 1]

        def vec(ap):
            return ap.rearrange("(p a) -> p a", a=1)

        def tmp(j, s):
            return big[:, NP + (2 * j + s) * CN:NP + (2 * j + s + 1) * CN]

        def tmp_acc(j, s):
            return acc[:, (2 * j + s) * CN:(2 * j + s + 1) * CN]

        block = ctx.enter_context(nc.Block())

        @block.sync
        def _(sp):
            sp.wait_ge(S("edges_padded"), 3)
            for view, name, off in ((dst_e, "dst", 0), (src_e, "src", 0), (next_e, "dst", 1)):
                full = E_FULL * EC + off
                sp.dma_start(view[0:E_FULL, :], d[name][off:full].rearrange("(p c) -> p c", c=EC))\
                    .then_inc(S("edges_in"), 16)
                sp.dma_start(view[E_FULL:E_FULL + 1, 0:E - full], d[name][full:E].rearrange("(p c) -> p c", p=1))\
                    .then_inc(S("edges_in"), 16)
            sp.dma_start(raw_w[:, 0, :], d["L0_gnn_lin_w"]).then_inc(S("weights_in"), 16)
            sp.dma_start(raw_w[:, 1:4, :], d["L0_gnn_w_ih"].rearrange("(m p) f -> p m f", p=P)).then_inc(S("weights_in"), 16)
            sp.dma_start(raw_w[:, 4:7, :], d["L0_gnn_w_hh"].rearrange("(m p) f -> p m f", p=P)).then_inc(S("weights_in"), 16)
            sp.dma_start(raw_w[:, 7:10, :], d["L0_gnn_weight"].rearrange("m p f -> p m f")).then_inc(S("weights_in"), 16)
            sp.dma_start(w_hyper[:, :], d["L1_gnn_W"]).then_inc(S("weights_in"), 16)
            for j, ap in ((LIN_B, d["L0_gnn_lin_b"]), (13, d["L0_gnn_b_ih"][0:P]), (14, d["L0_gnn_b_ih"][P:2 * P]),
                          (B_IN, d["L0_gnn_b_ih"][2 * P:3 * P]), (15, d["L0_gnn_b_hh"][0:P]),
                          (16, d["L0_gnn_b_hh"][P:2 * P]), (B_HN, d["L0_gnn_b_hh"][2 * P:3 * P]),
                          (HY_B, d["L1_gnn_b"]), (HY_G, d["L1_gnn_gamma"]), (HY_BE, d["L1_gnn_beta"]),
                          (AT_G, d["L2_gnn_gamma"]), (AT_BE, d["L2_gnn_beta"]), (N1_B, d["L3_gnn_bn1"])):
                sp.dma_start(col(j), vec(ap)).then_inc(S("vectors_in"), 16)
            sp.dma_start(row0[:, 0:P], d["L3_gnn_be2"].rearrange("(a n) -> a n", a=1)).then_inc(S("vectors_in"), 16)
            sp.dma_start(row0[:, P:2 * P], d["L3_gnn_bn2"].rearrange("(a n) -> a n", a=1)).then_inc(S("vectors_in"), 16)
            sp.wait_ge(S("x_zero"), 1)
            sp.dma_start(x_nm[:, 0:NB - 1, :], d["x"][0:(NB - 1) * P, :].rearrange("(b p) f -> p b f", p=P)).then_inc(S("x_in"), 16)
            sp.dma_start(x_nm[0:N - (NB - 1) * P, NB - 1, :], d["x"][(NB - 1) * P:N, :]).then_inc(S("x_in"), 16)
            sp.wait_ge(S("consts"), 1)
            sp.dma_start(table[3][:, P:P + 1].rearrange("(b p) f -> p (b f)", p=P), ones[:, 0:NBP],
                         allow_slow_non_contiguous=True).then_inc(S("const_columns"), 16)
            sp.dma_start(table[4][0:N, P:P + 1], d["L1_gnn_hyperedge_weight"].rearrange("(n a) -> n a", a=1),
                         allow_slow_non_contiguous=True).then_inc(S("const_columns"), 16)
            sp.wait_ge(S("packed_ready"), 1)
            sp.dma_start(edges.rearrange("(p c) a -> p (c a)", c=EC), packed).then_inc(S("edges_stored"), 16)
            def h0_out(i):
                sp.wait_ge(S("h0_staged"), 2 * i + 2)
                sp.dma_start(table[0][bass.ds(i * 2 * CN, 2 * CN), :].rearrange("(b p) f -> p b f", p=P),
                             stage_rows[:, bass.ds(i * 2 * CB, 2 * CB), :]).then_inc(S("h0_stored"), 16)
            turns(sp, NODE_ITERS, h0_out)
            sp.wait_ge(S("h0_stored"), 16 * NODE_ITERS)
            sp.wait_ge(S("const_columns"), 32)
            end_stage(sp, nc.sync)
            for p in range(GRU_LAYERS):
                end_stage(sp, nc.sync)
                if p < GRU_LAYERS - 1:
                    def rows_out(i, p=p):
                        wait(sp, Q("flip_taken_gru", p), 2 * i + 2)
                        sp.dma_start(table[p + 1][bass.ds(i * 2 * CN, 2 * CN), :].rearrange("(b p) f -> p b f", p=P),
                                     stage_rows[:, bass.ds(i * 2 * CB, 2 * CB), :]).then_inc(Q("stored_gru", p).sem, 16)
                    turns(sp, NODE_ITERS, rows_out)
                    wait(sp, Q("stored_gru", p), 16 * NODE_ITERS)
                end_stage(sp, nc.sync)
            for ap, src in ((w_att[:, 0:P], d["L2_gnn_kernel"]), (w_att[:, P:2 * P], d["L2_gnn_kernel1"]),
                            (w_att[:, 2 * P:3 * P], d["L2_gnn_kernel2"]),
                            (w_e1[:, 0:P], d["L3_gnn_We1"][0:P, :]), (w_e1[:, P:2 * P], d["L3_gnn_We1"][P:2 * P, :]),
                            (w_e2, d["L3_gnn_We2"]), (w_n1[:, 0:P], d["L3_gnn_Wn1"][0:P, :]),
                            (w_n1[:, P:2 * P], d["L3_gnn_Wn1"][P:2 * P, :]), (w_n2, d["L3_gnn_Wn2"]),
                            (be1_rows, d["L3_gnn_be1"].rearrange("(a n) -> a n", a=1).to_broadcast([P, P]))):
                sp.dma_start(ap, src).then_inc(S("late_weights"), 16)
            store_norm_sp(sp, table[3])
            sp.wait_ge(S("late_weights"), 160)
            end_stage(sp, nc.sync)
            end_stage(sp, nc.sync)
            sp.wait_ge(S("degree_ready"), 1)
            sp.dma_start(degree_row.rearrange("(b p) a -> p (b a)", p=P), small[:, 4, :],
                         allow_slow_non_contiguous=True).then_inc(S("degree_out"), 16)

            def hyper_out(i):
                sp.wait_ge(S("hyper_scaled"), (i + 1) * 2 * CB)
                sp.dma_start(table[4][bass.ds(i * 2 * CN, 2 * CN), 0:P].rearrange("(b p) f -> p b f", p=P),
                             stage_rows[:, bass.ds(i * 2 * CB, 2 * CB), :]).then_inc(S("hyper_stored"), 16)
            turns(sp, NODE_ITERS, hyper_out)
            sp.wait_ge(S("hyper_stored"), 16 * NODE_ITERS)
            sp.wait_ge(S("degree_out"), 16)
            end_stage(sp, nc.sync)
            end_stage(sp, nc.sync)
            end_stage(sp, nc.sync)
            end_stage(sp, nc.sync)
            end_stage(sp, nc.sync)
            end_stage(sp, nc.sync)
            end_stage(sp, nc.sync)
            sp.wait_ge(S("score_cols"), 1)

            def att_out(i):
                sp.dma_start(table[5][bass.ds(i * 2 * CN, 2 * CN), :].rearrange("(b p) f -> p b f", p=P),
                             stage_nm[:, bass.ds(i * 2 * CB, 2 * CB), 0:P + 3]).then_inc(S("att_stored"), 16)
            turns(sp, NODE_ITERS, att_out)
            sp.wait_ge(S("att_stored"), 16 * NODE_ITERS)
            end_stage(sp, nc.sync)
            end_stage(sp, nc.sync)
            end_stage(sp, nc.sync)
            end_stage(sp, nc.sync)

            def edge_out(i):
                sp.wait_ge(S("p_staged"), 2 * i + 2)
                sp.dma_start(table[6][bass.ds(i * 2 * CN, 2 * CN), :].rearrange("(b p) f -> p b f", p=P),
                             stage_rows[:, bass.ds(i * 2 * CB, 2 * CB), :]).then_inc(S("p_stored"), 16)
            turns(sp, NODE_ITERS, edge_out)
            sp.wait_ge(S("p_stored"), 16 * NODE_ITERS)
            end_stage(sp, nc.sync)
            end_stage(sp, nc.sync)
            sp.dma_start(stage[0:1, 0:NP], degree_row.rearrange("(a n) o -> a (n o)", a=1)).then_inc(S("degree_in"), 16)
            end_stage(sp, nc.sync)
            full = NB - 1
            for n in range(full // (2 * CB)):
                sp.wait_ge(S("normed"), 3 * NBP + (n + 1) * 2 * CB)
                sp.dma_start(d["out"][n * 2 * CN:(n + 1) * 2 * CN, :].rearrange("(b p) f -> p b f", p=P),
                             x_nm[:, n * 2 * CB:(n + 1) * 2 * CB, :]).then_inc(S("out_stored"), 16)
            sp.wait_ge(S("normed"), 3 * NBP + NB)
            sp.dma_start(d["out"][full * P:N, :], x_nm[0:N - full * P, full, :]).then_inc(S("out_stored"), 16)
            sp.wait_ge(S("out_stored"), 16 * (full // (2 * CB) + 1))
            end_stage(sp, nc.sync)

        @block.gpsimd
        def _(pool):
            step = Steps(pool, "const_steps", 0)
            step(nc.gpsimd.memset(ones[:, :], 1.0))
            step(nc.gpsimd.memset(ident[:, :], 0.0))
            step(nc.gpsimd.affine_select(out=ident[:, :], in_=ident[:, :], compare_op=ALU.not_equal, fill=1.0,
                                         base=0, pattern=[[-1, P]], channel_multiplier=1))
            step(nc.gpsimd.affine_select(out=lower[:, :], in_=ones[:, :], compare_op=ALU.is_ge, fill=0.0,
                                         base=-1, pattern=[[1, P]], channel_multiplier=-1))
            step(nc.gpsimd.affine_select(out=sel_blocks[:, :], in_=ones[:, :], compare_op=ALU.is_ge, fill=0.0,
                                         base=-1, pattern=[[0, P]], channel_multiplier=1))
            step(nc.gpsimd.affine_select(out=sel_blocks[:, :], in_=sel_blocks[:, :], compare_op=ALU.is_ge, fill=0.0,
                                         base=NB - 1, pattern=[[0, P]], channel_multiplier=-1))
            step(nc.gpsimd.affine_select(out=step_down[:, :], in_=ident[:, :], compare_op=ALU.not_equal, fill=-1.0,
                                         base=1, pattern=[[-1, P]], channel_multiplier=1))
            step(nc.gpsimd.iota(iota[:, :], pattern=[[1, P]], base=0, channel_multiplier=0,
                                allow_small_or_imprecise_dtypes=True))
            step(nc.gpsimd.iota(tile_iota[:, :], pattern=[[1, TP]], base=0, channel_multiplier=0,
                                allow_small_or_imprecise_dtypes=True))
            step(nc.gpsimd.iota(block_no[:, :], pattern=[[1, PASS_ITERS]], base=0, channel_multiplier=0,
                                allow_small_or_imprecise_dtypes=True))
            step(nc.gpsimd.memset(block_no[:, NB:PASS_ITERS], 200.0))
            step(nc.gpsimd.affine_select(out=real_block[:, :], in_=ones[:, 0:1], compare_op=ALU.is_ge, fill=0.0,
                                         base=NB - 1, pattern=[[0, 1]], channel_multiplier=-1))
            step(nc.gpsimd.iota(pair_blk[:, :], pattern=[[P, TG]], base=0, channel_multiplier=1,
                                allow_small_or_imprecise_dtypes=True))
            nc.gpsimd.memset(rows[:, :, :], 0.0).then_inc(S("consts"), 1)
            pool.wait_ge(S("edges_stored"), 16)
            pool.wait_ge(S("flag_ready"), 1)
            with pool.If(pool.value_load(flag[0:1, 0:1], min_val=0, max_val=E)):
                def scatter(i):
                    for h in range(2):
                        pool.wait_ge(S("ring_filled"), 2 * i + h + 1)
                        pool.sem_inc(rows_opened, 1)
                        for u in range(SC):
                            s = h * SC + u
                            nc.gpsimd.indirect_dma_start(
                                edges, bass.IndirectOffsetOnAxis(idx_ring[:, s:s + 1], 0),
                                val_ring[:, s:s + 1], None).then_inc(S("scattered" + str(h)), 16)
                with pool.Fori(0, SCATTER_ITERS) as i:
                    scatter(i)
                for h in range(2):
                    pool.wait_ge(S("scattered" + str(h)), 16 * SC * SCATTER_ITERS)
            pool.wait_ge(S("pairs_ready"), 1)
            for g in range(TG):
                nc.gpsimd.indirect_dma_start(pair_rows[:, g, :], None, edges.rearrange("(t e) a -> t (e a)", e=P),
                                             bass.IndirectOffsetOnAxis(pair_idx[:, g:g + 1], 0)
                                             ).then_inc(S("pairs_in"), 16)
            end_stage(pool, nc.gpsimd)
            follow = [1, 1, 1 + 1, 1, 5 + 1, 3, 2]
            for p in range(7):
                pass_pool(p, pool)
                end_stage(pool, nc.gpsimd)
                for _ in range(follow[p]):
                    end_stage(pool, nc.gpsimd)

        @block.scalar
        def _(act):
            act.wait_ge(S("w_flipped"), 1)
            nc.scalar.copy(w_lin[:, :], ps[:, 5, 0:P])
            nc.scalar.copy(tr_w[:, 0:3, :].rearrange("p m f -> p (m f)"), ps[:, 5, P:4 * P])
            nc.scalar.copy(w_hh[:, :], ps[:, 6, 0:3 * P])
            nc.scalar.copy(tr_w[:, 3, :], ps[:, 6, 3 * P:4 * P])
            nc.scalar.copy(tr_w[:, 4:6, :].rearrange("p m f -> p (m f)"), ps[:, 7, 0:2 * P]).then_inc(S("w_copied"), 1)
            act.wait_ge(S("w_combined"), 1)
            for l in range(GRU_LAYERS):
                last = nc.scalar.copy(w_comb[:, l, :], ps[:, 1 + l, 0:3 * P])
            last.then_inc(S("w_comb_copied"), 1)
            act.wait_ge(S("x_in"), 32)
            act.wait_ge(S("vectors_in"), 16 * 15)

            def h0_fm(c, s):
                act.wait_ge(S("h0_product"), c + 1)
                wait(act, S("h0_rows"), c - 1)
                nc.scalar.activation(tmp(2, s), ps[:, s, 0:CN], ACT.Identity, bias=col(LIN_B)).then_inc(S("h0_ready"), 1)
                act.wait_ge(S("h0_ready"), c + 1)
                nc.scalar.copy(x_fm[:, cslice(c)], tmp(2, s)).then_inc(S("h0_kept"), 1)

            def h0_nm(c, s):
                act.wait_ge(S("h0_rows"), c + 1)
                nc.scalar.copy(stage_rows[:, bslice(c), :].rearrange("p b f -> p (b f)"), ps[:, 6 + s, 0:CN])\
                    .then_inc(S("h0_staged"), 1)

            def h0(i):
                for s in range(2):
                    c = 2 * i + s
                    wait(act, S("flip_done_h0x"), c - 1)
                    nc.scalar.copy(tmp(0, s), x_nm[:, bslice(c), :].rearrange("p b f -> p (b f)")).then_inc(S("cut_h0x"), 1)
                    act.wait_ge(S("flip_done_h0x"), c + 1)
                    wait(act, S("h0_product"), c - 1)
                    nc.scalar.copy(tmp(1, s), tslot(s)).then_inc(S("flip_taken_h0x"), 1)
                    if not (isinstance(i, int) and c == 0):
                        h0_fm(c - 1, 1 - s)
                    if not (isinstance(i, int) and i == 0):
                        h0_nm(c - 2, s)
            turns(act, NODE_ITERS, h0, peeled=2)
            h0_fm(NC - 1, 1)
            h0_nm(NC - 2, 0)
            h0_nm(NC - 1, 1)
            act.wait_ge(S("flag_ready"), 1)
            with act.If(act.value_load(flag[0:1, 0:1], min_val=0, max_val=E)):
                act.wait_ge(S("addr_ready"), 1)

                def ring(i):
                    for h in range(2):
                        wait(act, S("scattered" + str(h)), 16 * SC * i)
                        c = 2 * i + h
                        nc.scalar.copy(idx_ring[:, h * SC:(h + 1) * SC], slot_addr[:, bass.ds(SC * c, SC)])\
                            .then_inc(S("ring_idx"), 1)
                        act.wait_ge(S("ring_idx"), c + 1)
                        act.sem_inc(S("ring_half"), 1)
                turns(act, SCATTER_ITERS, ring)
            end_stage(act, nc.scalar)

            for p in range(GRU_LAYERS):
                pass_act(p, act)
                end_stage(act, nc.scalar)

                def keep(c, s, p=p):
                    wait(act, Q("h_ready", p), c + 1)
                    nc.scalar.copy(x_fm[:, cslice(c)], tmp(6, s)).then_inc(Q("h_kept", p).sem, 1)
                    wait(act, Q("flip_done_gru", p), c + 1)
                    nc.scalar.copy(stage_rows[:, bslice(c), :].rearrange("p b f -> p (b f)"),
                                   tslot(s)).then_inc(Q("flip_taken_gru", p).sem, 1)

                def gates_all(i, p=p):
                    for s in range(2):
                        c = 2 * i + s
                        wait(act, Q("rz_ready", p), c + 1)
                        wait(act, Q("n_in", p), c - 1)
                        nc.scalar.activation(tmp(0, s), ps[:, s, 0:CN], ACT.Sigmoid, bias=col(B_R)).then_inc(Q("r_ready", p).sem, 1)
                        wait(act, Q("h_ready", p), c - 1)
                        nc.scalar.activation(tmp(1, s), ps[:, s, CN:2 * CN], ACT.Sigmoid, bias=col(B_Z)).then_inc(Q("z_ready", p).sem, 1)
                        wait(act, Q("n_in", p), c + 1)
                        nc.scalar.activation(tmp(3, s), tmp(2, s), ACT.Tanh, bias=col(B_IN)).then_inc(Q("n_ready", p).sem, 1)
                        if p < GRU_LAYERS - 1 and not (isinstance(i, int) and s == 0):
                            keep(c - 1, 1 - s)
                turns(act, NODE_ITERS, gates_all)
                if p < GRU_LAYERS - 1:
                    keep(2 * NODE_ITERS - 1, 1)
                end_stage(act, nc.scalar)
            norm_act(0, act)
            end_stage(act, nc.scalar)
            pass_act(3, act)
            end_stage(act, nc.scalar)
            end_stage(act, nc.scalar)
            pass_act(4, act)
            end_stage(act, nc.scalar)

            def hyper_product(i):
                for s in range(2):
                    c = 2 * i + s
                    act.wait_ge(S("flip_done_hy"), c + 1)
                    wait(act, S("hy_product"), c - 1)
                    nc.scalar.copy(tmp(1, s), tslot(s)).then_inc(S("flip_taken_hy"), 1)
                    act.wait_ge(S("hy_product"), c + 1)
                    nc.scalar.activation(big[:, cslice(c)], ps[:, s, 0:CN], ACT.Identity, bias=col(HY_B))\
                        .then_inc(S("hy_out"), 1)
            turns(act, NODE_ITERS, hyper_product)
            batch_act(0, act, col(SCALE))
            end_stage(act, nc.scalar)

            def hyper_relu(i):
                for s in range(2):
                    c = 2 * i + s
                    wait(act, S("flip_done_hr"), c - 1)
                    nc.scalar.activation(tmp(0, s), big[:, cslice(c)], ACT.Relu,
                                         bias=col(SHIFT), scale=col(SCALE)).then_inc(S("hy_relu"), 1)
            turns(act, NODE_ITERS, hyper_relu)
            end_stage(act, nc.scalar)
            norm_act(1, act)
            end_stage(act, nc.scalar)

            def copy_fm(tag):
                def body(i):
                    for s in range(2):
                        c = 2 * i + s
                        act.wait_ge(S("flip_done" + tag), c + 1)
                        nc.scalar.copy(x_fm[:, cslice(c)], tslot(s)).then_inc(S("flip_taken" + tag), 1)
                turns(act, NODE_ITERS, body)

            copy_fm("_x2")
            batch_act(1, act, col(SCALE))
            end_stage(act, nc.scalar)

            def scores(i):
                for s in range(2):
                    c = 2 * i + s
                    act.wait_ge(S("s_ready"), c + 1)
                    nc.scalar.activation(u1_rows[:, cslice(c)], ps[:, 2 + s, 0:CN], ACT.Tanh).then_inc(S("act_sc"), 1)
                    nc.scalar.activation(small[:, 4, bslice(c)], ps[:, 2 + s, CN:CN + CB], ACT.Tanh).then_inc(S("act_sc"), 1)
                    nc.scalar.copy(stage_nm[:, bslice(c), 0:P],
                                   tslot(s).rearrange("p (b f) -> p b f", f=P)).then_inc(S("s_taken"), 1)
            turns(act, NODE_ITERS, scores)
            act.wait_ge(S("act_sc"), 4 * NODE_ITERS)
            nc.scalar.activation(u2_rows, u1_rows, ACT.Exp, scale=0.01).then_inc(S("act_exp"), 1)
            nc.scalar.activation(stage_nm[:, :, P + 1], small[:, 4, :], ACT.Exp).then_inc(S("act_exp"), 1)
            nc.scalar.activation(stage_nm[:, :, P + 2], small[:, 4, :], ACT.Exp, scale=0.01).then_inc(S("act_exp"), 1)
            act.wait_ge(S("act_exp"), 3)
            nc.scalar.activation(u1_rows, u1_rows, ACT.Exp).then_inc(S("act_exp"), 1)
            end_stage(act, nc.scalar)
            end_stage(act, nc.scalar)
            pass_act(5, act)
            end_stage(act, nc.scalar)

            def att_relu(i):
                for s in range(2 * CB):
                    b = i * 2 * CB + s
                    if s == 0 and not isinstance(i, int):
                        act.wait_ge(S("at_added"), 2 * i)
                    if s == 0 and isinstance(i, int):
                        act.wait_ge(S("inverse_done_at"), 1)
                    nc.scalar.activation(x_fm[:, s * P:(s + 1) * P], acc_nm[:, bass.ds(b, 1), 0:P]
                                         .rearrange("p b f -> p (b f)"), ACT.Relu,
                                         scale=small[:, 1, bass.ds(b, 1)]).then_inc(S("at_relu"), 1)
            turns(act, NODE_ITERS, att_relu)
            end_stage(act, nc.scalar)
            norm_act(2, act)
            end_stage(act, nc.scalar)

            def edge_halves(i):
                for s in range(2):
                    c = 2 * i + s
                    act.wait_ge(S("flip_done_x3"), c + 1)
                    wait(act, S("q_taken"), c - 1)
                    nc.scalar.copy(tmp(1, s), tslot(s)).then_inc(S("flip_taken_x3"), 1)
                    act.wait_ge(S("pq_ready"), c + 1)
                    nc.scalar.copy(stage_rows[:, bslice(c), :],
                                   ps[:, s, :].rearrange("p (b h f) -> p b h f", b=CB, h=2)[:, :, 0, :]
                                   ).then_inc(S("p_staged"), 1)
            turns(act, NODE_ITERS, edge_halves)
            end_stage(act, nc.scalar)
            pass_act(6, act)
            end_stage(act, nc.scalar)

            def node_mlp(i):
                for s in range(2):
                    c = 2 * i + s
                    act.wait_ge(S("agg_ready"), c + 1)
                    wait(act, S("hid_ready"), c - 1)
                    nc.scalar.copy(tmp(0, s), ps[:, s, 0:CN]).then_inc(S("agg_copied"), 1)
                    act.wait_ge(S("hid_ready"), c + 1)
                    wait(act, S("mesh_ready"), c - 1)
                    nc.scalar.activation(tmp(1, s), ps[:, 2 + s, 0:CN], ACT.Relu, bias=col(N1_B)).then_inc(S("hid_copied"), 1)
            turns(act, NODE_ITERS, node_mlp)
            end_stage(act, nc.scalar)
            norm_act(3, act)
            end_stage(act, nc.scalar)

        @block.tensor
        def _(pe):
            pe.wait_ge(S("consts"), 1)
            pe.wait_ge(S("weights_in"), 80)
            for j in range(10):
                last = nc.tensor.transpose(ps[:, 5 + j // 4, (j % 4) * P:(j % 4 + 1) * P], raw_w[:, j, :], ident[:, :])
            last.then_inc(S("w_flipped"), 1)
            pe.wait_ge(S("w_copied"), 1)
            for l in range(GRU_LAYERS):
                last = nc.tensor.matmul(ps[:, 1 + l, 0:3 * P], tr_w[:, 3 + l, :],
                                        tr_w[:, 0:3, :].rearrange("p m f -> p (m f)"), start=True, stop=True)
            last.then_inc(S("w_combined"), 1)

            def h0_product(c, s):
                pe.wait_ge(S("flip_taken_h0x"), c + 1)
                wait(pe, S("h0_ready"), c - 1)
                if isinstance(c, int) and c < 2:
                    pe.wait_ge(S("w_comb_copied"), 1)
                nc.tensor.matmul(ps[:, s, 0:CN], w_lin[:, :], tmp(1, s), start=True, stop=True)\
                    .then_inc(S("h0_product"), 1)

            def h0_rows(c, s):
                pe.wait_ge(S("h0_kept"), c + 1)
                wait(pe, S("h0_staged"), c - 1)
                for b in range(CB):
                    last = nc.tensor.transpose(ps[:, 6 + s, b * P:(b + 1) * P], tmp(2, s)[:, b * P:(b + 1) * P],
                                               ident[:, :])
                last.then_inc(S("h0_rows"), 1)

            def h0(i):
                for s in range(2):
                    c = 2 * i + s
                    flip_pe("_h0x", pe, tmp(0, s), c, s, S("cut_h0x"))
                    if not (isinstance(i, int) and c == 0):
                        h0_product(c - 1, 1 - s)
                    if not (isinstance(i, int) and i == 0):
                        h0_rows(c - 2, s)
            turns(pe, NODE_ITERS, h0, peeled=2)
            h0_product(NC - 1, 1)
            h0_rows(NC - 2, 0)
            h0_rows(NC - 1, 1)

            pe.wait_ge(S("h0_staged"), NC)
            pe.wait_ge(S("counted"), 1)
            nc.tensor.matmul(ps[:, 0, 0:1], count_b, ones[:, 0:1], start=True, stop=True)
            nc.tensor.matmul(ps[:, 0, 1:2], ones[:, :], tiny[:, 0:1], start=True, stop=True).then_inc(S("totals"), 1)
            pe.wait_ge(S("tot_copied"), 1)
            nc.tensor.matmul(ps[:, 1, 0:1], lower[:, :], tiny[:, 1:2], start=True, stop=True).then_inc(S("bases"), 1)
            pe.wait_ge(S("flag_ready"), 1)
            with pe.If(pe.value_load(flag[0:1, 0:1], min_val=0, max_val=E)):
                pe.wait_ge(S("diag0_ready"), 1)
                nc.tensor.matmul(ps[:, 2, 0:MASKB], lower[:, :], count_b, start=True, stop=False)
                nc.tensor.matmul(ps[:, 2, 0:MASKB], ones[:, :], diag, start=False, stop=True).then_inc(S("places0"), 1)
            pe.wait_ge(S("pair_cols"), 1)
            nc.tensor.matmul(ps[:, 3, 0:1], lower[:, :], tiny[:, 5:6], start=True, stop=True).then_inc(S("pair_sums"), 1)
            pe.wait_ge(S("pair_cols"), 2)
            nc.tensor.matmul(ps[:, 4, 0:1], step_down[:, :], tiny[:, 7:8], start=True, stop=True).then_inc(S("pair_sums"), 1)
            pe.wait_ge(S("pair_cols"), 3)
            for g in range(TG):
                nc.tensor.matmul(ps[:, 5, 2 * g:2 * g + 2], tile_ge[:, g * P:(g + 1) * P], tiny[:, 8:10],
                                 start=True, stop=True)
            for j in range(2):
                last = nc.tensor.matmul(ps[:, 6 + j, 0:T // 2], sel_blocks[:, :],
                                        tile_ge[:, j * (T // 2):(j + 1) * (T // 2)], start=True, stop=True)
            last.then_inc(S("pair_sums"), 1)
            for n in range(2):
                pe.wait_ge(S("pair_values"), n + 1)
                for g in range(TG):
                    last = nc.tensor.transpose(ps[:, 2 * n + g // 4, (g % 4) * P:(g % 4 + 1) * P], pair_f[:, g, :],
                                               ident[:, :])
                last.then_inc(S("pair_flipped"), 1)
            end_stage(pe, nc.tensor)

            for p in range(GRU_LAYERS):
                pass_pe(p, pe)
                end_stage(pe, nc.tensor)

                def flip_new(c, s, p=p):
                    flip_pe(p, pe, tmp(6, s), c, s, Q("h_ready", p))

                def gru(i, p=p):
                    for s in range(2):
                        c = 2 * i + s
                        wait(pe, Q("z_ready", p), c - 1)
                        for j in range(2):
                            nc.tensor.matmul(ps[:, s, j * CN:(j + 1) * CN], w_comb[:, p, j * P:(j + 1) * P],
                                             acc[:, cslice(c)], start=True, stop=False)
                            last = nc.tensor.matmul(ps[:, s, j * CN:(j + 1) * CN], w_hh[:, j * P:(j + 1) * P],
                                                    x_fm[:, cslice(c)], start=False, stop=True)
                        last.then_inc(Q("rz_ready", p).sem, 1)
                        wait(pe, Q("n_in", p), c - 1)
                        nc.tensor.matmul(ps[:, 2 + s, 0:CN], w_comb[:, p, 2 * P:3 * P], acc[:, cslice(c)],
                                         start=True, stop=True)
                        nc.tensor.matmul(ps[:, 2 + s, CN:2 * CN], w_hh[:, 2 * P:3 * P], x_fm[:, cslice(c)],
                                         start=True, stop=True).then_inc(Q("nh_ready", p).sem, 1)
                        if not (isinstance(i, int) and s == 0):
                            flip_new(c - 1, 1 - s)
                turns(pe, NODE_ITERS, gru)
                flip_new(2 * NODE_ITERS - 1, 1)
                end_stage(pe, nc.tensor)
            end_stage(pe, nc.tensor)
            pass_pe(3, pe)
            end_stage(pe, nc.tensor)
            end_stage(pe, nc.tensor)
            pass_pe(4, pe)
            end_stage(pe, nc.tensor)

            def hyper_product(i):
                for s in range(2):
                    c = 2 * i + s
                    flip_pe("_hy", pe, tmp(0, s), c, s, S("hy_scaled"))
                    pe.wait_ge(S("flip_taken_hy"), c + 1)
                    wait(pe, S("hy_out"), c - 1)
                    nc.tensor.matmul(ps[:, s, 0:CN], w_hyper[:, :], tmp(1, s), start=True, stop=True).then_inc(S("hy_product"), 1)
            turns(pe, NODE_ITERS, hyper_product)
            end_stage(pe, nc.tensor)

            def hyper_rows(i):
                for s in range(2):
                    c = 2 * i + s
                    flip_pe("_hr", pe, tmp(0, s), c, s, S("hy_relu"))
            turns(pe, NODE_ITERS, hyper_rows)
            end_stage(pe, nc.tensor)
            end_stage(pe, nc.tensor)

            def to_fm(i):
                for s in range(2):
                    c = 2 * i + s
                    flip_pe("_x2", pe, tmp(0, s), c, s, S("cut_x2"))
            turns(pe, NODE_ITERS, to_fm)
            end_stage(pe, nc.tensor)

            def scores(i):
                for s in range(2):
                    c = 2 * i + s
                    pe.wait_ge(S("xn_ready"), c + 1)
                    for j in range(2):
                        last = nc.tensor.matmul(ps[:, s, j * CN:(j + 1) * CN], w_att[:, (1 + j) * P:(2 + j) * P],
                                                tmp_acc(0, s), start=True, stop=True)
                    last.then_inc(S("sc_ready"), 1)
                    wait(pe, S("s_taken"), c - 1)
                    for b in range(CB):
                        nc.tensor.matmul(ps[:, 4 + s, b * P:(b + 1) * P], tmp_acc(0, s)[:, b * P:(b + 1) * P],
                                         w_att[:, 0:P], start=True, stop=True)
                    pe.wait_ge(S("sc_prod"), c + 1)
                    nc.tensor.matmul(ps[:, 2 + s, 0:CN], ones[:, :], tmp_acc(1, s), start=True, stop=True)
                    for b in range(CB):
                        last = nc.tensor.matmul(ps[:, 2 + s, CN + b:CN + b + 1],
                                                tmp_acc(2, s)[:, b * P:(b + 1) * P], ones[:, 0:1],
                                                start=True, stop=True)
                    last.then_inc(S("s_ready"), 1)
            turns(pe, NODE_ITERS, scores)
            end_stage(pe, nc.tensor)
            end_stage(pe, nc.tensor)
            pass_pe(5, pe)
            end_stage(pe, nc.tensor)
            end_stage(pe, nc.tensor)
            end_stage(pe, nc.tensor)

            def edge_halves(i):
                for s in range(2):
                    c = 2 * i + s
                    flip_pe("_x3", pe, tmp(0, s), c, s, S("cut_x3"))
                    pe.wait_ge(S("flip_taken_x3"), c + 1)
                    wait(pe, S("p_staged"), c - 1)
                    wait(pe, S("q_taken"), c - 1)
                    for b in range(CB):
                        last = nc.tensor.matmul(ps[:, s, b * CN:(b + 1) * CN], tmp(1, s)[:, b * P:(b + 1) * P],
                                                w_e1, start=True, stop=True)
                    last.then_inc(S("pq_ready"), 1)
            turns(pe, NODE_ITERS, edge_halves)
            end_stage(pe, nc.tensor)
            pass_pe(6, pe)
            end_stage(pe, nc.tensor)
            pe.wait_ge(S("degree_in"), 16)

            def node_mlp(i):
                for s in range(2):
                    c = 2 * i + s
                    wait(pe, S("agg_copied"), c - 1)
                    nc.tensor.matmul(ps[:, s, 0:CN], w_e2, acc[:, cslice(c)], start=True, stop=False)
                    nc.tensor.matmul(ps[:, s, 0:CN], row0[0:1, 0:P], stage[0:1, cslice(c)], start=False, stop=True)\
                        .then_inc(S("agg_ready"), 1)
                    wait(pe, S("hid_copied"), c - 1)
                    nc.tensor.matmul(ps[:, 2 + s, 0:CN], w_n1[:, 0:P], x_fm[:, cslice(c)], start=True, stop=False)
                    pe.wait_ge(S("agg_copied"), c + 1)
                    nc.tensor.matmul(ps[:, 2 + s, 0:CN], w_n1[:, P:2 * P], tmp(0, s), start=False, stop=True)\
                        .then_inc(S("hid_ready"), 1)
                    pe.wait_ge(S("hid_copied"), c + 1)
                    wait(pe, S("mesh_added"), c - 1)
                    for b in range(CB):
                        nc.tensor.matmul(ps[:, 4 + s, b * P:(b + 1) * P], tmp(1, s)[:, b * P:(b + 1) * P], w_n2,
                                         start=True, stop=False)
                        last = nc.tensor.matmul(ps[:, 4 + s, b * P:(b + 1) * P], ones[0:1, :], row0[0:1, P:2 * P],
                                                start=False, stop=True)
                    last.then_inc(S("mesh_ready"), 1)
            turns(pe, NODE_ITERS, node_mlp)
            end_stage(pe, nc.tensor)
            end_stage(pe, nc.tensor)

        @block.vector
        def _(dve):
            for view in (dst_e, src_e, next_e):
                nc.vector.memset(view, PAD_NODE).then_inc(S("edges_padded"), 1)
            nc.vector.memset(x_nm[:, :, :], 0.0).then_inc(S("x_zero"), 1)
            step = chain(dve)
            nc.vector.memset(ones_row, 1.0)
            nc.vector.memset(small[:, :, :], 0.0)
            nc.vector.memset(big[:, 0:4 * T], 0.0)
            nc.vector.memset(tiny, 0.0)
            step(nc.vector.memset(count_b, 0.0))
            dve.wait_ge(S("edges_in"), 96)
            step(nc.vector.tensor_scalar(int_a, src_e, NODE_BITS, None, ALU.logical_shift_left))
            nc.vector.tensor_tensor(packed, int_a, dst_e, ALU.bitwise_or).then_inc(S("packed_ready"), 1)
            step(nc.vector.tensor_scalar(int_b, dst_e, 7, None, ALU.logical_shift_right))
            step(nc.vector.tensor_copy(blk0, int_b))
            step(nc.vector.tensor_scalar(int_b, next_e, 7, None, ALU.logical_shift_right))
            step(nc.vector.tensor_copy(next_blk, int_b))
            step(nc.vector.tensor_tensor(scan, next_blk, blk0, ALU.is_lt))
            nc.vector.tensor_reduce(tiny[:, 0:1], scan, AX_X, ALU.add)
            dve.wait_ge(S("consts"), 1)

            def count_block(b):
                wait(dve, S("masked"), b)
                nc.vector.tensor_scalar(mask, blk0, iota[:, bass.ds(b, 1)], None, ALU.is_equal, ALU.add,
                                        accum_out=count_b[:, bass.ds(b, 1)]).then_inc(S("masked"), 1)
            turns(dve, NB1, count_block)
            dve.wait_ge(S("masked"), NB1)
            dve.sem_inc(S("counted"), 1)
            dve.wait_ge(S("totals"), 1)
            nc.vector.tensor_copy(flag[:, :], ps[:, 0, 1:2]).then_inc(S("flag_ready"), 1)
            nc.vector.tensor_copy(tiny[:, 1:2], ps[:, 0, 0:1]).then_inc(S("tot_copied"), 1)
            dve.wait_ge(S("bases"), 1)
            step(nc.vector.tensor_copy(tiny[:, 2:3], ps[:, 1, 0:1]))
            with dve.If(dve.value_load(flag[0:1, 0:1], min_val=0, max_val=E)):
                sort = Steps(dve, "sort_steps", 0)
                nc.vector.tensor_scalar(diag, ident[:, :], tiny[:, 2:3], None, ALU.mult).then_inc(S("diag0_ready"), 1)
                dve.wait_ge(S("places0"), 1)
                sort(nc.vector.tensor_copy(base, ps[:, 2, 0:MASKB]))
                sort(nc.vector.memset(pos0, 0.0))
                with dve.Fori(0, NB1) as b:
                    rank = Steps(dve, "sort_ranks", 4)
                    rank.chunk(b)
                    rank(nc.vector.tensor_scalar(mask, blk0, iota[:, bass.ds(b, 1)], None, ALU.is_equal))
                    rank(nc.vector.tensor_tensor_scan(scan, ones_row, mask, base[:, bass.ds(b, 1)], ALU.mult, ALU.add))
                    rank(nc.vector.tensor_tensor(prod, scan, mask, ALU.mult))
                    rank(nc.vector.tensor_tensor(pos0, pos0, prod, ALU.add))
                nc.vector.tensor_scalar(slot_addr, pos0, -1.0, None, ALU.add).then_inc(S("addr_ready"), 1)

                def ring(i):
                    for h in range(2):
                        c = 2 * i + h
                        dve.wait_ge(S("ring_half"), c + 1)
                        nc.vector.tensor_copy(val_ring[:, h * SC:(h + 1) * SC], packed[:, bass.ds(SC * c, SC)])\
                            .then_inc(S("ring_filled"), 1)
                turns(dve, SCATTER_ITERS, ring)
            step(nc.vector.tensor_copy(tiny_i[:, 0:1], tiny[:, 2:3]))
            step(nc.vector.tensor_scalar(tiny_i[:, 1:2], tiny_i[:, 0:1], 7, None, ALU.logical_shift_right))
            step(nc.vector.tensor_copy(tiny[:, 3:4], tiny_i[:, 1:2]))
            step(nc.vector.scalar_tensor_tensor(tiny_i[:, 2:3], tiny[:, 1:2], -1.0, tiny[:, 2:3], ALU.add, ALU.add))
            step(nc.vector.tensor_scalar(tiny_i[:, 3:4], tiny_i[:, 2:3], 7, None, ALU.arith_shift_right))
            step(nc.vector.tensor_scalar(tiny[:, 4:5], tiny[:, 1:2], 0.0, None, ALU.is_gt))
            step(nc.vector.scalar_tensor_tensor(tiny[:, 5:6], tiny_i[:, 3:4], 1.0, tiny[:, 3:4], ALU.add, ALU.subtract))
            step(nc.vector.tensor_tensor(tiny[:, 5:6], tiny[:, 5:6], tiny[:, 4:5], ALU.mult))
            nc.vector.tensor_tensor(tiny[:, 5:6], tiny[:, 5:6], real_block[:, :], ALU.mult).then_inc(S("pair_cols"), 1)
            dve.wait_ge(S("pair_sums"), 1)
            step(nc.vector.tensor_copy(tiny[:, 6:7], ps[:, 3, 0:1]))
            nc.vector.tensor_tensor(tiny[:, 7:8], tiny[:, 3:4], tiny[:, 6:7], ALU.subtract).then_inc(S("pair_cols"), 1)
            nc.vector.tensor_scalar(tile_ge, tile_iota[:, :], tiny[:, 6:7], None, ALU.is_ge)
            dve.wait_ge(S("pair_sums"), 2)
            nc.vector.tensor_copy(tiny[:, 9:10], sel_blocks[:, 0:1])
            nc.vector.tensor_tensor(tiny[:, 8:9], ps[:, 4, 0:1], sel_blocks[:, 0:1], ALU.mult).then_inc(S("pair_cols"), 1)
            dve.wait_ge(S("pair_sums"), 3)
            pairs = ps[:, 5, 0:2 * TG].rearrange("p (g a) -> p g a", a=2)
            step(nc.vector.tensor_tensor(pair_blk[:, :], pair_blk[:, :], pairs[:, :, 0], ALU.add))
            nc.vector.tensor_scalar(pair_idx[:, :], pair_blk[:, :], float(EDGE_TILES - 1), None, ALU.min)\
                .then_inc(S("pairs_ready"), 1)
            dve.wait_ge(S("pairs_ready"), 1)
            step(nc.vector.tensor_scalar(pair_blk[:, :], pairs[:, :, 1], float(P), None, ALU.mult))
            for j in range(2):
                nc.vector.tensor_copy(block_of[0][:, j * (T // 2):(j + 1) * (T // 2)], ps[:, 6 + j, 0:T // 2])
            step(nc.vector.tensor_scalar(int_a, src_e, 7, None, ALU.logical_shift_right))
            nc.vector.memset(blk1[:, EC:T], 255.0)
            step(nc.vector.tensor_copy(blk1[:, 0:EC], int_a))
            step(nc.vector.tensor_scalar(int_b, src_e, P - 1, None, ALU.bitwise_and))
            step(nc.vector.scalar_tensor_tensor(int_a, dst_e, float(P), int_b, ALU.mult, ALU.add))
            step(nc.vector.tensor_scalar(int_a, int_a, 1.0, None, ALU.add))
            step(nc.vector.tensor_scalar(int_b, int_a, LOW_BITS, None, ALU.logical_shift_right))
            step(nc.vector.tensor_copy(hi1[:, 0:EC], int_b))
            step(nc.vector.tensor_scalar(int_b, int_a, (1 << LOW_BITS) - 1, None, ALU.bitwise_and))
            step(nc.vector.tensor_scalar(lo1[:, 0:EC], int_b, 1.0 / (1 << LOW_BITS), None, ALU.mult))
            step(nc.vector.memset(count_b, 0.0))
            dve.wait_ge(S("vectors_in"), 16 * 15)
            nc.vector.tensor_tensor(col(B_R), col(13), col(15), ALU.add)
            step(nc.vector.tensor_tensor(col(B_Z), col(14), col(16), ALU.add))
            dve.wait_ge(S("pairs_in"), 16 * TG)
            step(nc.vector.tensor_scalar(pair_a, pair_rows, (1 << NODE_BITS) - 1, None, ALU.bitwise_and))
            for g in range(TG):
                last = nc.vector.tensor_scalar(pair_f[:, g, :], pair_a[:, g, :], pair_blk[:, g:g + 1], None, ALU.subtract)
            last.then_inc(S("pair_values"), 1)
            step(nc.vector.tensor_scalar(pair_b, pair_rows, NODE_BITS, None, ALU.logical_shift_right))
            for n, (out, cast) in enumerate(((local[0], None), (gather_idx[0], None))):
                dve.wait_ge(S("pair_flipped"), n + 1)
                if n == 0:
                    step(nc.vector.tensor_scalar(pair_a, pair_b, float(N), None, ALU.is_lt))
                    nc.vector.tensor_tensor(pair_f, pair_b, pair_a, ALU.mult).then_inc(S("pair_values"), 1)
                for j in range(2):
                    w = min(4, TG - 4 * j) * P
                    nc.vector.tensor_copy(out[:, j * 4 * P:j * 4 * P + w], ps[:, 2 * n + j, 0:w])
            end_stage(dve, nc.vector)

            for p in range(GRU_LAYERS):
                pass_dve(p, dve)
                end_stage(dve, nc.vector)
                last_layer = p == GRU_LAYERS - 1
                steps = Steps(dve, "gru_steps", 3, 3 * NC * p)
                stat = Steps(dve, "gru_stats", 2 * CB)

                def residual(c, s, p=p, stat=stat):
                    stat.chunk(c)
                    blk = x_nm[:, bslice(c), :].rearrange("p b f -> p (b f)")
                    wait(dve, Q("flip_done_gru", p), c + 1)
                    nc.vector.tensor_tensor(blk, blk, tslot(s), ALU.add).then_inc(Q("flip_taken_gru", p).sem, 1)
                    wait(dve, Q("flip_taken_gru", p), c + 1)
                    stats_dve("", dve, c, stat)

                def gru(i, p=p, steps=steps, last_layer=last_layer):
                    for s in range(2):
                        c = 2 * i + s
                        steps.chunk(c)
                        wait(dve, Q("nh_ready", p), c + 1)
                        wait(dve, Q("r_ready", p), c + 1)
                        steps(nc.vector.scalar_tensor_tensor(tmp(4, s), ps[:, 2 + s, CN:2 * CN], col(B_HN),
                                                             tmp(0, s), ALU.add, ALU.mult))
                        nc.vector.tensor_tensor(tmp(2, s), tmp(4, s), ps[:, 2 + s, 0:CN], ALU.add)\
                            .then_inc(Q("n_in", p).sem, 1)
                        if last_layer and not (isinstance(i, int) and s == 0):
                            residual(c - 1, 1 - s)
                        wait(dve, Q("n_ready", p), c + 1)
                        steps(nc.vector.tensor_tensor(tmp(5, s), x_fm[:, cslice(c)], tmp(3, s), ALU.subtract))
                        steps(nc.vector.tensor_tensor(tmp(5, s), tmp(5, s), tmp(1, s), ALU.mult))
                        wait(dve, Q("flip_done_gru", p), c - 1)
                        if not last_layer:
                            wait(dve, Q("h_kept", p), c - 1)
                        nc.vector.tensor_tensor(tmp(6, s), tmp(5, s), tmp(3, s), ALU.add).then_inc(Q("h_ready", p).sem, 1)
                turns(dve, NODE_ITERS, gru)
                if last_layer:
                    residual(2 * NODE_ITERS - 1, 1)
                end_stage(dve, nc.vector)
            norm_dve(0, dve)
            end_stage(dve, nc.vector)
            pass_dve(3, dve)
            end_stage(dve, nc.vector)

            unpack1_dve(dve)
            nc.vector.tensor_copy(small[:, 4, :], acc_nm[:, :, P]).then_inc(S("degree_ready"), 1)
            safe_inverse_dve("_b", dve)

            def hyper_scale(i):
                for s in range(2 * CB):
                    b = i * 2 * CB + s
                    nc.vector.tensor_scalar(stage_rows[:, bass.ds(b, 1), :].rearrange("p b f -> p (b f)"),
                                            acc_nm[:, bass.ds(b, 1), 0:P].rearrange("p b f -> p (b f)"),
                                            small[:, 1, bass.ds(b, 1)], None, ALU.mult).then_inc(S("hyper_scaled"), 1)
            turns(dve, NODE_ITERS, hyper_scale)
            end_stage(dve, nc.vector)
            pass_dve(4, dve)
            end_stage(dve, nc.vector)

            safe_inverse_dve("_d", dve)

            def node_scale(i):
                for s in range(2):
                    c = 2 * i + s
                    wait(dve, S("flip_done_hy"), c - 1)
                    for b in range(CB):
                        last = nc.vector.tensor_scalar(tmp(0, s)[:, b * P:(b + 1) * P],
                                                       acc_nm[:, bass.ds(c * CB + b, 1), 0:P].rearrange("p b f -> p (b f)"),
                                                       small[:, 1, bass.ds(c * CB + b, 1)], None, ALU.mult)
                    last.then_inc(S("hy_scaled"), 1)
            turns(dve, NODE_ITERS, node_scale)
            dve.wait_ge(S("hy_out"), 2 * NODE_ITERS)
            batch_dve(0, dve, big, col(HY_G), col(HY_BE), col(SCALE), col(SHIFT))
            end_stage(dve, nc.vector)

            stat = Steps(dve, "hr_steps", 2 * CB)

            def hyper_residual(i):
                for s in range(2):
                    c = 2 * i + s
                    stat.chunk(c)
                    blk = x_nm[:, bslice(c), :].rearrange("p b f -> p (b f)")
                    dve.wait_ge(S("flip_done_hr"), c + 1)
                    nc.vector.tensor_tensor(blk, blk, tslot(s), ALU.add).then_inc(S("flip_taken_hr"), 1)
                    dve.wait_ge(S("flip_taken_hr"), c + 1)
                    stats_dve("", dve, c, stat)
            turns(dve, NODE_ITERS, hyper_residual)
            end_stage(dve, nc.vector)
            norm_dve(1, dve)
            end_stage(dve, nc.vector)

            def cut_x2(i):
                for s in range(2):
                    cut_dve("_x2", dve, 2 * i + s, s, tmp(0, s))
            turns(dve, NODE_ITERS, cut_x2)
            dve.wait_ge(S("flip_taken_x2"), 2 * NODE_ITERS)
            batch_dve(1, dve, x_fm, col(AT_G), col(AT_BE), col(SCALE), col(SHIFT))
            end_stage(dve, nc.vector)

            nc.vector.memset(stage_nm[:, :, P], 1.0)

            def scores(i):
                for s in range(2):
                    c = 2 * i + s
                    wait(dve, S("s_ready"), c - 1)
                    nc.vector.tensor_scalar(tmp_acc(0, s), x_fm[:, cslice(c)], col(SCALE), col(SHIFT), ALU.mult, ALU.add)\
                        .then_inc(S("xn_ready"), 1)
                    dve.wait_ge(S("xn_ready"), c + 1)
                    dve.wait_ge(S("sc_ready"), c + 1)
                    nc.vector.tensor_tensor(tmp_acc(1, s), ps[:, s, 0:CN], tmp_acc(0, s), ALU.mult)
                    nc.vector.tensor_tensor(tmp_acc(2, s), ps[:, s, CN:2 * CN], tmp_acc(0, s), ALU.mult)\
                        .then_inc(S("sc_prod"), 1)
            turns(dve, NODE_ITERS, scores)
            end_stage(dve, nc.vector)
            dve.sem_inc(S("score_cols"), 1)
            end_stage(dve, nc.vector)
            pass_dve(5, dve)
            end_stage(dve, nc.vector)

            one = chain(dve)
            one(nc.vector.tensor_scalar(small[:, 0, :], acc_nm[:, :, P], 1e-16, None, ALU.max))
            nc.vector.reciprocal(small[:, 1, :], small[:, 0, :]).then_inc(S("inverse_done_at"), 1)
            stat2 = Steps(dve, "at_stats", 2 * CB)

            def att_residual(i):
                for s in range(2):
                    c = 2 * i + s
                    stat2.chunk(c)
                    blk = x_nm[:, bslice(c), :].rearrange("p b f -> p (b f)")
                    dve.wait_ge(S("at_relu"), (c + 1) * CB)
                    nc.vector.tensor_tensor(blk, blk, x_fm[:, s * CN:(s + 1) * CN], ALU.add).then_inc(S("at_added"), 1)
                    dve.wait_ge(S("at_added"), c + 1)
                    stats_dve("", dve, c, stat2)
            turns(dve, NODE_ITERS, att_residual)
            end_stage(dve, nc.vector)
            norm_dve(2, dve)
            end_stage(dve, nc.vector)

            def edge_halves(i):
                for s in range(2):
                    c = 2 * i + s
                    cut_dve("_x3", dve, c, s, tmp(0, s))
                    dve.wait_ge(S("flip_taken_x3"), c + 1)
                    nc.vector.tensor_copy(x_fm[:, cslice(c)], tmp(1, s))
                    dve.wait_ge(S("p_staged"), c + 1)
                    nc.vector.tensor_tensor(q_nm[:, cslice(c)].rearrange("p (b f) -> p b f", b=CB),
                                            ps[:, s, :].rearrange("p (b h f) -> p b h f", b=CB, h=2)[:, :, 1, :],
                                            be1_rows.unsqueeze(1).to_broadcast([P, CB, P]), ALU.add)\
                        .then_inc(S("q_taken"), 1)
            turns(dve, NODE_ITERS, edge_halves)
            end_stage(dve, nc.vector)
            pass_dve(6, dve)
            end_stage(dve, nc.vector)

            stat3 = Steps(dve, "mesh_stats", 2 * CB)

            def mesh_residual(i):
                for s in range(2):
                    c = 2 * i + s
                    stat3.chunk(c)
                    blk = x_nm[:, bslice(c), :].rearrange("p b f -> p (b f)")
                    dve.wait_ge(S("mesh_ready"), c + 1)
                    nc.vector.scalar_tensor_tensor(blk, blk, 2.0, ps[:, 4 + s, 0:CN], ALU.mult, ALU.add)\
                        .then_inc(S("mesh_added"), 1)
                    dve.wait_ge(S("mesh_added"), c + 1)
                    stats_dve("", dve, c, stat3)
            turns(dve, NODE_ITERS, mesh_residual)
            end_stage(dve, nc.vector)
            norm_dve(3, dve)
            end_stage(dve, nc.vector)


_INS = ["x", "src", "dst", "L0_gnn_lin_w", "L0_gnn_lin_b", "L0_gnn_weight", "L0_gnn_w_ih", "L0_gnn_w_hh",
        "L0_gnn_b_ih", "L0_gnn_b_hh", "L1_gnn_hyperedge_weight", "L1_gnn_W", "L1_gnn_b", "L1_gnn_gamma",
        "L1_gnn_beta", "L2_gnn_kernel", "L2_gnn_kernel1", "L2_gnn_kernel2", "L2_gnn_gamma", "L2_gnn_beta",
        "L3_gnn_We1", "L3_gnn_be1", "L3_gnn_We2", "L3_gnn_be2", "L3_gnn_Wn1", "L3_gnn_bn1", "L3_gnn_Wn2",
        "L3_gnn_bn2"]


def kernel(**inputs):
    import numpy as np
    import concourse.bacc as bacc
    from concourse.bass_utils import run_bass_kernel_spmd

    nc = bacc.Bacc("TRN2", target_bir_lowering=False, num_devices=1)
    arrays = {name: np.ascontiguousarray(inputs[name]) for name in _INS}
    d = {name: nc.dram_tensor(name, a.shape, mybir.dt.from_np(a.dtype), kind="ExternalInput").ap()
         for name, a in arrays.items()}
    d["out"] = nc.dram_tensor("out", (N, P), F32, kind="ExternalOutput").ap()
    gnn(nc, d)
    return run_bass_kernel_spmd(nc, [arrays], core_ids=[0]).results[0]["out"]
```

```python
from contextlib import ExitStack

import concourse.bass as bass
from concourse import mybir

F32 = mybir.dt.float32
F16 = mybir.dt.float16
I32 = mybir.dt.int32
I16 = mybir.dt.int16
U8 = mybir.dt.uint8
ALU = mybir.AluOpType
ACT = mybir.ActivationFunctionType
AX_X = mybir.AxisListType.X

P = 128
N = 6250
E = 106250
NB = (N + P - 1) // P
NB1 = NB + 1
NBP = 52
NP = NBP * P
CB = 2
CN = CB * P
NODE_ITERS = NP // (2 * CN)
NC = 2 * NODE_ITERS
EC = 832
E_FULL = E // EC
CH = 8
T = -(-((E + NB * (P - 1)) // P) // (2 * CH)) * 2 * CH
PASS_ITERS = T // (2 * CH)
TP = T + 2 * CH
assert TP == -(-T // P) * P
W = 132
SC = 16
SCATTER_ITERS = EC // (2 * SC)
EDGE_TILES = P * EC // P
PAD_NODE = NB * P
NODE_BITS = 13
TG = -(-T // P)
LOW_BITS = 11
BUILD = 4
MASKB = 128
ST = 250
NST = N // ST
H0_FIRST = 7
EPS = 1e-5
GRU_LAYERS = 3


class Count:
    def __init__(self, sem, base):
        self.sem, self.base = sem, base


def wait(eng, sem, value):
    if isinstance(value, int) and value <= 0:
        return
    if isinstance(sem, Count):
        eng.wait_ge(sem.sem, value + sem.base)
    else:
        eng.wait_ge(sem, value)


def turns(eng, count, body, peeled=1):
    for i in range(peeled):
        body(i)
    with eng.Fori(peeled, count) as i:
        body(i)


def pass_turns(eng, mode, body):
    if mode != "fm":
        turns(eng, PASS_ITERS, lambda i: body(i, False))
        return
    turns(eng, NC, lambda i: body(i, True))
    with eng.Fori(NC, PASS_ITERS) as i:
        body(i, False)


def gnn(nc, d):
    ctx = ExitStack()
    with ctx:
        def sb(name, shape, dt=F32):
            return ctx.enter_context(nc.sbuf_tensor(name, shape, dt))

        def sem(name):
            return ctx.enter_context(nc.semaphore(name))

        def dram(name, shape, dt=F32):
            return nc.dram_tensor(name, shape, dt, kind="Internal").ap()

        x_nm = sb("x_nm", [P, NBP, P])
        x_fm = sb("x_fm", [P, NP])
        acc = sb("acc", [P, NBP * W])
        stage = sb("stage", [P, NBP * W])
        big = sb("big", [P, 2 * NP])
        gather_idx = [sb(f"gather_idx{k}", [P, TP], I32) for k in range(2)]
        local = [sb(f"local{k}", [P, TP]) for k in range(2)]
        block_of = [sb(f"block_of{k}", [P, T], I16) for k in range(2)]
        rows = sb("rows", [P, 2 * CH, W])
        onehot = sb("onehot", [P, 2 * CH, P])
        idx_ring = sb("idx_ring", [P, 2 * SC], I32)
        val_ring = sb("val_ring", [P, 2 * SC], I32)
        w_late = sb("w_late", [P, 10 * P])
        w_hh = sb("w_hh", [P, 3 * P])
        w_lin = sb("w_lin", [P, P])
        w_hyper = sb("w_hyper", [P, P])
        ident = sb("ident", [P, P])
        ones = sb("ones", [P, P])
        iota = sb("iota", [P, P])
        lower = sb("lower", [P, P])
        sel_blocks = sb("sel_blocks", [P, P])
        step_down = sb("step_down", [P, P])
        tile_iota = sb("tile_iota", [P, TP], F16)
        block_no = sb("block_no", [P, PASS_ITERS])
        cols = sb("cols", [P, 24])
        small = sb("small", [P, 6, NBP])
        mv = sb("mv", [P, NBP, 2])
        mv_chunk = sb("mv_chunk", [P, 2, CB, 2])
        bst = sb("bst", [P, NST, 6])
        bmv = sb("bmv", [P, 2])
        st6 = sb("st6", [P, 2, CB, 6])
        row0 = sb("row0", [1, P])
        ps = ctx.enter_context(nc.psum_tensor("ps", [P, 8, 512], F32))

        acc_nm = acc[:, :].rearrange("p (b w) -> p b w", w=W)
        stage_nm = stage[:, :].rearrange("p (b w) -> p b w", w=W)
        stage_rows = stage[:, 0:NP].rearrange("p (b f) -> p b f", f=P)
        w_comb = w_late[:, 0:9 * P].rearrange("p (l m) -> p l m", l=3)
        w_att = w_late[:, 0:3 * P]
        w_e1 = w_late[:, 3 * P:5 * P]
        w_e2 = w_late[:, 5 * P:6 * P]
        w_n1 = w_late[:, 6 * P:8 * P]
        w_n2 = w_late[:, 8 * P:9 * P]
        be1_rows = w_late[:, 9 * P:10 * P]
        bn2_rows = w_late[:, 0:P]

        dst_e, src_e, int_a, int_b, next_e, packed, slot_addr = [
            acc[:, k * EC:(k + 1) * EC].bitcast(I32) for k in range(7)]
        blk0 = acc[:, 7 * EC:8 * EC]
        blk1, pos1, hi1, lo1, row1, tile1 = [big[:, k * T:(k + 1) * T] for k in range(6)]
        next_blk = big[:, 6 * T:6 * T + EC]
        assert 6 * T + EC <= NP and 8 * EC <= NBP * W
        h = NP + 14 * CN
        scan, prod, ones_row = [big[:, h + k * EC:h + (k + 1) * EC] for k in range(3)]
        blk0_h = prod[:, 0:EC // 2].bitcast(F16)
        mask_h = [t.bitcast(F16) for t in (prod[:, EC // 2:EC], scan[:, 0:EC // 2])]
        assert NB1 % 2 == 0
        mask = big[:, h + 3 * EC:h + 3 * EC + EC // 4].bitcast(U8)
        h += 3 * EC + EC // 4
        count_b, base = big[:, h:h + MASKB], big[:, h + MASKB:h + 2 * MASKB]
        tiny = big[:, h + 2 * MASKB:h + 2 * MASKB + 16]
        tiny_i = big[:, h + 2 * MASKB + 16:h + 2 * MASKB + 24].bitcast(I32)
        assert h + 2 * MASKB + 24 <= 2 * NP and 6 * T <= NP
        diag = scan[:, 0:MASKB]
        tile_ge = big[:, NP + 6 * CN:NP + 6 * CN + TP]
        pos0 = next_blk
        pair_rows, pair_a, pair_b = [acc[:, 4 * EC + k * TP:4 * EC + (k + 1) * TP].bitcast(I32)
                                     .rearrange("p (g e) -> p g e", g=TG) for k in range(3)]
        pair_f = big[:, NP + 6 * CN + TP:NP + 6 * CN + 2 * TP].rearrange("p (g e) -> p g e", g=TG)
        pair_src = big[:, NP + 14 * CN:NP + 14 * CN + TP].rearrange("p (g e) -> p g e", g=TG)
        assert 4 * EC + 3 * TP <= NBP * W and 6 * CN + 2 * TP <= 14 * CN
        pair_idx = sb("pair_idx", [P, TG], I32)
        pair_blk = sb("pair_blk", [P, TG])
        flag = sb("flag", [P, 1], I32)
        real_block = sb("real_block", [P, 1])
        h = NP + 14 * CN
        hot_tile = [big[:, a:a + BUILD * T // 2].bitcast(F16).rearrange("p (m t) -> p m t", m=BUILD)
                    for a in (0, h)]
        h += BUILD * T // 2
        hot_row = [big[:, h + n * BUILD * P:h + (n + 1) * BUILD * P].bitcast(F16)
                   .rearrange("p (m a r) -> p m a r", m=BUILD, a=2) for n in range(2)]
        assert h + 2 * BUILD * P <= 2 * NP
        raw_w = stage[:, 0:10 * P].rearrange("p (m f) -> p m f", f=P)
        tr_w = stage[:, 10 * P:16 * P].rearrange("p (m f) -> p m f", f=P)

        edges = dram("edges", (P * EC, 1), I32)
        widths = [P, P, P, P + 1, P + 1, P + 3, P]
        table = [dram(f"table{p}", (NP, w)) for p, w in enumerate(widths)]
        degree_row = dram("degree_row", (NP, 1))

        stage_end = sem("stage_end")
        boundary = {}

        def end_stage(eng, nc_eng):
            boundary[eng] = boundary.get(eng, 0) + 1
            nc_eng.drain().then_inc(stage_end, 1)
            eng.wait_ge(stage_end, 5 * boundary[eng])

        row_landed = [sem(f"row_landed{s}") for s in range(2 * CH)]
        rows_opened = sem("rows_opened")

        made = {}

        def S(name):
            if name not in made:
                made[name] = sem(name)
            return made[name]

        moves = {"idx_ready": TP // CH, "summed": T, "added": T, "hn_sum": NC, "hn_kept": NC, "hot_ready": T // CH + 1, "acc_zero": 1,
                 "rz_ready": NC, "nh_ready": NC, "r_ready": NC, "z_ready": NC, "n_ready": NC, "n_in": NC,
                 "h_ready": NC, "h_kept": NC, "flip_done_gru": NC, "flip_taken_gru": NC,
                 "stored_gru": 16 * NODE_ITERS}

        def Q(name, p):
            before = p
            if name == "hot_ready":
                before = sum(m != "att" for m in MODES[:p])
            return Count(S(name), moves.get(name, 0) * before)

        LISTS = [0, 0, 0, 0, 1, 1, 0]
        MODES = ["fm", "fm", "fm", "nm", "nm", "att", "edge"]

        def cslice(c):
            return bass.ds(c * CN, CN)

        def bslice(c):
            return bass.ds(c * CB, CB)

        LIN_B, B_R, B_Z, B_IN, B_HN, HY_B, HY_G, HY_BE, AT_G, AT_BE, N1_B, SCALE, SHIFT = range(13)
        E2_B = 17

        def col(j):
            return cols[:, j:j + 1]

        ring_ohT = stage[:, 0:CH * P].rearrange("p (t e) -> p t e", e=P)
        ring_e = stage[:, CH * P:3 * CH * P].rearrange("p (t e) -> p t e", e=P)
        u1_rows = big[:, 0:NP]
        u2_rows = big[:, NP:2 * NP]
        q_nm = big[:, 0:NP]

        block_regs = {}

        def tile_blocks(eng, k, c, which="block"):
            if (eng, which) not in block_regs:
                block_regs[eng, which] = [eng.alloc_register(f"{which}{u}") for u in range(CH)]
            eng.load(block_regs[eng, which], block_of[k][0:1, bass.ds(CH * c, CH)])
            return [eng.snap(r, min_val=0, max_val=NB - 1) for r in block_regs[eng, which]]

        def groups(w):
            per = 512 // w
            return [(g, range(g * per, min((g + 1) * per, CH))) for g in range(-(-CH // per))]

        def psum_sum(h, u, w):
            per = 512 // w
            return ps[:, h * -(-CH // per) + u // per, (u % per) * w:(u % per + 1) * w]

        def pass_pool(p, pool):
            idx_ready, summed = Q("idx_ready", p), Q("summed", p)

            def body(i):
                for h in range(2):
                    wait(pool, idx_ready, 2 * i + h + 1)
                    pool.sem_inc(rows_opened, 1)
                    if not isinstance(i, int):
                        wait(pool, summed, 2 * CH * i + CH * h - CH)
                        pool.sem_inc(rows_opened, 1)
                    for u in range(CH):
                        s = h * CH + u
                        nc.gpsimd.indirect_dma_start(
                            rows[:, s, 0:widths[p]], None, table[p][0:N, :],
                            bass.IndirectOffsetOnAxis(idx_ring[:, s:s + 1], 0),
                        ).then_inc(row_landed[s], 16)
            turns(pool, PASS_ITERS, body)

        def pass_act(p, act):
            k, mode = LISTS[p], MODES[p]
            idx_ready = Q("idx_ready", p)
            for h in range(2):
                nc.scalar.copy(idx_ring[:, h * CH:(h + 1) * CH],
                               gather_idx[k][:, h * CH:(h + 1) * CH]).then_inc(idx_ready.sem, 1)

            def body(i, with_nodes):
                for h in range(2):
                    c = 2 * i + h
                    if mode == "att":
                        blk = tile_blocks(act, k, c)
                        for u in range(CH):
                            s = h * CH + u
                            wait(act, row_landed[s], 16 * (PASS_ITERS * p + i + 1))
                            if u == 0:
                                wait(act, Q("weighed", p), CH * (c - 1))
                            nc.scalar.activation(onehot[:, s, :], u1_rows[:, bass.ds(blk[u] * P, P)],
                                                 ACT.Copy, scale=rows[:, s, 129:130]
                                                 ).then_inc(Q("scaled", p).sem, 1)
                    if mode == "edge":
                        for g in range(2):
                            wait(act, Q("flipped", p), 2 * c + g + 1)
                            nc.scalar.copy(ring_ohT[:, 4 * g:4 * g + 4, :].rearrange("p t e -> p (t e)"), ps[:, 4 + g, :]
                                           ).then_inc(Q("flip_copied", p).sem, 1)
                        for g in range(2):
                            wait(act, Q("edge_pre", p), 2 * c + g + 1)
                            nc.scalar.activation(ring_e[:, h * CH + 4 * g:h * CH + 4 * g + 4, :]
                                                 .rearrange("p t e -> p (t e)"), ps[:, 6 + g, :], ACT.Relu
                                                 ).then_inc(Q("edge_act", p).sem, 1)
                    if mode != "att":
                        for u in range(CH):
                            wait(act, row_landed[h * CH + u], 16 * (PASS_ITERS * p + i + 1))
                    nc.scalar.copy(idx_ring[:, h * CH:(h + 1) * CH],
                                   gather_idx[k][:, bass.ds(CH * (c + 2), CH)]).then_inc(idx_ready.sem, 1)
                if with_nodes:
                    wait(act, Q("hn_sum", p), i + 1)
                    nc.scalar.activation(stage[:, cslice(i)], ps[:, 5, 0:CN], ACT.Identity, bias=col(B_HN)
                                         ).then_inc(Q("hn_kept", p).sem, 1)
            pass_turns(act, mode, body)

        def bases_pe(pe):
            pe.wait_ge(S("counted"), 2)
            nc.tensor.matmul(ps[:, 4, 0:1], count_b, ones[:, 0:1], start=True, stop=True).then_inc(S("totals"), 1)
            pe.wait_ge(S("tiles_b"), 1)
            nc.tensor.matmul(ps[:, 5, 0:1], lower[:, :], tiny[:, 2:3], start=True, stop=True).then_inc(S("bases"), 1)
            pe.wait_ge(S("diag_ready"), 1)
            nc.tensor.matmul(ps[:, 6, 0:MASKB], lower[:, :], count_b, start=True, stop=False)
            nc.tensor.matmul(ps[:, 6, 0:MASKB], ones[:, :], diag, start=False, stop=True)
            for j in range(2):
                last = nc.tensor.matmul(ps[:, 7 - 3 * j, 0:T // 2], sel_blocks[:, :],
                                        tile_ge[:, j * (T // 2):(j + 1) * (T // 2)], start=True, stop=True)
            last.then_inc(S("places"), 1)

        def bases_dve(dve):
            step = chain(dve)
            dve.sem_inc(S("counted"), 1)
            dve.wait_ge(S("totals"), 2)
            step(nc.vector.tensor_scalar(tiny_i[:, 0:1], ps[:, 4, 0:1], float(P - 1), None, ALU.add))
            step(nc.vector.tensor_scalar(tiny_i[:, 1:2], tiny_i[:, 0:1], 7, None, ALU.logical_shift_right))
            nc.vector.tensor_copy(tiny[:, 2:3], tiny_i[:, 1:2]).then_inc(S("tiles_b"), 1)
            dve.wait_ge(S("bases"), 2)
            step(nc.vector.tensor_copy(tiny[:, 3:4], ps[:, 5, 0:1]))
            step(nc.vector.tensor_scalar(diag, ident[:, :], tiny[:, 3:4], float(P), ALU.mult, ALU.mult))
            nc.vector.tensor_scalar(tile_ge, tile_iota[:, :], tiny[:, 3:4], None, ALU.is_ge).then_inc(S("diag_ready"), 1)
            dve.wait_ge(S("places"), 1)
            for j in range(2):
                nc.vector.tensor_copy(block_of[1][:, j * (T // 2):(j + 1) * (T // 2)], ps[:, 7 - 3 * j, 0:T // 2])
            step(nc.vector.tensor_copy(base, ps[:, 6, 0:MASKB]))

        def places_dve(dve):
            step = chain(dve)
            a, b = scan[:, 0:EC].bitcast(I32), prod[:, 0:EC].bitcast(I32)
            step(nc.vector.tensor_scalar(a, pos1[:, 0:EC], -1.0, None, ALU.add))
            step(nc.vector.tensor_scalar(b, a, P - 1, None, ALU.bitwise_and))
            nc.vector.tensor_copy(row1[:, 0:EC], b)
            step(nc.vector.memset(row1[:, EC:T], -1.0))
            step(nc.vector.tensor_scalar(b, a, 7, None, ALU.arith_shift_right))
            nc.vector.tensor_copy(tile1[:, 0:EC], b)
            step(nc.vector.memset(tile1[:, EC:T], -1.0))

        def list1_dve(p, dve, i, h):
            if p == 0 and h == 0:
                blk = block_no[:, bass.ds(i, 1)]
                ranks = Steps(dve, "rank_steps", 4)
                ranks.chunk(i)
                ranks(nc.vector.tensor_scalar(mask, blk1[:, 0:EC], blk, None, ALU.is_equal, ALU.add,
                                              accum_out=count_b[:, bass.ds(i, 1)]))
                ranks(nc.vector.tensor_tensor_scan(scan, ones_row, mask, 0.0, ALU.mult, ALU.add))
                ranks(nc.vector.tensor_tensor(prod, scan, mask, ALU.mult))
                ranks(nc.vector.tensor_tensor(pos1[:, 0:EC], pos1[:, 0:EC], prod, ALU.add))
            if p == 1 and h == 0:
                places = Steps(dve, "place_steps", 2)
                places.chunk(i)
                places(nc.vector.tensor_scalar(prod, blk1[:, 0:EC], block_no[:, bass.ds(i, 1)],
                                               base[:, bass.ds(i, 1)], ALU.is_equal, ALU.mult))
                places(nc.vector.tensor_tensor(pos1[:, 0:EC], pos1[:, 0:EC], prod, ALU.add))

        def hot_cols_dve(p, dve, c, h, u):
            if u % 2:
                return
            m = u // 2
            turn = 2 * PASS_ITERS * (p - 2) + c
            if m == 0:
                wait(dve, S("built"), turn - 1)
            one_col = bass.ds(BUILD * turn + m, 1)
            last = nc.vector.tensor_scalar(hot_tile[h][:, m, :], tile_iota[:, 0:T], tile1[:, one_col], None,
                                           ALU.is_equal)
            for a, value in enumerate((hi1, lo1)):
                last = nc.vector.tensor_scalar(hot_row[h][:, m, a, :], tile_iota[:, 0:P], row1[:, one_col],
                                               value[:, one_col], ALU.is_equal, ALU.mult)
            if m == BUILD - 1:
                last.then_inc(S("hot_cols"), 1)

        def list1_pe(p, pe, c, h):
            turn = 2 * PASS_ITERS * (p - 2) + c
            pe.wait_ge(S("hot_cols"), turn + 1)
            for m in range(BUILD):
                for a in range(2):
                    first = isinstance(turn, int) and turn == 0 and m == 0 and a == 0
                    for j in range(2):
                        last = nc.tensor.matmul(ps[:, 6 + j, 0:T // 2], hot_row[h][:, m, a, :],
                                                hot_tile[h][:, m, j * (T // 2):(j + 1) * (T // 2)],
                                                start=first, stop=True, skip_group_check=True)
            last.then_inc(S("built"), 1)

        def unpack1_dve(dve):
            step = chain(dve)
            v, a, b = [big[:, k * T:(k + 1) * T] for k in range(3)]
            v_i, a_i, b_i = [t.bitcast(I32) for t in (v, a, b)]
            for j in range(2):
                last = nc.vector.tensor_scalar(v_i[:, j * (T // 2):(j + 1) * (T // 2)], ps[:, 6 + j, 0:T // 2],
                                               float(1 << LOW_BITS), None, ALU.mult)
            step(last)
            step(nc.vector.tensor_scalar(a_i, v_i, -1.0, 0.0, ALU.add, ALU.max))
            nc.vector.tensor_scalar(b, v_i, 0.0, float(P), ALU.is_equal, ALU.mult)
            nc.vector.memset(gather_idx[1][:, T:TP], 0)
            nc.vector.memset(local[1][:, T:TP], float(P))
            step(nc.vector.tensor_scalar(gather_idx[1][:, 0:T], a_i, 7, None, ALU.logical_shift_right))
            step(nc.vector.tensor_scalar(v_i, a_i, P - 1, None, ALU.bitwise_and))
            step(nc.vector.tensor_tensor(local[1][:, 0:T], v_i, b, ALU.add))

        def pass_pe(p, pe):
            k, mode = LISTS[p], MODES[p]
            if p == 1:
                bases_pe(pe)
            w = P if mode in ("fm", "edge") else P + 1
            hot_ready, summed, added = Q("weighted" if MODES[p] == "att" else "hot_ready", p), Q("summed", p), Q("added", p)

            def body(i, with_nodes):
                for h in range(2):
                    c = 2 * i + h
                    if mode == "edge":
                        blk = tile_blocks(pe, k, c)
                        wait(pe, hot_ready, c + 1)
                        for g in range(2):
                            wait(pe, Q("flip_copied", p), 2 * (c - 1) + g + 1)
                            for u in range(4):
                                last = nc.tensor.transpose(ps[:, 4 + g, u * P:(u + 1) * P],
                                                           onehot[:, h * CH + 4 * g + u, :], ident[:, :])
                            last.then_inc(Q("flipped", p).sem, 1)
                        for g in range(2):
                            wait(pe, Q("edge_act", p), 2 * (c - 1) + g + 1)
                            wait(pe, Q("flip_copied", p), 2 * c + g + 1)
                            for u in range(4):
                                s = h * CH + 4 * g + u
                                out = ps[:, 6 + g, u * P:(u + 1) * P]
                                wait(pe, row_landed[s], 16 * (PASS_ITERS * p + i + 1))
                                nc.tensor.matmul(out, ident[:, :], rows[:, s, 0:P], start=True, stop=False,
                                                 skip_group_check=True)
                                last = nc.tensor.matmul(out, ring_ohT[:, 4 * g + u, :],
                                                        q_nm[:, bass.ds(blk[4 * g + u] * P, P)],
                                                        start=False, stop=True, skip_group_check=True)
                            last.then_inc(Q("edge_pre", p).sem, 1)
                    elif mode != "att":
                        wait(pe, hot_ready, c + 1)
                    for g, tiles in groups(w):
                        if p in (2, 3) and tiles[-1] == CH - 1 and not (isinstance(c, int) and c == 0):
                            list1_pe(p, pe, c - 1, 1 - h)
                        wait(pe, added, CH * (c - 2) + tiles[-1] + 1)
                        if mode == "edge":
                            wait(pe, Q("edge_act", p), 2 * c + g + 1)
                        for u in tiles:
                            s = h * CH + u
                            if mode == "edge":
                                lhs, rhs = ring_e[:, s, :], onehot[:, s, :]
                            else:
                                wait(pe, row_landed[s], 16 * (PASS_ITERS * p + i + 1))
                                if mode == "fm":
                                    lhs, rhs = rows[:, s, 0:P], onehot[:, s, :]
                                elif mode == "nm":
                                    lhs, rhs = onehot[:, s, :], rows[:, s, 0:w]
                                else:
                                    wait(pe, hot_ready, CH * c + u + 1)
                                    lhs, rhs = ring_e[:, s, :], rows[:, s, 0:w]
                            nc.tensor.matmul(psum_sum(h, u, w), lhs, rhs, start=True, stop=True,
                                             skip_group_check=True).then_inc(summed.sem, 1)
                if with_nodes:
                    wait(pe, Q("hn_kept", p), i)
                    nc.tensor.matmul(ps[:, 5, 0:CN], w_hh[:, 2 * P:3 * P], x_fm[:, cslice(i)],
                                     start=True, stop=True).then_inc(Q("hn_sum", p).sem, 1)
            pass_turns(pe, mode, body)
            if p in (2, 3):
                list1_pe(p, pe, 2 * PASS_ITERS - 1, 1)

        def pass_dve(p, dve):
            k, mode = LISTS[p], MODES[p]
            w = P if mode in ("fm", "edge") else P + 1
            stride = P if mode in ("fm", "edge") else W
            hot_ready, summed, added = Q("weighted" if MODES[p] == "att" else "hot_ready", p), Q("summed", p), Q("added", p)
            nc.vector.memset(acc[:, :], 0.0).then_inc(Q("acc_zero", p).sem, 1)
            wait(dve, Q("acc_zero", p), 1)

            def hots(c, h):
                nc.vector.tensor_tensor(
                    onehot[:, h * CH:(h + 1) * CH, :],
                    iota[:, :].unsqueeze(1).to_broadcast([P, CH, P]),
                    local[k][:, bass.ds(CH * c, CH)].unsqueeze(2).to_broadcast([P, CH, P]),
                    ALU.is_equal).then_inc(hot_ready.sem, 1)

            if mode != "att":
                hots(0, 0)
            if p == 1:
                bases_dve(dve)
            if p == 2:
                places_dve(dve)

            last_of = {u: tiles[-1] for g, tiles in groups(w) for u in tiles}

            def add_sum(c, h, blk, u):
                if u == 0 or last_of[u] != last_of[u - 1]:
                    wait(dve, summed, CH * c + last_of[u] + 1)
                dst = acc[:, bass.ds(blk[u] * stride, w)]
                wait(dve, added, CH * c + u)
                nc.vector.tensor_tensor(dst, psum_sum(h, u, w), dst, ALU.add).then_inc(added.sem, 1)

            def body(i):
                for h in range(2):
                    c = 2 * i + h
                    blk = tile_blocks(dve, k, c)
                    if mode != "att":
                        hots(c + 1, 1 - h)
                        list1_dve(p, dve, i, h)
                        for u in range(CH):
                            add_sum(c, h, blk, u)
                            if p in (2, 3):
                                hot_cols_dve(p, dve, c, h, u)
                        continue
                    before = None if isinstance(c, int) and c == 0 else tile_blocks(dve, k, c - 1, "before")
                    for u in range(CH + 1):
                        if u < CH:
                            s = h * CH + u
                            wait(dve, Q("scaled", p), CH * c + u + 1)
                            nc.vector.scalar_tensor_tensor(
                                ring_e[:, s, :], u2_rows[:, bass.ds(blk[u] * P, P)], rows[:, s, 130:131],
                                onehot[:, s, :], ALU.mult, ALU.max).then_inc(Q("weighed", p).sem, 1)
                        if u > 0:
                            s = h * CH + u - 1
                            wait(dve, Q("weighed", p), CH * c + u)
                            nc.vector.scalar_tensor_tensor(
                                ring_e[:, s, :], iota[:, :], local[k][:, bass.ds(CH * c + u - 1, 1)],
                                ring_e[:, s, :], ALU.is_equal, ALU.mult).then_inc(hot_ready.sem, 1)
                            if before:
                                add_sum(c - 1, 1 - h, before, u - 1)
            turns(dve, PASS_ITERS, body)
            if mode == "att":
                blk = tile_blocks(dve, k, 2 * PASS_ITERS - 1)
                for u in range(CH):
                    add_sum(2 * PASS_ITERS - 1, 1, blk, u)

        def tslot(s):
            return ps[:, 4 + s, 0:CN]

        def flip_pe(tag, pe, src, c, s, ready):
            taken, done = (Q("flip_taken_gru", tag), Q("flip_done_gru", tag)) if isinstance(tag, int) else \
                (Count(S("flip_taken" + tag), 0), Count(S("flip_done" + tag), 0))
            wait(pe, ready, c + 1)
            wait(pe, taken, c - 1)
            for b in range(CB):
                last = nc.tensor.transpose(ps[:, 4 + s, b * P:(b + 1) * P], src[:, b * P:(b + 1) * P], ident[:, :])
            last.then_inc(done.sem, 1)

        def cut_dve(tag, dve, c, s, slot):
            wait(dve, S("flip_done" + tag), c - 1)
            nc.vector.tensor_copy(slot, x_nm[:, bslice(c), :].rearrange("p b f -> p (b f)")).then_inc(S("cut" + tag), 1)

        class Steps:
            def __init__(self, eng, name, per_chunk, base=0):
                self.eng, self.sem, self.per, self.c, self.n = eng, S(name), per_chunk, 0, 0
                self.base = base

            def chunk(self, c):
                self.c, self.n = c, 0

            def __call__(self, ins):
                self.n += 1
                ins.then_inc(self.sem, 1)
                self.eng.wait_ge(self.sem, self.c * self.per + self.n + self.base)

        chained = []

        def chain(dve):
            if not chained:
                chained.append(Steps(dve, "dve_chain", 0))
            return chained[0]

        def hold(eng):
            eng.sem_inc(S("held"), 1)

        def node_stats(n):
            return Count(S("node_stats"), 2 * CB * NC * n)

        def mean_var_dve(dve, c, s, sem):
            wait(dve, sem, 2 * CB * c + CB)
            hold(dve)
            for b in range(CB):
                nc.vector.bn_aggr(mv_chunk[:, s, b, :], st6[:, s, b, :]).then_inc(sem.sem, 1)

        def keep_mean_var_dve(dve, c, s, sem):
            wait(dve, sem, 2 * CB * (c + 1))
            nc.vector.tensor_copy(mv[:, bslice(c), :], mv_chunk[:, s, :, :])

        def stats_dve(dve, c, s, sem, added):
            first = isinstance(c, int) and c == 0
            if not first:
                mean_var_dve(dve, c - 1, 1 - s, sem)
            wait(dve, added, c + 1)
            hold(dve)
            for b in range(CB):
                nc.vector.bn_stats(st6[:, s, b, :], x_nm[:, bass.ds(c * CB + b, 1), :]
                                   .rearrange("p b f -> p (b f)")).then_inc(sem.sem, 1)
            if not first:
                keep_mean_var_dve(dve, c - 1, 1 - s, sem)

        def last_stats_dve(dve, sem):
            mean_var_dve(dve, NC - 1, 1, sem)
            keep_mean_var_dve(dve, NC - 1, 1, sem)

        def norm_dve(n, dve):
            one = chain(dve)
            one(nc.vector.tensor_scalar(small[:, 0, :], mv[:, :, 1], EPS, None, ALU.add))
            nc.vector.tensor_scalar(small[:, 2, :], mv[:, :, 0], -1.0, None, ALU.mult).then_inc(S("norm_var"), 1)
            dve.wait_ge(S("norm_var"), n + 1)
            dve.wait_ge(S("norm_std"), n + 1)
            one(nc.vector.reciprocal(small[:, 1, :], small[:, 1, :]))
            nc.vector.tensor_tensor(small[:, 3, :], small[:, 2, :], small[:, 1, :], ALU.mult).then_inc(S("norm_cols"), 1)

            def body(i):
                for s in range(CB):
                    b = i * 2 * CB + s
                    blk = x_nm[:, bass.ds(b, 1), :].rearrange("p b f -> p (b f)")
                    nc.vector.tensor_scalar(blk, blk, small[:, 2, bass.ds(b, 1)], small[:, 1, bass.ds(b, 1)],
                                            ALU.add, ALU.mult).then_inc(S("normed"), 1)
            turns(dve, NODE_ITERS, body)

        def norm_act(n, act):
            act.wait_ge(S("norm_var"), n + 1)
            nc.scalar.activation(small[:, 1, :], small[:, 0, :], ACT.Sqrt).then_inc(S("norm_std"), 1)
            act.wait_ge(S("norm_cols"), n + 1)

            def body(i):
                for s in range(CB):
                    b = i * 2 * CB + CB + s
                    blk = x_nm[:, bass.ds(b, 1), :].rearrange("p b f -> p (b f)")
                    nc.scalar.activation(blk, blk, ACT.Identity, bias=small[:, 3, bass.ds(b, 1)],
                                         scale=small[:, 1, bass.ds(b, 1)]).then_inc(S("act_normed"), 1)
            turns(act, NODE_ITERS, body)

        def store_norm_sp(sp, dst):
            def body(i):
                sp.wait_ge(S("normed"), (i + 1) * CB)
                sp.wait_ge(S("act_normed"), (i + 1) * CB)
                sp.dma_start(dst[bass.ds(i * 2 * CN, 2 * CN), 0:P].rearrange("(b p) f -> p b f", p=P),
                             x_nm[:, bass.ds(i * 2 * CB, 2 * CB), :]).then_inc(S("norm_stored"), 16)
            turns(sp, NODE_ITERS, body)
            sp.wait_ge(S("norm_stored"), 16 * NODE_ITERS)

        def safe_inverse_dve(tag, dve):
            one = chain(dve)
            one(nc.vector.tensor_copy(small[:, 0, :], acc_nm[:, :, P]))
            one(nc.vector.tensor_scalar(small[:, 2, :], small[:, 0, :], 0.0, None, ALU.is_gt))
            one(nc.vector.tensor_tensor(small[:, 1, :], small[:, 0, :], small[:, 2, :], ALU.mult))
            one(nc.vector.tensor_scalar(small[:, 3, :], small[:, 2, :], -1.0, 1.0, ALU.mult, ALU.add))
            one(nc.vector.tensor_tensor(small[:, 1, :], small[:, 1, :], small[:, 3, :], ALU.add))
            one(nc.vector.reciprocal(small[:, 1, :], small[:, 1, :]))
            one(nc.vector.tensor_tensor(small[:, 1, :], small[:, 1, :], small[:, 2, :], ALU.mult))

        def batch_dve(n_done, dve, src, gamma, beta, scale, shift):
            one = chain(dve)

            for n in range(NST):
                last = nc.vector.bn_stats(bst[:, n, :], src[:, n * ST:(n + 1) * ST])
            one(last)
            one(nc.vector.bn_aggr(bmv[:, :], bst[:, :, :].rearrange("p n s -> p (n s)")))
            nc.vector.tensor_scalar(bmv[:, 1:2], bmv[:, 1:2], EPS, None, ALU.add).then_inc(S("batch_var"), 1)
            dve.wait_ge(S("batch_std"), n_done + 1)
            one(nc.vector.reciprocal(scale, scale))
            one(nc.vector.tensor_tensor(scale, scale, gamma, ALU.mult))
            one(nc.vector.tensor_tensor(shift, bmv[:, 0:1], scale, ALU.mult))
            one(nc.vector.tensor_tensor(shift, beta, shift, ALU.subtract))

        def batch_act(n_done, act, scale):
            act.wait_ge(S("batch_var"), n_done + 1)
            nc.scalar.activation(scale, bmv[:, 1:2], ACT.Sqrt).then_inc(S("batch_std"), 1)

        def vec(ap):
            return ap.rearrange("(p a) -> p a", a=1)

        def tmp(j, s):
            return big[:, NP + (2 * j + s) * CN:NP + (2 * j + s + 1) * CN]

        def tmp_acc(j, s):
            return acc[:, (2 * j + s) * CN:(2 * j + s + 1) * CN]

        block = ctx.enter_context(nc.Block())

        @block.sync
        def _(sp):
            sp.wait_ge(S("edges_padded"), 3)
            for view, name, off in ((dst_e, "dst", 0), (src_e, "src", 0), (next_e, "dst", 1)):
                full = E_FULL * EC + off
                sp.dma_start(view[0:E_FULL, :], d[name][off:full].rearrange("(p c) -> p c", c=EC))\
                    .then_inc(S("edges_in"), 16)
                sp.dma_start(view[E_FULL:E_FULL + 1, 0:E - full], d[name][full:E].rearrange("(p c) -> p c", p=1))\
                    .then_inc(S("edges_in"), 16)
            sp.dma_start(raw_w[:, 0, :], d["L0_gnn_lin_w"]).then_inc(S("weights_in"), 16)
            sp.dma_start(raw_w[:, 1:4, :], d["L0_gnn_w_ih"].rearrange("(m p) f -> p m f", p=P)).then_inc(S("weights_in"), 16)
            sp.dma_start(raw_w[:, 4:7, :], d["L0_gnn_w_hh"].rearrange("(m p) f -> p m f", p=P)).then_inc(S("weights_in"), 16)
            sp.dma_start(raw_w[:, 7:10, :], d["L0_gnn_weight"].rearrange("m p f -> p m f")).then_inc(S("weights_in"), 16)
            sp.dma_start(w_hyper[:, :], d["L1_gnn_W"]).then_inc(S("weights_in"), 16)
            for j, ap in ((LIN_B, d["L0_gnn_lin_b"]), (13, d["L0_gnn_b_ih"][0:P]), (14, d["L0_gnn_b_ih"][P:2 * P]),
                          (B_IN, d["L0_gnn_b_ih"][2 * P:3 * P]), (15, d["L0_gnn_b_hh"][0:P]),
                          (16, d["L0_gnn_b_hh"][P:2 * P]), (B_HN, d["L0_gnn_b_hh"][2 * P:3 * P]),
                          (HY_B, d["L1_gnn_b"]), (HY_G, d["L1_gnn_gamma"]), (HY_BE, d["L1_gnn_beta"]),
                          (AT_G, d["L2_gnn_gamma"]), (AT_BE, d["L2_gnn_beta"]), (N1_B, d["L3_gnn_bn1"])):
                sp.dma_start(col(j), vec(ap)).then_inc(S("vectors_in"), 16)
            sp.dma_start(col(E2_B), vec(d["L3_gnn_be2"])).then_inc(S("vectors_in"), 16)
            sp.wait_ge(S("x_zero"), 1)
            sp.dma_start(x_nm[:, 0:NB - 1, :], d["x"][0:(NB - 1) * P, :].rearrange("(b p) f -> p b f", p=P)).then_inc(S("x_in"), 16)
            sp.dma_start(x_nm[0:N - (NB - 1) * P, NB - 1, :], d["x"][(NB - 1) * P:N, :]).then_inc(S("x_in"), 16)
            sp.wait_ge(S("consts"), 1)
            sp.dma_start(table[3][:, P:P + 1].rearrange("(b p) f -> p (b f)", p=P), ones[:, 0:NBP],
                         allow_slow_non_contiguous=True).then_inc(S("const_columns"), 16)
            sp.dma_start(table[4][0:N, P:P + 1], d["L1_gnn_hyperedge_weight"].rearrange("(n a) -> n a", a=1),
                         allow_slow_non_contiguous=True).then_inc(S("const_columns"), 16)
            sp.wait_ge(S("packed_ready"), 1)
            sp.dma_start(edges.rearrange("(p c) a -> p (c a)", c=EC), packed).then_inc(S("edges_stored"), 16)
            def h0_out(i):
                sp.wait_ge(S("h0_staged"), 2 * i + 2)
                sp.dma_start(table[0][bass.ds(i * 2 * CN, 2 * CN), :].rearrange("(b p) f -> p b f", p=P),
                             stage_rows[:, bass.ds(i * 2 * CB, 2 * CB), :]).then_inc(S("h0_stored"), 16)
            turns(sp, NODE_ITERS, h0_out)
            sp.wait_ge(S("h0_stored"), 16 * NODE_ITERS)
            sp.wait_ge(S("const_columns"), 32)
            end_stage(sp, nc.sync)
            for p in range(GRU_LAYERS):
                end_stage(sp, nc.sync)
                if p < GRU_LAYERS - 1:
                    def rows_out(i, p=p):
                        wait(sp, Q("flip_taken_gru", p), 2 * i + 2)
                        sp.dma_start(table[p + 1][bass.ds(i * 2 * CN, 2 * CN), :].rearrange("(b p) f -> p b f", p=P),
                                     stage_rows[:, bass.ds(i * 2 * CB, 2 * CB), :]).then_inc(Q("stored_gru", p).sem, 16)
                    turns(sp, NODE_ITERS, rows_out)
                    wait(sp, Q("stored_gru", p), 16 * NODE_ITERS)
                end_stage(sp, nc.sync)
            for ap, src in ((w_att[:, 0:P], d["L2_gnn_kernel"]), (w_att[:, P:2 * P], d["L2_gnn_kernel1"]),
                            (w_att[:, 2 * P:3 * P], d["L2_gnn_kernel2"]),
                            (w_e1[:, 0:P], d["L3_gnn_We1"][0:P, :]), (w_e1[:, P:2 * P], d["L3_gnn_We1"][P:2 * P, :]),
                            (w_e2, d["L3_gnn_We2"]), (w_n1[:, 0:P], d["L3_gnn_Wn1"][0:P, :]),
                            (w_n1[:, P:2 * P], d["L3_gnn_Wn1"][P:2 * P, :]), (w_n2, d["L3_gnn_Wn2"]),
                            (be1_rows, d["L3_gnn_be1"].rearrange("(a n) -> a n", a=1).to_broadcast([P, P]))):
                sp.dma_start(ap, src).then_inc(S("late_weights"), 16)
            store_norm_sp(sp, table[3])
            sp.wait_ge(S("late_weights"), 160)
            end_stage(sp, nc.sync)
            end_stage(sp, nc.sync)
            sp.wait_ge(S("degree_ready"), 1)
            sp.dma_start(degree_row.rearrange("(b p) a -> p (b a)", p=P), small[:, 4, :],
                         allow_slow_non_contiguous=True).then_inc(S("degree_out"), 16)

            def hyper_out(i):
                sp.wait_ge(S("hyper_scaled"), (i + 1) * 2 * CB)
                sp.dma_start(table[4][bass.ds(i * 2 * CN, 2 * CN), 0:P].rearrange("(b p) f -> p b f", p=P),
                             stage_rows[:, bass.ds(i * 2 * CB, 2 * CB), :]).then_inc(S("hyper_stored"), 16)
            turns(sp, NODE_ITERS, hyper_out)
            sp.wait_ge(S("hyper_stored"), 16 * NODE_ITERS)
            sp.wait_ge(S("degree_out"), 16)
            end_stage(sp, nc.sync)
            end_stage(sp, nc.sync)
            end_stage(sp, nc.sync)
            end_stage(sp, nc.sync)
            end_stage(sp, nc.sync)
            end_stage(sp, nc.sync)
            sp.wait_ge(S("ones_cols"), 1)

            def att_out(i):
                sp.wait_ge(S("s_taken"), 2 * i + 2)
                sp.wait_ge(S("score_cols"), 2 * i + 2)
                sp.dma_start(table[5][bass.ds(i * 2 * CN, 2 * CN), :].rearrange("(b p) f -> p b f", p=P),
                             stage_nm[:, bass.ds(i * 2 * CB, 2 * CB), 0:P + 3]).then_inc(S("att_stored"), 16)
            turns(sp, NODE_ITERS, att_out)
            sp.wait_ge(S("att_stored"), 16 * NODE_ITERS)
            end_stage(sp, nc.sync)
            end_stage(sp, nc.sync)
            sp.dma_start(bn2_rows, d["L3_gnn_bn2"].rearrange("(a n) -> a n", a=1).to_broadcast([P, P]))\
                .then_inc(S("bn2_in"), 16)
            sp.wait_ge(S("bn2_in"), 16)
            end_stage(sp, nc.sync)
            end_stage(sp, nc.sync)

            def edge_out(i):
                sp.wait_ge(S("p_staged"), 2 * i + 2)
                sp.dma_start(table[6][bass.ds(i * 2 * CN, 2 * CN), :].rearrange("(b p) f -> p b f", p=P),
                             stage_rows[:, bass.ds(i * 2 * CB, 2 * CB), :]).then_inc(S("p_stored"), 16)
            turns(sp, NODE_ITERS, edge_out)
            sp.wait_ge(S("p_stored"), 16 * NODE_ITERS)
            end_stage(sp, nc.sync)
            end_stage(sp, nc.sync)
            sp.dma_start(stage[0:1, 0:NP], degree_row.rearrange("(a n) o -> a (n o)", a=1)).then_inc(S("degree_in"), 16)
            end_stage(sp, nc.sync)
            full = NB - 1
            for n in range(full // (2 * CB)):
                sp.wait_ge(S("normed"), 3 * NBP // 2 + (n + 1) * CB)
                sp.wait_ge(S("act_normed"), 3 * NBP // 2 + (n + 1) * CB)
                sp.dma_start(d["out"][n * 2 * CN:(n + 1) * 2 * CN, :].rearrange("(b p) f -> p b f", p=P),
                             x_nm[:, n * 2 * CB:(n + 1) * 2 * CB, :]).then_inc(S("out_stored"), 16)
            sp.wait_ge(S("normed"), 3 * NBP // 2 + full // 2 + 1)
            sp.dma_start(d["out"][full * P:N, :], x_nm[0:N - full * P, full, :]).then_inc(S("out_stored"), 16)
            sp.wait_ge(S("out_stored"), 16 * (full // (2 * CB) + 1))
            end_stage(sp, nc.sync)

        @block.gpsimd
        def _(pool):
            step = Steps(pool, "const_steps", 0)
            step(nc.gpsimd.memset(ones[:, :], 1.0))
            step(nc.gpsimd.memset(ident[:, :], 0.0))
            step(nc.gpsimd.affine_select(out=ident[:, :], in_=ident[:, :], compare_op=ALU.not_equal, fill=1.0,
                                         base=0, pattern=[[-1, P]], channel_multiplier=1))
            step(nc.gpsimd.affine_select(out=lower[:, :], in_=ones[:, :], compare_op=ALU.is_ge, fill=0.0,
                                         base=-1, pattern=[[1, P]], channel_multiplier=-1))
            step(nc.gpsimd.affine_select(out=sel_blocks[:, :], in_=ones[:, :], compare_op=ALU.is_ge, fill=0.0,
                                         base=-1, pattern=[[0, P]], channel_multiplier=1))
            step(nc.gpsimd.affine_select(out=sel_blocks[:, :], in_=sel_blocks[:, :], compare_op=ALU.is_ge, fill=0.0,
                                         base=NB - 1, pattern=[[0, P]], channel_multiplier=-1))
            step(nc.gpsimd.affine_select(out=step_down[:, :], in_=ident[:, :], compare_op=ALU.not_equal, fill=-1.0,
                                         base=1, pattern=[[-1, P]], channel_multiplier=1))
            step(nc.gpsimd.iota(iota[:, :], pattern=[[1, P]], base=0, channel_multiplier=0,
                                allow_small_or_imprecise_dtypes=True))
            step(nc.gpsimd.iota(tile_iota[:, :], pattern=[[1, TP]], base=0, channel_multiplier=0,
                                allow_small_or_imprecise_dtypes=True))
            step(nc.gpsimd.iota(block_no[:, :], pattern=[[1, PASS_ITERS]], base=0, channel_multiplier=0,
                                allow_small_or_imprecise_dtypes=True))
            step(nc.gpsimd.memset(block_no[:, NB:PASS_ITERS], 200.0))
            step(nc.gpsimd.affine_select(out=real_block[:, :], in_=ones[:, 0:1], compare_op=ALU.is_ge, fill=0.0,
                                         base=NB - 1, pattern=[[0, 1]], channel_multiplier=-1))
            step(nc.gpsimd.iota(pair_blk[:, :], pattern=[[P, TG]], base=0, channel_multiplier=1,
                                allow_small_or_imprecise_dtypes=True))
            nc.gpsimd.memset(rows[:, :, :], 0.0).then_inc(S("consts"), 1)
            pool.wait_ge(S("edges_stored"), 16)
            pool.wait_ge(S("flag_ready"), 1)
            with pool.If(pool.value_load(flag[0:1, 0:1], min_val=0, max_val=E)):
                def scatter(i):
                    for h in range(2):
                        pool.wait_ge(S("ring_filled"), 2 * i + h + 1)
                        pool.sem_inc(rows_opened, 1)
                        for u in range(SC):
                            s = h * SC + u
                            nc.gpsimd.indirect_dma_start(
                                edges, bass.IndirectOffsetOnAxis(idx_ring[:, s:s + 1], 0),
                                val_ring[:, s:s + 1], None).then_inc(S("scattered" + str(h)), 16)
                with pool.Fori(0, SCATTER_ITERS) as i:
                    scatter(i)
                for h in range(2):
                    pool.wait_ge(S("scattered" + str(h)), 16 * SC * SCATTER_ITERS)
            pool.wait_ge(S("pairs_ready"), 1)
            for g in range(TG):
                nc.gpsimd.indirect_dma_start(pair_rows[:, g, :], None, edges.rearrange("(t e) a -> t (e a)", e=P),
                                             bass.IndirectOffsetOnAxis(pair_idx[:, g:g + 1], 0)
                                             ).then_inc(S("pairs_in"), 16)
            end_stage(pool, nc.gpsimd)
            follow = [1, 1, 1 + 1, 1, 5, 3, 2]
            for p in range(7):
                pass_pool(p, pool)
                end_stage(pool, nc.gpsimd)
                for _ in range(follow[p]):
                    end_stage(pool, nc.gpsimd)

        @block.scalar
        def _(act):
            act.wait_ge(S("w_flipped"), 1)
            nc.scalar.copy(w_lin[:, :], ps[:, 5, 0:P])
            nc.scalar.copy(tr_w[:, 0:3, :].rearrange("p m f -> p (m f)"), ps[:, 5, P:4 * P])
            nc.scalar.copy(w_hh[:, :], ps[:, 6, 0:3 * P])
            nc.scalar.copy(tr_w[:, 3, :], ps[:, 6, 3 * P:4 * P])
            nc.scalar.copy(tr_w[:, 4:6, :].rearrange("p m f -> p (m f)"), ps[:, 7, 0:2 * P]).then_inc(S("w_copied"), 1)
            act.wait_ge(S("w_combined"), 1)
            for l in range(GRU_LAYERS):
                last = nc.scalar.copy(w_comb[:, l, :], ps[:, 1 + l, 0:3 * P])
            last.then_inc(S("w_comb_copied"), 1)
            act.wait_ge(S("x_in"), 32)
            act.wait_ge(S("vectors_in"), 16 * 14)

            def h0_fm(c, s):
                act.wait_ge(S("h0_product"), c + 1)
                wait(act, S("h0_rows"), c - 1)
                nc.scalar.activation(tmp(2, s), ps[:, s, 0:CN], ACT.Identity, bias=col(LIN_B)).then_inc(S("h0_ready"), 1)
                act.wait_ge(S("h0_ready"), c + 1)
                nc.scalar.copy(x_fm[:, cslice(c)], tmp(2, s)).then_inc(S("h0_kept"), 1)

            def h0_nm(c, s):
                act.wait_ge(S("h0_rows"), c + 1)
                nc.scalar.copy(stage_rows[:, bslice(c), :].rearrange("p b f -> p (b f)"), ps[:, 6 + s, 0:CN])\
                    .then_inc(S("h0_staged"), 1)

            def h0_flipped(c, s):
                act.wait_ge(S("flip_done_h0x"), c + 1)
                wait(act, S("h0_product"), c - 1)
                nc.scalar.copy(tmp(1, s), tslot(s)).then_inc(S("flip_taken_h0x"), 1)

            def h0(i):
                for s in range(2):
                    c = 2 * i + s
                    known = isinstance(i, int)
                    wait(act, S("flip_done_h0x"), c - 1)
                    nc.scalar.copy(tmp(0, s), x_nm[:, bslice(c), :].rearrange("p b f -> p (b f)")).then_inc(S("cut_h0x"), 1)
                    if not known or c >= 1:
                        h0_flipped(c - 1, 1 - s)
                    if not known or c >= 2:
                        h0_fm(c - 2, s)
                    if not known or c >= 3:
                        h0_nm(c - 3, 1 - s)
            turns(act, NODE_ITERS, h0, peeled=2)
            h0_flipped(NC - 1, 1)
            h0_fm(NC - 2, 0)
            h0_nm(NC - 3, 1)
            h0_fm(NC - 1, 1)
            h0_nm(NC - 2, 0)
            h0_nm(NC - 1, 1)
            act.wait_ge(S("flag_ready"), 1)
            with act.If(act.value_load(flag[0:1, 0:1], min_val=0, max_val=E)):
                act.wait_ge(S("addr_ready"), 1)

                def ring(i):
                    for h in range(2):
                        wait(act, S("scattered" + str(h)), 16 * SC * i)
                        c = 2 * i + h
                        nc.scalar.copy(idx_ring[:, h * SC:(h + 1) * SC], slot_addr[:, bass.ds(SC * c, SC)])\
                            .then_inc(S("ring_idx"), 1)
                        act.wait_ge(S("ring_idx"), c + 1)
                        act.sem_inc(S("ring_half"), 1)
                turns(act, SCATTER_ITERS, ring)
            end_stage(act, nc.scalar)

            for p in range(GRU_LAYERS):
                pass_act(p, act)
                end_stage(act, nc.scalar)

                def keep(c, s, p=p):
                    wait(act, Q("h_ready", p), c + 1)
                    nc.scalar.copy(x_fm[:, cslice(c)], tmp(6, s)).then_inc(Q("h_kept", p).sem, 1)
                    wait(act, Q("flip_done_gru", p), c + 1)
                    nc.scalar.copy(stage_rows[:, bslice(c), :].rearrange("p b f -> p (b f)"),
                                   tslot(s)).then_inc(Q("flip_taken_gru", p).sem, 1)

                def gates_all(i, p=p):
                    for s in range(2):
                        c = 2 * i + s
                        wait(act, Q("rz_ready", p), c + 1)
                        wait(act, Q("n_in", p), c - 1)
                        nc.scalar.activation(tmp(0, s), ps[:, s, 0:CN], ACT.Sigmoid, bias=col(B_R)).then_inc(Q("r_ready", p).sem, 1)
                        wait(act, Q("h_ready", p), c - 1)
                        nc.scalar.activation(tmp(1, s), ps[:, s, CN:2 * CN], ACT.Sigmoid, bias=col(B_Z)).then_inc(Q("z_ready", p).sem, 1)
                        wait(act, Q("n_in", p), c + 1)
                        nc.scalar.activation(tmp(3, s), tmp(2, s), ACT.Tanh, bias=col(B_IN)).then_inc(Q("n_ready", p).sem, 1)
                        if p < GRU_LAYERS - 1 and (not isinstance(i, int) or c >= 2):
                            keep(c - 2, s)
                turns(act, NODE_ITERS, gates_all, peeled=2)
                if p < GRU_LAYERS - 1:
                    keep(NC - 2, 0)
                    keep(NC - 1, 1)
                end_stage(act, nc.scalar)
            norm_act(0, act)
            end_stage(act, nc.scalar)
            pass_act(3, act)
            end_stage(act, nc.scalar)
            act.wait_ge(S("inverse_done_b"), 1)

            def hyper_scale(i):
                for s in range(2 * CB):
                    b = i * 2 * CB + s
                    nc.scalar.activation(stage_rows[:, bass.ds(b, 1), :].rearrange("p b f -> p (b f)"),
                                         acc_nm[:, bass.ds(b, 1), 0:P].rearrange("p b f -> p (b f)"),
                                         ACT.Copy, scale=small[:, 1, bass.ds(b, 1)]).then_inc(S("hyper_scaled"), 1)
            turns(act, NODE_ITERS, hyper_scale)
            end_stage(act, nc.scalar)
            pass_act(4, act)
            end_stage(act, nc.scalar)

            def product_out(c, s):
                act.wait_ge(S("hy_product"), c + 1)
                nc.scalar.activation(big[:, cslice(c)], ps[:, s, 0:CN], ACT.Identity, bias=col(HY_B))\
                    .then_inc(S("hy_out"), 1)

            def hyper_product(i):
                for s in range(2):
                    c = 2 * i + s
                    act.wait_ge(S("flip_done_hy"), c + 1)
                    wait(act, S("hy_product"), c - 1)
                    nc.scalar.copy(tmp(1, s), tslot(s)).then_inc(S("flip_taken_hy"), 1)
                    if not (isinstance(c, int) and c == 0):
                        product_out(c - 1, 1 - s)
            turns(act, NODE_ITERS, hyper_product)
            product_out(NC - 1, 1)
            batch_act(0, act, col(SCALE))
            end_stage(act, nc.scalar)

            def hyper_relu(i):
                for s in range(2):
                    c = 2 * i + s
                    wait(act, S("flip_done_hr"), c - 1)
                    nc.scalar.activation(tmp(0, s), big[:, cslice(c)], ACT.Relu,
                                         bias=col(SHIFT), scale=col(SCALE)).then_inc(S("hy_relu"), 1)
            turns(act, NODE_ITERS, hyper_relu)
            end_stage(act, nc.scalar)
            norm_act(1, act)
            end_stage(act, nc.scalar)

            def copy_fm(tag):
                def body(i):
                    for s in range(2):
                        c = 2 * i + s
                        act.wait_ge(S("flip_done" + tag), c + 1)
                        nc.scalar.copy(x_fm[:, cslice(c)], tslot(s)).then_inc(S("flip_taken" + tag), 1)
                turns(act, NODE_ITERS, body)

            copy_fm("_x2")
            batch_act(1, act, col(SCALE))
            end_stage(act, nc.scalar)

            def exponentials(c, s):
                act.wait_ge(S("act_sc"), 2 * c + 2)
                nc.scalar.activation(stage_nm[:, bslice(c), P + 1], small[:, 4, bslice(c)], ACT.Exp)
                nc.scalar.activation(stage_nm[:, bslice(c), P + 2], small[:, 4, bslice(c)], ACT.Exp, scale=0.01)\
                    .then_inc(S("score_cols"), 1)
                nc.scalar.activation(u1_rows[:, cslice(c)], tmp_acc(3, s), ACT.Exp)
                nc.scalar.activation(u2_rows[:, cslice(c)], tmp_acc(3, s), ACT.Exp, scale=0.01)\
                    .then_inc(S("act_exp"), 1)

            def scores(i):
                for s in range(2):
                    c = 2 * i + s
                    act.wait_ge(S("s_ready"), c + 1)
                    wait(act, S("act_exp"), c - 1)
                    nc.scalar.activation(tmp_acc(3, s), ps[:, 2 + s, 0:CN], ACT.Tanh).then_inc(S("act_sc"), 1)
                    nc.scalar.activation(small[:, 4, bslice(c)], ps[:, 2 + s, CN:CN + CB], ACT.Tanh).then_inc(S("act_sc"), 1)
                    nc.scalar.copy(stage_nm[:, bslice(c), 0:P],
                                   tslot(s).rearrange("p (b f) -> p b f", f=P)).then_inc(S("s_taken"), 1)
                    if not (isinstance(c, int) and c == 0):
                        exponentials(c - 1, 1 - s)
            turns(act, NODE_ITERS, scores)
            exponentials(NC - 1, 1)
            end_stage(act, nc.scalar)
            pass_act(5, act)
            end_stage(act, nc.scalar)

            def att_relu(i):
                for s in range(2 * CB):
                    b = i * 2 * CB + s
                    if s == 0 and not isinstance(i, int):
                        act.wait_ge(S("at_added"), 2 * i)
                    if s == 0 and isinstance(i, int):
                        act.wait_ge(S("inverse_done_at"), 1)
                    nc.scalar.activation(x_fm[:, s * P:(s + 1) * P], acc_nm[:, bass.ds(b, 1), 0:P]
                                         .rearrange("p b f -> p (b f)"), ACT.Relu,
                                         scale=small[:, 1, bass.ds(b, 1)]).then_inc(S("at_relu"), 1)
            turns(act, NODE_ITERS, att_relu)
            end_stage(act, nc.scalar)
            norm_act(2, act)
            act.wait_ge(S("e2_flipped"), 1)
            nc.scalar.copy(tmp(0, 0)[:, 0:P], ps[:, 0, 0:P]).then_inc(S("e2_copied"), 1)
            act.wait_ge(S("e2_combined"), 1)
            nc.scalar.copy(w_e2, ps[:, 1, 0:P])
            nc.scalar.copy(row0[:, 0:P], ps[0:1, 1, P:2 * P])
            end_stage(act, nc.scalar)

            def p_rows(c, s):
                act.wait_ge(S("pq_ready"), c + 1)
                nc.scalar.copy(stage_rows[:, bslice(c), :],
                               ps[:, s, :].rearrange("p (b h f) -> p b h f", b=CB, h=2)[:, :, 0, :]
                               ).then_inc(S("p_staged"), 1)

            def edge_halves(i):
                for s in range(2):
                    c = 2 * i + s
                    act.wait_ge(S("flip_done_x3"), c + 1)
                    wait(act, S("q_taken"), c - 1)
                    nc.scalar.copy(tmp(1, s), tslot(s)).then_inc(S("flip_taken_x3"), 1)
                    if not (isinstance(c, int) and c == 0):
                        p_rows(c - 1, 1 - s)
            turns(act, NODE_ITERS, edge_halves)
            p_rows(NC - 1, 1)
            end_stage(act, nc.scalar)
            pass_act(6, act)
            end_stage(act, nc.scalar)

            def node_mlp(i):
                for s in range(2):
                    c = 2 * i + s
                    act.wait_ge(S("hid_ready"), c + 1)
                    wait(act, S("mesh_ready"), c - 1)
                    nc.scalar.activation(tmp(1, s), ps[:, 2 + s, 0:CN], ACT.Relu, bias=col(N1_B)).then_inc(S("hid_copied"), 1)
            turns(act, NODE_ITERS, node_mlp)
            end_stage(act, nc.scalar)
            norm_act(3, act)
            end_stage(act, nc.scalar)

        @block.tensor
        def _(pe):
            pe.wait_ge(S("consts"), 1)
            pe.wait_ge(S("weights_in"), 80)
            for j in range(10):
                last = nc.tensor.transpose(ps[:, 5 + j // 4, (j % 4) * P:(j % 4 + 1) * P], raw_w[:, j, :], ident[:, :])
            last.then_inc(S("w_flipped"), 1)
            pe.wait_ge(S("w_copied"), 1)
            for l in range(GRU_LAYERS):
                last = nc.tensor.matmul(ps[:, 1 + l, 0:3 * P], tr_w[:, 3 + l, :],
                                        tr_w[:, 0:3, :].rearrange("p m f -> p (m f)"), start=True, stop=True)
            last.then_inc(S("w_combined"), 1)

            def h0_product(c, s):
                pe.wait_ge(S("flip_taken_h0x"), c + 1)
                wait(pe, S("h0_ready"), c - 1)
                if isinstance(c, int) and c < 2:
                    pe.wait_ge(S("w_comb_copied"), 1)
                nc.tensor.matmul(ps[:, s, 0:CN], w_lin[:, :], tmp(1, s), start=True, stop=True)\
                    .then_inc(S("h0_product"), 1)

            def h0_rows(c, s):
                pe.wait_ge(S("h0_kept"), c + 1)
                wait(pe, S("h0_staged"), c - 1)
                for b in range(CB):
                    last = nc.tensor.transpose(ps[:, 6 + s, b * P:(b + 1) * P], tmp(2, s)[:, b * P:(b + 1) * P],
                                               ident[:, :])
                last.then_inc(S("h0_rows"), 1)

            def h0(i):
                for s in range(2):
                    c = 2 * i + s
                    flip_pe("_h0x", pe, tmp(0, s), c, s, S("cut_h0x"))
                    if not (isinstance(i, int) and c == 0):
                        h0_product(c - 1, 1 - s)
                    if not (isinstance(i, int) and i == 0):
                        h0_rows(c - 2, s)
            for i in range(2):
                h0(i)
            with pe.Fori(2, H0_FIRST) as i:
                h0(i)

            pe.wait_ge(S("counted"), 1)
            nc.tensor.matmul(ps[:, 2, 0:1], count_b, ones[:, 0:1], start=True, stop=True)
            nc.tensor.matmul(ps[:, 2, 1:2], ones[:, :], tiny[:, 0:1], start=True, stop=True).then_inc(S("totals"), 1)
            pe.wait_ge(S("tot_copied"), 1)
            nc.tensor.matmul(ps[:, 2, 2:3], lower[:, :], tiny[:, 1:2], start=True, stop=True).then_inc(S("bases"), 1)
            pe.wait_ge(S("flag_ready"), 1)
            with pe.If(pe.value_load(flag[0:1, 0:1], min_val=0, max_val=E)):
                pe.wait_ge(S("diag0_ready"), 1)
                nc.tensor.matmul(ps[:, 3, 0:MASKB], lower[:, :], count_b, start=True, stop=False)
                nc.tensor.matmul(ps[:, 3, 0:MASKB], ones[:, :], diag, start=False, stop=True).then_inc(S("places0"), 1)
            pe.wait_ge(S("pair_cols"), 1)
            nc.tensor.matmul(ps[:, 2, 3:4], lower[:, :], tiny[:, 5:6], start=True, stop=True).then_inc(S("pair_sums"), 1)
            pe.wait_ge(S("pair_cols"), 2)
            nc.tensor.matmul(ps[:, 2, 4:5], step_down[:, :], tiny[:, 7:8], start=True, stop=True).then_inc(S("pair_sums"), 1)
            pe.wait_ge(S("pair_cols"), 3)
            for g in range(TG):
                last = nc.tensor.matmul(ps[:, 3, T // 2 + 2 * g:T // 2 + 2 * g + 2], tile_ge[:, g * P:(g + 1) * P],
                                        tiny[:, 8:10], start=True, stop=True)
            last.then_inc(S("pair_sums"), 1)
            pe.wait_ge(S("pairs_ready"), 2)
            for j in range(2):
                last = nc.tensor.matmul(ps[:, 2 + j, 0:T // 2], sel_blocks[:, :],
                                        tile_ge[:, j * (T // 2):(j + 1) * (T // 2)], start=True, stop=True)
            last.then_inc(S("pair_sums"), 1)

            with pe.Fori(H0_FIRST, NODE_ITERS) as i:
                h0(i)
            h0_product(NC - 1, 1)
            h0_rows(NC - 2, 0)
            h0_rows(NC - 1, 1)
            pe.wait_ge(S("h0_staged"), NC)
            pe.wait_ge(S("pair_values"), 1)
            for n, values in enumerate((pair_f, pair_src)):
                for g in range(TG):
                    last = nc.tensor.transpose(ps[:, (0, 6)[n] + g // 4, (g % 4) * P:(g % 4 + 1) * P],
                                               values[:, g, :], ident[:, :])
            last.then_inc(S("pair_flipped"), 1)
            end_stage(pe, nc.tensor)

            for p in range(GRU_LAYERS):
                pass_pe(p, pe)
                end_stage(pe, nc.tensor)

                def flip_new(c, s, p=p):
                    flip_pe(p, pe, tmp(6, s), c, s, Q("h_ready", p))

                def gru(i, p=p):
                    for s in range(2):
                        c = 2 * i + s
                        wait(pe, Q("z_ready", p), c - 1)
                        for j in range(2):
                            nc.tensor.matmul(ps[:, s, j * CN:(j + 1) * CN], w_comb[:, p, j * P:(j + 1) * P],
                                             acc[:, cslice(c)], start=True, stop=False)
                            last = nc.tensor.matmul(ps[:, s, j * CN:(j + 1) * CN], w_hh[:, j * P:(j + 1) * P],
                                                    x_fm[:, cslice(c)], start=False, stop=True)
                        last.then_inc(Q("rz_ready", p).sem, 1)
                        wait(pe, Q("n_in", p), c - 1)
                        nc.tensor.matmul(ps[:, 2 + s, 0:CN], w_comb[:, p, 2 * P:3 * P], acc[:, cslice(c)],
                                         start=True, stop=True).then_inc(Q("nh_ready", p).sem, 1)
                        if not isinstance(i, int) or c >= 2:
                            flip_new(c - 2, s)
                turns(pe, NODE_ITERS, gru, peeled=2)
                flip_new(NC - 2, 0)
                flip_new(NC - 1, 1)
                end_stage(pe, nc.tensor)
            end_stage(pe, nc.tensor)
            pass_pe(3, pe)
            end_stage(pe, nc.tensor)
            end_stage(pe, nc.tensor)
            pass_pe(4, pe)
            end_stage(pe, nc.tensor)

            def product(c, s):
                pe.wait_ge(S("flip_taken_hy"), c + 1)
                wait(pe, S("hy_out"), c - 1)
                nc.tensor.matmul(ps[:, s, 0:CN], w_hyper[:, :], tmp(1, s), start=True, stop=True)\
                    .then_inc(S("hy_product"), 1)

            def hyper_product(i):
                for s in range(2):
                    c = 2 * i + s
                    flip_pe("_hy", pe, tmp(0, s), c, s, S("hy_scaled"))
                    if not (isinstance(c, int) and c == 0):
                        product(c - 1, 1 - s)
            turns(pe, NODE_ITERS, hyper_product)
            product(NC - 1, 1)
            end_stage(pe, nc.tensor)

            def hyper_rows(i):
                for s in range(2):
                    c = 2 * i + s
                    flip_pe("_hr", pe, tmp(0, s), c, s, S("hy_relu"))
            turns(pe, NODE_ITERS, hyper_rows)
            end_stage(pe, nc.tensor)
            end_stage(pe, nc.tensor)

            def to_fm(i):
                for s in range(2):
                    c = 2 * i + s
                    flip_pe("_x2", pe, tmp(0, s), c, s, S("cut_x2"))
            turns(pe, NODE_ITERS, to_fm)
            end_stage(pe, nc.tensor)

            def score_sums(c, s):
                pe.wait_ge(S("sc_prod"), c + 1)
                nc.tensor.matmul(ps[:, 2 + s, 0:CN], ones[:, :], tmp_acc(1, s), start=True, stop=True)
                for b in range(CB):
                    last = nc.tensor.matmul(ps[:, 2 + s, CN + b:CN + b + 1],
                                            tmp_acc(2, s)[:, b * P:(b + 1) * P], ones[:, 0:1],
                                            start=True, stop=True)
                last.then_inc(S("s_ready"), 1)

            def scores(i):
                for s in range(2):
                    c = 2 * i + s
                    pe.wait_ge(S("xn_ready"), c + 1)
                    wait(pe, S("sc_prod"), c - 1)
                    for j in range(2):
                        last = nc.tensor.matmul(ps[:, s, j * CN:(j + 1) * CN], w_att[:, (1 + j) * P:(2 + j) * P],
                                                tmp_acc(0, s), start=True, stop=True)
                    last.then_inc(S("sc_ready"), 1)
                    wait(pe, S("s_taken"), c - 1)
                    for b in range(CB):
                        last = nc.tensor.matmul(ps[:, 4 + s, b * P:(b + 1) * P],
                                                tmp_acc(0, s)[:, b * P:(b + 1) * P],
                                                w_att[:, 0:P], start=True, stop=True)
                    last.then_inc(S("mapped"), 1)
                    if not (isinstance(c, int) and c == 0):
                        score_sums(c - 1, 1 - s)
            turns(pe, NODE_ITERS, scores)
            score_sums(NC - 1, 1)
            end_stage(pe, nc.tensor)
            pass_pe(5, pe)
            end_stage(pe, nc.tensor)
            end_stage(pe, nc.tensor)
            nc.tensor.transpose(ps[:, 0, 0:P], w_e2, ident[:, :]).then_inc(S("e2_flipped"), 1)
            pe.wait_ge(S("e2_copied"), 1)
            nc.tensor.matmul(ps[:, 1, 0:P], tmp(0, 0)[:, 0:P], w_n1[:, P:2 * P], start=True, stop=True)
            nc.tensor.matmul(ps[0:1, 1, P:2 * P], col(E2_B), w_n1[:, P:2 * P], start=True, stop=True)\
                .then_inc(S("e2_combined"), 1)
            end_stage(pe, nc.tensor)

            def halves(c, s):
                pe.wait_ge(S("flip_taken_x3"), c + 1)
                wait(pe, S("p_staged"), c - 1)
                wait(pe, S("q_taken"), c - 1)
                for b in range(CB):
                    last = nc.tensor.matmul(ps[:, s, b * CN:(b + 1) * CN], tmp(1, s)[:, b * P:(b + 1) * P],
                                            w_e1, start=True, stop=True)
                last.then_inc(S("pq_ready"), 1)

            def edge_halves(i):
                for s in range(2):
                    c = 2 * i + s
                    flip_pe("_x3", pe, tmp(0, s), c, s, S("cut_x3"))
                    if not (isinstance(c, int) and c == 0):
                        halves(c - 1, 1 - s)
            turns(pe, NODE_ITERS, edge_halves)
            halves(NC - 1, 1)
            end_stage(pe, nc.tensor)
            pass_pe(6, pe)
            end_stage(pe, nc.tensor)
            pe.wait_ge(S("degree_in"), 16)

            def mesh_out(c, s):
                pe.wait_ge(S("hid_copied"), c + 1)
                wait(pe, S("mesh_added"), c - 1)
                for b in range(CB):
                    last = nc.tensor.matmul(ps[:, 4 + s, b * P:(b + 1) * P], tmp(1, s)[:, b * P:(b + 1) * P], w_n2,
                                            start=True, stop=True)
                last.then_inc(S("mesh_ready"), 1)

            def node_mlp(i):
                for s in range(2):
                    c = 2 * i + s
                    wait(pe, S("hid_copied"), c - 1)
                    nc.tensor.matmul(ps[:, 2 + s, 0:CN], w_n1[:, 0:P], x_fm[:, cslice(c)], start=True, stop=False)
                    nc.tensor.matmul(ps[:, 2 + s, 0:CN], w_e2, acc[:, cslice(c)], start=False, stop=False)
                    nc.tensor.matmul(ps[:, 2 + s, 0:CN], row0[0:1, 0:P], stage[0:1, cslice(c)], start=False, stop=True)\
                        .then_inc(S("hid_ready"), 1)
                    if not (isinstance(c, int) and c == 0):
                        mesh_out(c - 1, 1 - s)
            turns(pe, NODE_ITERS, node_mlp)
            mesh_out(NC - 1, 1)
            end_stage(pe, nc.tensor)
            end_stage(pe, nc.tensor)

        @block.vector
        def _(dve):
            for view in (dst_e, src_e, next_e):
                nc.vector.memset(view, PAD_NODE).then_inc(S("edges_padded"), 1)
            nc.vector.memset(x_nm[:, NB - 1:NBP, :], 0.0).then_inc(S("x_zero"), 1)
            step = chain(dve)
            nc.vector.memset(ones_row, 1.0)
            nc.vector.memset(small[:, :, :], 0.0)
            nc.vector.memset(big[:, 0:4 * T], 0.0)
            nc.vector.memset(tiny, 0.0)
            step(nc.vector.memset(count_b, 0.0))
            dve.wait_ge(S("edges_in"), 96)
            step(nc.vector.tensor_scalar(int_a, src_e, NODE_BITS, None, ALU.logical_shift_left))
            nc.vector.tensor_tensor(packed, int_a, dst_e, ALU.bitwise_or).then_inc(S("packed_ready"), 1)
            step(nc.vector.tensor_scalar(int_b, dst_e, 7, None, ALU.logical_shift_right))
            nc.vector.tensor_copy(blk0_h, int_b)
            step(nc.vector.tensor_copy(blk0, int_b))
            step(nc.vector.tensor_scalar(int_b, next_e, 7, None, ALU.logical_shift_right))
            step(nc.vector.tensor_copy(next_blk, int_b))
            step(nc.vector.tensor_tensor(scan, next_blk, blk0, ALU.is_lt))
            step(nc.vector.tensor_reduce(tiny[:, 0:1], scan, AX_X, ALU.add))
            dve.wait_ge(S("consts"), 1)

            def count_block(b):
                for s in range(2):
                    wait(dve, S("masked"), 2 * b + s - 1)
                    nc.vector.tensor_scalar(mask_h[s], blk0_h, iota[:, bass.ds(2 * b + s, 1)], None, ALU.is_equal,
                                            ALU.add, accum_out=count_b[:, bass.ds(2 * b + s, 1)]
                                            ).then_inc(S("masked"), 1)
            turns(dve, NB1 // 2, count_block)
            dve.wait_ge(S("masked"), NB1)
            dve.sem_inc(S("counted"), 1)
            dve.wait_ge(S("totals"), 1)
            nc.vector.tensor_copy(flag[:, :], ps[:, 2, 1:2]).then_inc(S("flag_ready"), 1)
            nc.vector.tensor_copy(tiny[:, 1:2], ps[:, 2, 0:1]).then_inc(S("tot_copied"), 1)
            dve.wait_ge(S("bases"), 1)
            step(nc.vector.tensor_copy(tiny[:, 2:3], ps[:, 2, 2:3]))
            with dve.If(dve.value_load(flag[0:1, 0:1], min_val=0, max_val=E)):
                sort = Steps(dve, "sort_steps", 0)
                nc.vector.tensor_scalar(diag, ident[:, :], tiny[:, 2:3], None, ALU.mult).then_inc(S("diag0_ready"), 1)
                dve.wait_ge(S("places0"), 1)
                sort(nc.vector.tensor_copy(base, ps[:, 3, 0:MASKB]))
                sort(nc.vector.memset(pos0, 0.0))
                with dve.Fori(0, NB1) as b:
                    rank = Steps(dve, "sort_ranks", 4)
                    rank.chunk(b)
                    rank(nc.vector.tensor_scalar(mask, blk0, iota[:, bass.ds(b, 1)], None, ALU.is_equal))
                    rank(nc.vector.tensor_tensor_scan(scan, ones_row, mask, base[:, bass.ds(b, 1)], ALU.mult, ALU.add))
                    rank(nc.vector.tensor_tensor(prod, scan, mask, ALU.mult))
                    rank(nc.vector.tensor_tensor(pos0, pos0, prod, ALU.add))
                nc.vector.tensor_scalar(slot_addr, pos0, -1.0, None, ALU.add).then_inc(S("addr_ready"), 1)
            step(nc.vector.tensor_copy(tiny_i[:, 0:1], tiny[:, 2:3]))
            step(nc.vector.tensor_scalar(tiny_i[:, 1:2], tiny_i[:, 0:1], 7, None, ALU.logical_shift_right))
            step(nc.vector.tensor_copy(tiny[:, 3:4], tiny_i[:, 1:2]))
            step(nc.vector.scalar_tensor_tensor(tiny_i[:, 2:3], tiny[:, 1:2], -1.0, tiny[:, 2:3], ALU.add, ALU.add))
            step(nc.vector.tensor_scalar(tiny_i[:, 3:4], tiny_i[:, 2:3], 7, None, ALU.arith_shift_right))
            step(nc.vector.tensor_scalar(tiny[:, 4:5], tiny[:, 1:2], 0.0, None, ALU.is_gt))
            step(nc.vector.scalar_tensor_tensor(tiny[:, 5:6], tiny_i[:, 3:4], 1.0, tiny[:, 3:4], ALU.add, ALU.subtract))
            step(nc.vector.tensor_tensor(tiny[:, 5:6], tiny[:, 5:6], tiny[:, 4:5], ALU.mult))
            nc.vector.tensor_tensor(tiny[:, 5:6], tiny[:, 5:6], real_block[:, :], ALU.mult).then_inc(S("pair_cols"), 1)
            dve.wait_ge(S("pair_sums"), 1)
            step(nc.vector.tensor_copy(tiny[:, 6:7], ps[:, 2, 3:4]))
            nc.vector.tensor_tensor(tiny[:, 7:8], tiny[:, 3:4], tiny[:, 6:7], ALU.subtract).then_inc(S("pair_cols"), 1)
            nc.vector.tensor_scalar(tile_ge, tile_iota[:, :], tiny[:, 6:7], None, ALU.is_ge)
            dve.wait_ge(S("pair_sums"), 2)
            nc.vector.tensor_copy(tiny[:, 9:10], sel_blocks[:, 0:1])
            nc.vector.tensor_tensor(tiny[:, 8:9], ps[:, 2, 4:5], sel_blocks[:, 0:1], ALU.mult).then_inc(S("pair_cols"), 1)
            dve.wait_ge(S("pair_sums"), 3)
            pairs = ps[:, 3, T // 2:T // 2 + 2 * TG].rearrange("p (g a) -> p g a", a=2)
            step(nc.vector.tensor_tensor(pair_blk[:, :], pair_blk[:, :], pairs[:, :, 0], ALU.add))
            nc.vector.tensor_scalar(pair_idx[:, :], pair_blk[:, :], float(EDGE_TILES - 1), None, ALU.min)\
                .then_inc(S("pairs_ready"), 1)
            dve.wait_ge(S("pairs_ready"), 1)
            nc.vector.tensor_scalar(pair_blk[:, :], pairs[:, :, 1], float(P), None, ALU.mult)\
                .then_inc(S("pairs_ready"), 1)
            dve.wait_ge(S("pairs_ready"), 2)
            with dve.If(dve.value_load(flag[0:1, 0:1], min_val=0, max_val=E)):
                def ring(i):
                    for h in range(2):
                        c = 2 * i + h
                        dve.wait_ge(S("ring_half"), c + 1)
                        nc.vector.tensor_copy(val_ring[:, h * SC:(h + 1) * SC], packed[:, bass.ds(SC * c, SC)])\
                            .then_inc(S("ring_filled"), 1)
                turns(dve, SCATTER_ITERS, ring)
            step(nc.vector.tensor_scalar(int_a, src_e, 7, None, ALU.logical_shift_right))
            nc.vector.memset(blk1[:, EC:T], 255.0)
            step(nc.vector.tensor_copy(blk1[:, 0:EC], int_a))
            step(nc.vector.tensor_scalar(int_b, src_e, P - 1, None, ALU.bitwise_and))
            step(nc.vector.scalar_tensor_tensor(int_a, dst_e, float(P), int_b, ALU.mult, ALU.add))
            step(nc.vector.tensor_scalar(int_a, int_a, 1.0, None, ALU.add))
            step(nc.vector.tensor_scalar(int_b, int_a, LOW_BITS, None, ALU.logical_shift_right))
            step(nc.vector.tensor_copy(hi1[:, 0:EC], int_b))
            step(nc.vector.tensor_scalar(int_b, int_a, (1 << LOW_BITS) - 1, None, ALU.bitwise_and))
            step(nc.vector.tensor_scalar(lo1[:, 0:EC], int_b, 1.0 / (1 << LOW_BITS), None, ALU.mult))
            step(nc.vector.memset(count_b, 0.0))
            dve.wait_ge(S("vectors_in"), 16 * 14)
            nc.vector.tensor_tensor(col(B_R), col(13), col(15), ALU.add)
            step(nc.vector.tensor_tensor(col(B_Z), col(14), col(16), ALU.add))
            dve.wait_ge(S("pairs_in"), 16 * TG)
            step(nc.vector.tensor_scalar(pair_a, pair_rows, (1 << NODE_BITS) - 1, None, ALU.bitwise_and))
            for g in range(TG):
                last = nc.vector.tensor_scalar(pair_f[:, g, :], pair_a[:, g, :], pair_blk[:, g:g + 1], None, ALU.subtract)
            step(last)
            step(nc.vector.tensor_scalar(pair_b, pair_rows, NODE_BITS, None, ALU.logical_shift_right))
            step(nc.vector.tensor_scalar(pair_a, pair_b, float(N), None, ALU.is_lt))
            nc.vector.tensor_tensor(pair_src, pair_b, pair_a, ALU.mult).then_inc(S("pair_values"), 1)
            dve.wait_ge(S("pair_sums"), 4)
            for j in range(2):
                nc.vector.tensor_copy(block_of[0][:, j * (T // 2):(j + 1) * (T // 2)], ps[:, 2 + j, 0:T // 2])
            dve.wait_ge(S("pair_flipped"), 1)
            for n, out in enumerate((local[0], gather_idx[0])):
                for j in range(2):
                    w = min(4, TG - 4 * j) * P
                    nc.vector.tensor_copy(out[:, j * 4 * P:j * 4 * P + w], ps[:, (0, 6)[n] + j, 0:w])
            end_stage(dve, nc.vector)

            for p in range(GRU_LAYERS):
                pass_dve(p, dve)
                end_stage(dve, nc.vector)
                last_layer = p == GRU_LAYERS - 1
                in_steps = Steps(dve, "gru_in_steps", 1, NC * p)
                steps = Steps(dve, "gru_steps", 2, 2 * NC * p)

                def residual(c, s, p=p):
                    blk = x_nm[:, bslice(c), :].rearrange("p b f -> p (b f)")
                    wait(dve, Q("flip_done_gru", p), c + 1)
                    nc.vector.tensor_tensor(blk, blk, tslot(s), ALU.add).then_inc(Q("flip_taken_gru", p).sem, 1)
                    stats_dve(dve, c, s, node_stats(0), Q("flip_taken_gru", p))

                def new_state(c, s, p=p, steps=steps, last_layer=last_layer):
                    steps.chunk(c)
                    wait(dve, Q("n_ready", p), c + 1)
                    steps(nc.vector.tensor_tensor(tmp(5, s), x_fm[:, cslice(c)], tmp(3, s), ALU.subtract))
                    steps(nc.vector.tensor_tensor(tmp(5, s), tmp(5, s), tmp(1, s), ALU.mult))
                    wait(dve, Q("flip_done_gru", p), c - 1)
                    if not last_layer:
                        wait(dve, Q("h_kept", p), c - 1)
                    nc.vector.tensor_tensor(tmp(6, s), tmp(5, s), tmp(3, s), ALU.add).then_inc(Q("h_ready", p).sem, 1)

                def gru(i, p=p, steps=in_steps, last_layer=last_layer):
                    for s in range(2):
                        c = 2 * i + s
                        known = isinstance(i, int)
                        steps.chunk(c)
                        wait(dve, Q("nh_ready", p), c + 1)
                        wait(dve, Q("r_ready", p), c + 1)
                        steps(nc.vector.tensor_tensor(tmp(4, s), stage[:, cslice(c)], tmp(0, s), ALU.mult))
                        nc.vector.tensor_tensor(tmp(2, s), tmp(4, s), ps[:, 2 + s, 0:CN], ALU.add)\
                            .then_inc(Q("n_in", p).sem, 1)
                        if not known or c >= 1:
                            new_state(c - 1, 1 - s)
                        if last_layer and (not known or c >= 2):
                            residual(c - 2, s)
                turns(dve, NODE_ITERS, gru, peeled=2)
                new_state(NC - 1, 1)
                if last_layer:
                    residual(NC - 2, 0)
                    residual(NC - 1, 1)
                    last_stats_dve(dve, node_stats(0))
                end_stage(dve, nc.vector)
            norm_dve(0, dve)
            end_stage(dve, nc.vector)
            pass_dve(3, dve)
            end_stage(dve, nc.vector)

            nc.vector.tensor_copy(small[:, 4, :], acc_nm[:, :, P]).then_inc(S("degree_ready"), 1)
            safe_inverse_dve("_b", dve)
            dve.sem_inc(S("inverse_done_b"), 1)
            unpack1_dve(dve)
            end_stage(dve, nc.vector)
            pass_dve(4, dve)
            end_stage(dve, nc.vector)

            safe_inverse_dve("_d", dve)

            def node_scale(i):
                for s in range(2):
                    c = 2 * i + s
                    wait(dve, S("flip_done_hy"), c - 1)
                    for b in range(CB):
                        last = nc.vector.tensor_scalar(tmp(0, s)[:, b * P:(b + 1) * P],
                                                       acc_nm[:, bass.ds(c * CB + b, 1), 0:P].rearrange("p b f -> p (b f)"),
                                                       small[:, 1, bass.ds(c * CB + b, 1)], None, ALU.mult)
                    last.then_inc(S("hy_scaled"), 1)
            turns(dve, NODE_ITERS, node_scale)
            dve.wait_ge(S("hy_out"), 2 * NODE_ITERS)
            batch_dve(0, dve, big, col(HY_G), col(HY_BE), col(SCALE), col(SHIFT))
            end_stage(dve, nc.vector)

            def hyper_residual(i):
                for s in range(2):
                    c = 2 * i + s
                    blk = x_nm[:, bslice(c), :].rearrange("p b f -> p (b f)")
                    dve.wait_ge(S("flip_done_hr"), c + 1)
                    nc.vector.tensor_tensor(blk, blk, tslot(s), ALU.add).then_inc(S("flip_taken_hr"), 1)
                    stats_dve(dve, c, s, node_stats(1), S("flip_taken_hr"))
            turns(dve, NODE_ITERS, hyper_residual)
            last_stats_dve(dve, node_stats(1))
            end_stage(dve, nc.vector)
            norm_dve(1, dve)
            end_stage(dve, nc.vector)

            def cut_x2(i):
                for s in range(2):
                    cut_dve("_x2", dve, 2 * i + s, s, tmp(0, s))
            turns(dve, NODE_ITERS, cut_x2)
            dve.wait_ge(S("flip_taken_x2"), 2 * NODE_ITERS)
            batch_dve(1, dve, x_fm, col(AT_G), col(AT_BE), col(SCALE), col(SHIFT))
            end_stage(dve, nc.vector)

            def score_products(c, s):
                dve.wait_ge(S("xn_ready"), c + 1)
                wait(dve, S("s_ready"), c - 1)
                dve.wait_ge(S("sc_ready"), c + 1)
                nc.vector.tensor_tensor(tmp_acc(1, s), ps[:, s, 0:CN], tmp_acc(0, s), ALU.mult)
                nc.vector.tensor_tensor(tmp_acc(2, s), ps[:, s, CN:2 * CN], tmp_acc(0, s), ALU.mult)\
                    .then_inc(S("sc_prod"), 1)

            nc.vector.memset(stage_nm[:, :, P], 1.0).then_inc(S("ones_cols"), 1)

            def scores(i):
                for s in range(2):
                    c = 2 * i + s
                    wait(dve, S("mapped"), c - 1)
                    wait(dve, S("sc_prod"), c - 1)
                    nc.vector.tensor_scalar(tmp_acc(0, s), x_fm[:, cslice(c)], col(SCALE), col(SHIFT), ALU.mult, ALU.add)\
                        .then_inc(S("xn_ready"), 1)
                    if not (isinstance(c, int) and c == 0):
                        score_products(c - 1, 1 - s)
            turns(dve, NODE_ITERS, scores)
            score_products(NC - 1, 1)
            end_stage(dve, nc.vector)
            pass_dve(5, dve)
            end_stage(dve, nc.vector)

            one = chain(dve)
            one(nc.vector.tensor_scalar(small[:, 0, :], acc_nm[:, :, P], 1e-16, None, ALU.max))
            nc.vector.reciprocal(small[:, 1, :], small[:, 0, :]).then_inc(S("inverse_done_at"), 1)

            def att_residual(i):
                for s in range(2):
                    c = 2 * i + s
                    blk = x_nm[:, bslice(c), :].rearrange("p b f -> p (b f)")
                    dve.wait_ge(S("at_relu"), (c + 1) * CB)
                    nc.vector.tensor_tensor(blk, blk, x_fm[:, s * CN:(s + 1) * CN], ALU.add).then_inc(S("at_added"), 1)
                    stats_dve(dve, c, s, node_stats(2), S("at_added"))
            turns(dve, NODE_ITERS, att_residual)
            last_stats_dve(dve, node_stats(2))
            end_stage(dve, nc.vector)
            norm_dve(2, dve)
            end_stage(dve, nc.vector)

            def edge_taken(c, s):
                dve.wait_ge(S("flip_taken_x3"), c + 1)
                nc.vector.tensor_copy(x_fm[:, cslice(c)], tmp(1, s))
                for b in range(CB):
                    blk = x_nm[:, bass.ds(c * CB + b, 1), :].rearrange("p b f -> p (b f)")
                    nc.vector.scalar_tensor_tensor(blk, blk, 2.0, bn2_rows, ALU.mult, ALU.add)
                dve.wait_ge(S("p_staged"), c + 1)
                nc.vector.tensor_tensor(q_nm[:, cslice(c)].rearrange("p (b f) -> p b f", b=CB),
                                        ps[:, s, :].rearrange("p (b h f) -> p b h f", b=CB, h=2)[:, :, 1, :],
                                        be1_rows.unsqueeze(1).to_broadcast([P, CB, P]), ALU.add)\
                    .then_inc(S("q_taken"), 1)

            def edge_halves(i):
                for s in range(2):
                    c = 2 * i + s
                    cut_dve("_x3", dve, c, s, tmp(0, s))
                    if not (isinstance(i, int) and i == 0):
                        edge_taken(c - 2, s)
            turns(dve, NODE_ITERS, edge_halves)
            edge_taken(NC - 2, 0)
            edge_taken(NC - 1, 1)
            end_stage(dve, nc.vector)
            pass_dve(6, dve)
            end_stage(dve, nc.vector)

            def mesh_residual(i):
                for s in range(2):
                    c = 2 * i + s
                    blk = x_nm[:, bslice(c), :].rearrange("p b f -> p (b f)")
                    dve.wait_ge(S("mesh_ready"), c + 1)
                    nc.vector.tensor_tensor(blk, blk, ps[:, 4 + s, 0:CN], ALU.add).then_inc(S("mesh_added"), 1)
                    stats_dve(dve, c, s, node_stats(3), S("mesh_added"))
            turns(dve, NODE_ITERS, mesh_residual)
            last_stats_dve(dve, node_stats(3))
            end_stage(dve, nc.vector)
            norm_dve(3, dve)
            end_stage(dve, nc.vector)


_INS = ["x", "src", "dst", "L0_gnn_lin_w", "L0_gnn_lin_b", "L0_gnn_weight", "L0_gnn_w_ih", "L0_gnn_w_hh",
        "L0_gnn_b_ih", "L0_gnn_b_hh", "L1_gnn_hyperedge_weight", "L1_gnn_W", "L1_gnn_b", "L1_gnn_gamma",
        "L1_gnn_beta", "L2_gnn_kernel", "L2_gnn_kernel1", "L2_gnn_kernel2", "L2_gnn_gamma", "L2_gnn_beta",
        "L3_gnn_We1", "L3_gnn_be1", "L3_gnn_We2", "L3_gnn_be2", "L3_gnn_Wn1", "L3_gnn_bn1", "L3_gnn_Wn2",
        "L3_gnn_bn2"]


def kernel(**inputs):
    import numpy as np
    import concourse.bacc as bacc
    from concourse.bass_utils import run_bass_kernel_spmd

    nc = bacc.Bacc("TRN2", target_bir_lowering=False, num_devices=1)
    arrays = {name: np.ascontiguousarray(inputs[name]) for name in _INS}
    d = {name: nc.dram_tensor(name, a.shape, mybir.dt.from_np(a.dtype), kind="ExternalInput").ap()
         for name, a in arrays.items()}
    d["out"] = nc.dram_tensor("out", (N, P), F32, kind="ExternalOutput").ap()
    gnn(nc, d)
    return run_bass_kernel_spmd(nc, [arrays], core_ids=[0]).results[0]["out"]
```
